# Optimizing a Trainium2 kernel written in Bass

```python
import numpy as np
import jax
import jax.numpy as jnp

def _softmax(x, axis=-1):
    return jax.nn.softmax(x, axis=axis)
def _gelu(x):
    return jax.nn.gelu(x, approximate=True)
def _silu(x):
    return jax.nn.silu(x)
def _sigmoid(x):
    return jax.nn.sigmoid(x)
def _layernorm(x, axis=-1, eps=1e-5):
    m = jnp.mean(x, axis=axis, keepdims=True)
    v = jnp.var(x, axis=axis, keepdims=True)
    return (x - m) / jnp.sqrt(v + eps)
def _scatter_add(tgt, idx, src, axis=0):
    return tgt.at[idx].add(src)
def _segment_sum(src, seg, n):
    return jax.ops.segment_sum(src, seg, n)

kernel_name = 'mk_metaformer_d2_conv_nhwc256_8b7306'

def setup_inputs(seed: int = 0):
    np.random.seed(seed)
    _w = jnp.asarray
    def _rec_inputs():
        import jax
        import jax.numpy as jnp
        _gk = jax.random.key(seed)
        x = -0.0005207 + 1.001 * jax.random.normal(jax.random.fold_in(_gk, 1), (8, 32, 32, 256), jnp.float32)
        return x
    x = _rec_inputs()
    def _L0_conv_setup():
        import jax, jax.numpy as jnp
        import numpy as np
        B, N1, N2, E = (8, 32, 32, 256)
        H = 8
        KD = E // H
        HD = E // H
        L = N1 * N2
        SCALING = KD ** (-0.5)
        LN_EPS = 1e-05

        def _rel_pos_2d():
            half = 1.0 / 10000.0 ** jnp.linspace(0.0, 1.0, KD // 2)
            angle = jnp.repeat(half, 2)
            decay = jnp.log(1.0 - 2.0 ** (-2.0 - 5.0 * jnp.arange(H, dtype=jnp.float32) / H))
            i1 = jnp.arange(N1, dtype=jnp.float32)
            i2 = jnp.arange(N2, dtype=jnp.float32)
            index_k = (i1[:, None] + i2[None, :]).reshape(L)
            sin_k = jnp.sin(index_k[:, None] * angle[None, :])
            cos_k = jnp.cos(index_k[:, None] * angle[None, :])
            sin_q = sin_k[None, None]
            cos_q = cos_k[None, None]
            d = (jnp.abs(i1[:, None, None, None] - i1[None, None, :, None]) + jnp.abs(i2[None, :, None, None] - i2[None, None, None, :])).reshape(L, L)
            mask = jnp.exp(d[None, :, :] * decay[:, None, None])
            mask = jnp.nan_to_num(mask)
            mask = mask / jnp.sqrt(mask.sum(-1, keepdims=True))
            return (sin_q, cos_q, sin_k, cos_k, mask)

        def rotate_every_two(x):
            x1 = x[..., ::2]
            x2 = x[..., 1::2]
            return jnp.stack((-x2, x1), axis=-1).reshape(x.shape)

        def theta_shift(x, sin, cos):
            return x * cos + rotate_every_two(x) * sin
        key = jax.random.key(seed)
        ks = jax.random.split(key, 5)
        gain_qkv = 2.0 ** (-2.5) * (6.0 / (E + E)) ** 0.5
        gain_o = 2.0 ** (-1) * (6.0 / (E + E)) ** 0.5
        x = jax.random.normal(ks[0], (B, N1, N2, E), dtype=jnp.float32)
        Wq = jax.random.uniform(ks[1], (E, E), jnp.float32, -gain_qkv, gain_qkv)
        Wk = jax.random.uniform(ks[2], (E, E), jnp.float32, -gain_qkv, gain_qkv)
        Wv = jax.random.uniform(ks[3], (E, E), jnp.float32, -gain_qkv, gain_qkv)
        Wo = jax.random.uniform(ks[4], (E, E), jnp.float32, -gain_o, gain_o)
        ln_g = jnp.ones((HD,), jnp.float32)
        ln_b = jnp.zeros((HD,), jnp.float32)
        return {'x': x, 'Wq': Wq, 'Wk': Wk, 'Wv': Wv, 'Wo': Wo, 'ln_g': ln_g, 'ln_b': ln_b}
    _L0_conv_all = _L0_conv_setup()
    _L0_conv_in = {k: v for k, v in _L0_conv_all.items() if k in ('Wq', 'Wk', 'Wv', 'Wo', 'ln_g', 'ln_b', )}
    del _L0_conv_all

    def _L0_ffn_setup():
        import jax, jax.numpy as jnp
        import numpy as np
        B, N, D = (16, 4096, 256)
        NUM_EXPERTS, TOP_K, HEADS = (4, 2, 4)
        N_EDGES = 1048576
        LN_EPS = 1e-05

        def _layernorm(x, g, b):
            mu = x.mean(-1, keepdims=True)
            var = ((x - mu) ** 2).mean(-1, keepdims=True)
            return (x - mu) * jax.lax.rsqrt(var + LN_EPS) * g + b

        def _forward(x, edge_index, W_gat, att_src, att_dst, b_gat, ln_gamma, ln_beta, W1, b1, W2, b2):
            Bc, Nc, Dc = x.shape
            M = Bc * Nc
            x_flat = x.reshape(M, Dc)
            h = (x_flat @ W_gat).reshape(M, HEADS, NUM_EXPERTS)
            loops = jnp.arange(M, dtype=edge_index.dtype)
            src = jnp.concatenate([edge_index[0], loops])
            dst = jnp.concatenate([edge_index[1], loops])
            a_src = (h * att_src).sum(-1)
            a_dst = (h * att_dst).sum(-1)
            e = jax.nn.leaky_relu(a_src[src] + a_dst[dst], negative_slope=0.2)
            e_max = jax.ops.segment_max(e, dst, num_segments=M)
            ee = jnp.exp(e - e_max[dst])
            denom = jax.ops.segment_sum(ee, dst, num_segments=M)
            alpha = ee / (denom[dst] + 1e-16)
            msg = h[src] * alpha[:, :, None]
            agg = jax.ops.segment_sum(msg, dst, num_segments=M).reshape(M, HEADS * NUM_EXPERTS) + b_gat
            scores = _layernorm(agg, ln_gamma, ln_beta).reshape(M, HEADS, NUM_EXPERTS).mean(1)
            scores = scores.reshape(Bc, Nc, NUM_EXPERTS)
            topk_s, topk_i = jax.lax.top_k(scores, TOP_K)
            w = jax.nn.softmax(topk_s, axis=-1)
            out = jnp.zeros_like(x)
            for ei in range(NUM_EXPERTS):
                g = jnp.where(topk_i == ei, w, 0.0).sum(-1)
                hh = jax.nn.gelu(x @ W1[ei] + b1[ei], approximate=False)
                out = out + g[..., None] * (hh @ W2[ei] + b2[ei])
            return out
        key = jax.random.key(seed)
        ks = jax.random.split(key, 8)
        s = 0.05
        return {'x': jax.random.normal(ks[0], (B, N, D), jnp.float32), 'W_gat': jax.random.normal(ks[1], (D, HEADS * NUM_EXPERTS), jnp.float32) * s, 'att_src': jax.random.normal(ks[2], (HEADS, NUM_EXPERTS), jnp.float32) * s, 'att_dst': jax.random.normal(ks[3], (HEADS, NUM_EXPERTS), jnp.float32) * s, 'b_gat': jnp.zeros((HEADS * NUM_EXPERTS,), jnp.float32), 'ln_gamma': jnp.ones((HEADS * NUM_EXPERTS,), jnp.float32), 'ln_beta': jnp.zeros((HEADS * NUM_EXPERTS,), jnp.float32), 'W1': jax.random.normal(ks[4], (NUM_EXPERTS, D, 2 * D), jnp.float32) * s, 'b1': jnp.zeros((NUM_EXPERTS, 2 * D), jnp.float32), 'W2': jax.random.normal(ks[5], (NUM_EXPERTS, 2 * D, D), jnp.float32) * s, 'b2': jnp.zeros((NUM_EXPERTS, D), jnp.float32), 'edge_index': jax.random.randint(ks[6], (2, N_EDGES), 0, B * N, jnp.int32)}
    _L0_ffn_all = _L0_ffn_setup()
    _L0_ffn_in = {k: v for k, v in _L0_ffn_all.items() if k in ('W_gat', 'att_src', 'att_dst', 'b_gat', 'ln_gamma', 'ln_beta', 'W1', 'b1', 'W2', 'b2', 'edge_index', )}
    del _L0_ffn_all

    def _L1_conv_setup():
        import jax, jax.numpy as jnp
        import numpy as np
        _QMAX = 127.0

        def _quantize(x, axes):
            amax = jnp.max(jnp.abs(x), axis=axes, keepdims=True)
            scale = jnp.maximum(amax, 1e-06) / _QMAX
            q = jnp.clip(jnp.round(x / scale), -_QMAX, _QMAX)
            return (q, scale)
        key = jax.random.key(seed)
        k1, k2 = jax.random.split(key)
        lhs = jax.random.normal(k1, (32, 56, 56, 256), dtype=jnp.float32)
        rhs = jax.random.normal(k2, (3, 3, 256, 256), dtype=jnp.float32)
        return {'lhs': lhs, 'rhs': rhs}
    _L1_conv_all = _L1_conv_setup()
    _L1_conv_in = {k: v for k, v in _L1_conv_all.items() if k in ('rhs', )}
    del _L1_conv_all

    def _L1_ffn_setup():
        import jax, jax.numpy as jnp
        import numpy as np
        B, N, D = (16, 4096, 256)
        NUM_EXPERTS, TOP_K, HEADS = (4, 2, 4)
        N_EDGES = 1048576
        LN_EPS = 1e-05

        def _layernorm(x, g, b):
            mu = x.mean(-1, keepdims=True)
            var = ((x - mu) ** 2).mean(-1, keepdims=True)
            return (x - mu) * jax.lax.rsqrt(var + LN_EPS) * g + b

        def _forward(x, edge_index, W_gat, att_src, att_dst, b_gat, ln_gamma, ln_beta, W1, b1, W2, b2):
            Bc, Nc, Dc = x.shape
            M = Bc * Nc
            x_flat = x.reshape(M, Dc)
            h = (x_flat @ W_gat).reshape(M, HEADS, NUM_EXPERTS)
            loops = jnp.arange(M, dtype=edge_index.dtype)
            src = jnp.concatenate([edge_index[0], loops])
            dst = jnp.concatenate([edge_index[1], loops])
            a_src = (h * att_src).sum(-1)
            a_dst = (h * att_dst).sum(-1)
            e = jax.nn.leaky_relu(a_src[src] + a_dst[dst], negative_slope=0.2)
            e_max = jax.ops.segment_max(e, dst, num_segments=M)
            ee = jnp.exp(e - e_max[dst])
            denom = jax.ops.segment_sum(ee, dst, num_segments=M)
            alpha = ee / (denom[dst] + 1e-16)
            msg = h[src] * alpha[:, :, None]
            agg = jax.ops.segment_sum(msg, dst, num_segments=M).reshape(M, HEADS * NUM_EXPERTS) + b_gat
            scores = _layernorm(agg, ln_gamma, ln_beta).reshape(M, HEADS, NUM_EXPERTS).mean(1)
            scores = scores.reshape(Bc, Nc, NUM_EXPERTS)
            topk_s, topk_i = jax.lax.top_k(scores, TOP_K)
            w = jax.nn.softmax(topk_s, axis=-1)
            out = jnp.zeros_like(x)
            for ei in range(NUM_EXPERTS):
                g = jnp.where(topk_i == ei, w, 0.0).sum(-1)
                hh = jax.nn.gelu(x @ W1[ei] + b1[ei], approximate=False)
                out = out + g[..., None] * (hh @ W2[ei] + b2[ei])
            return out
        key = jax.random.key(seed)
        ks = jax.random.split(key, 8)
        s = 0.05
        return {'x': jax.random.normal(ks[0], (B, N, D), jnp.float32), 'W_gat': jax.random.normal(ks[1], (D, HEADS * NUM_EXPERTS), jnp.float32) * s, 'att_src': jax.random.normal(ks[2], (HEADS, NUM_EXPERTS), jnp.float32) * s, 'att_dst': jax.random.normal(ks[3], (HEADS, NUM_EXPERTS), jnp.float32) * s, 'b_gat': jnp.zeros((HEADS * NUM_EXPERTS,), jnp.float32), 'ln_gamma': jnp.ones((HEADS * NUM_EXPERTS,), jnp.float32), 'ln_beta': jnp.zeros((HEADS * NUM_EXPERTS,), jnp.float32), 'W1': jax.random.normal(ks[4], (NUM_EXPERTS, D, 2 * D), jnp.float32) * s, 'b1': jnp.zeros((NUM_EXPERTS, 2 * D), jnp.float32), 'W2': jax.random.normal(ks[5], (NUM_EXPERTS, 2 * D, D), jnp.float32) * s, 'b2': jnp.zeros((NUM_EXPERTS, D), jnp.float32), 'edge_index': jax.random.randint(ks[6], (2, N_EDGES), 0, B * N, jnp.int32)}
    _L1_ffn_all = _L1_ffn_setup()
    _L1_ffn_in = {k: v for k, v in _L1_ffn_all.items() if k in ('W_gat', 'att_src', 'att_dst', 'b_gat', 'ln_gamma', 'ln_beta', 'W1', 'b1', 'W2', 'b2', 'edge_index', )}
    del _L1_ffn_all

    return {
        "x": x,
        "L0_conv_Wq": _L0_conv_in["Wq"],
        "L0_conv_Wk": _L0_conv_in["Wk"],
        "L0_conv_Wv": _L0_conv_in["Wv"],
        "L0_conv_Wo": _L0_conv_in["Wo"],
        "L0_conv_ln_g": _L0_conv_in["ln_g"],
        "L0_conv_ln_b": _L0_conv_in["ln_b"],
        "L0_ffn_W_gat": _L0_ffn_in["W_gat"],
        "L0_ffn_att_src": _L0_ffn_in["att_src"],
        "L0_ffn_att_dst": _L0_ffn_in["att_dst"],
        "L0_ffn_b_gat": _L0_ffn_in["b_gat"],
        "L0_ffn_ln_gamma": _L0_ffn_in["ln_gamma"],
        "L0_ffn_ln_beta": _L0_ffn_in["ln_beta"],
        "L0_ffn_W1": _L0_ffn_in["W1"],
        "L0_ffn_b1": _L0_ffn_in["b1"],
        "L0_ffn_W2": _L0_ffn_in["W2"],
        "L0_ffn_b2": _L0_ffn_in["b2"],
        "L0_ffn_edge_index": _L0_ffn_in["edge_index"],
        "L1_conv_rhs": _L1_conv_in["rhs"],
        "L1_ffn_W_gat": _L1_ffn_in["W_gat"],
        "L1_ffn_att_src": _L1_ffn_in["att_src"],
        "L1_ffn_att_dst": _L1_ffn_in["att_dst"],
        "L1_ffn_b_gat": _L1_ffn_in["b_gat"],
        "L1_ffn_ln_gamma": _L1_ffn_in["ln_gamma"],
        "L1_ffn_ln_beta": _L1_ffn_in["ln_beta"],
        "L1_ffn_W1": _L1_ffn_in["W1"],
        "L1_ffn_b1": _L1_ffn_in["b1"],
        "L1_ffn_W2": _L1_ffn_in["W2"],
        "L1_ffn_b2": _L1_ffn_in["b2"],
        "L1_ffn_edge_index": _L1_ffn_in["edge_index"],
    }

def reference(x, L0_conv_Wq, L0_conv_Wk, L0_conv_Wv, L0_conv_Wo, L0_conv_ln_g, L0_conv_ln_b, L0_ffn_W_gat, L0_ffn_att_src, L0_ffn_att_dst, L0_ffn_b_gat, L0_ffn_ln_gamma, L0_ffn_ln_beta, L0_ffn_W1, L0_ffn_b1, L0_ffn_W2, L0_ffn_b2, L0_ffn_edge_index, L1_conv_rhs, L1_ffn_W_gat, L1_ffn_att_src, L1_ffn_att_dst, L1_ffn_b_gat, L1_ffn_ln_gamma, L1_ffn_ln_beta, L1_ffn_W1, L1_ffn_b1, L1_ffn_W2, L1_ffn_b2, L1_ffn_edge_index):
    import jax
    import jax.numpy as jnp
    def _L0_conv_ref(x, Wq, Wk, Wv, Wo, ln_g, ln_b):
        import jax, jax.numpy as jnp
        import numpy as np
        B, N1, N2, E = (8, 32, 32, 256)
        H = 8
        KD = E // H
        HD = E // H
        L = N1 * N2
        SCALING = KD ** (-0.5)
        LN_EPS = 1e-05

        def _rel_pos_2d():
            half = 1.0 / 10000.0 ** jnp.linspace(0.0, 1.0, KD // 2)
            angle = jnp.repeat(half, 2)
            decay = jnp.log(1.0 - 2.0 ** (-2.0 - 5.0 * jnp.arange(H, dtype=jnp.float32) / H))
            i1 = jnp.arange(N1, dtype=jnp.float32)
            i2 = jnp.arange(N2, dtype=jnp.float32)
            index_k = (i1[:, None] + i2[None, :]).reshape(L)
            sin_k = jnp.sin(index_k[:, None] * angle[None, :])
            cos_k = jnp.cos(index_k[:, None] * angle[None, :])
            sin_q = sin_k[None, None]
            cos_q = cos_k[None, None]
            d = (jnp.abs(i1[:, None, None, None] - i1[None, None, :, None]) + jnp.abs(i2[None, :, None, None] - i2[None, None, None, :])).reshape(L, L)
            mask = jnp.exp(d[None, :, :] * decay[:, None, None])
            mask = jnp.nan_to_num(mask)
            mask = mask / jnp.sqrt(mask.sum(-1, keepdims=True))
            return (sin_q, cos_q, sin_k, cos_k, mask)

        def rotate_every_two(x):
            x1 = x[..., ::2]
            x2 = x[..., 1::2]
            return jnp.stack((-x2, x1), axis=-1).reshape(x.shape)

        def theta_shift(x, sin, cos):
            return x * cos + rotate_every_two(x) * sin
        sin_q, cos_q, sin_k, cos_k, mask = _rel_pos_2d()
        xf = x.reshape(B, L, E)
        q = (xf @ Wq.T).reshape(B, L, H, KD).transpose(0, 2, 1, 3)
        k = (xf @ Wk.T * SCALING).reshape(B, L, H, KD).transpose(0, 2, 1, 3)
        vr = (xf @ Wv.T).reshape(B, L, H, HD).transpose(0, 2, 1, 3)
        qr = theta_shift(q, sin_q, cos_q)
        kr = theta_shift(k, sin_k[None, None], cos_k[None, None])
        qk = jnp.einsum('bhqd,bhkd->bhqk', qr, kr) * mask[None]
        den = jnp.clip(jax.lax.stop_gradient(jnp.abs(qk)).sum(-1, keepdims=True), 1.0, 50000.0)
        qk = qk / den
        out = jnp.einsum('bhqk,bhkd->bhqd', qk, vr).transpose(0, 2, 1, 3)
        mu = out.mean(-1, keepdims=True)
        var = out.var(-1, keepdims=True)
        out = (out - mu) / jnp.sqrt(var + LN_EPS) * ln_g + ln_b
        out = jax.nn.gelu(out.reshape(B, L, H * HD), approximate=False)
        out = out @ Wo.T
        return out.reshape(B, N1, N2, E)

    def _L0_ffn_ref(x, W_gat, att_src, att_dst, b_gat, ln_gamma, ln_beta, W1, b1, W2, b2, edge_index):
        import jax, jax.numpy as jnp
        import numpy as np
        B, N, D = (16, 4096, 256)
        NUM_EXPERTS, TOP_K, HEADS = (4, 2, 4)
        N_EDGES = 1048576
        LN_EPS = 1e-05

        def _layernorm(x, g, b):
            mu = x.mean(-1, keepdims=True)
            var = ((x - mu) ** 2).mean(-1, keepdims=True)
            return (x - mu) * jax.lax.rsqrt(var + LN_EPS) * g + b

        def _forward(x, edge_index, W_gat, att_src, att_dst, b_gat, ln_gamma, ln_beta, W1, b1, W2, b2):
            Bc, Nc, Dc = x.shape
            M = Bc * Nc
            x_flat = x.reshape(M, Dc)
            h = (x_flat @ W_gat).reshape(M, HEADS, NUM_EXPERTS)
            loops = jnp.arange(M, dtype=edge_index.dtype)
            src = jnp.concatenate([edge_index[0], loops])
            dst = jnp.concatenate([edge_index[1], loops])
            a_src = (h * att_src).sum(-1)
            a_dst = (h * att_dst).sum(-1)
            e = jax.nn.leaky_relu(a_src[src] + a_dst[dst], negative_slope=0.2)
            e_max = jax.ops.segment_max(e, dst, num_segments=M)
            ee = jnp.exp(e - e_max[dst])
            denom = jax.ops.segment_sum(ee, dst, num_segments=M)
            alpha = ee / (denom[dst] + 1e-16)
            msg = h[src] * alpha[:, :, None]
            agg = jax.ops.segment_sum(msg, dst, num_segments=M).reshape(M, HEADS * NUM_EXPERTS) + b_gat
            scores = _layernorm(agg, ln_gamma, ln_beta).reshape(M, HEADS, NUM_EXPERTS).mean(1)
            scores = scores.reshape(Bc, Nc, NUM_EXPERTS)
            topk_s, topk_i = jax.lax.top_k(scores, TOP_K)
            w = jax.nn.softmax(topk_s, axis=-1)
            out = jnp.zeros_like(x)
            for ei in range(NUM_EXPERTS):
                g = jnp.where(topk_i == ei, w, 0.0).sum(-1)
                hh = jax.nn.gelu(x @ W1[ei] + b1[ei], approximate=False)
                out = out + g[..., None] * (hh @ W2[ei] + b2[ei])
            return out
        return _forward(x, edge_index, W_gat, att_src, att_dst, b_gat, ln_gamma, ln_beta, W1, b1, W2, b2)

    def _L1_conv_ref(lhs, rhs):
        import jax, jax.numpy as jnp
        import numpy as np
        _QMAX = 127.0

        def _quantize(x, axes):
            amax = jnp.max(jnp.abs(x), axis=axes, keepdims=True)
            scale = jnp.maximum(amax, 1e-06) / _QMAX
            q = jnp.clip(jnp.round(x / scale), -_QMAX, _QMAX)
            return (q, scale)
        qlhs, s_lhs = _quantize(lhs, axes=(1, 2, 3))
        qrhs, s_rhs = _quantize(rhs, axes=(0, 1, 2))
        dn = jax.lax.conv_dimension_numbers(lhs.shape, rhs.shape, ('NHWC', 'HWIO', 'NHWC'))
        out = jax.lax.conv_general_dilated(qlhs, qrhs, window_strides=(1, 1), padding='SAME', dimension_numbers=dn, feature_group_count=1, batch_group_count=1, preferred_element_type=jnp.float32)
        return out * s_lhs * s_rhs.reshape(1, 1, 1, -1)

    def _L1_ffn_ref(x, W_gat, att_src, att_dst, b_gat, ln_gamma, ln_beta, W1, b1, W2, b2, edge_index):
        import jax, jax.numpy as jnp
        import numpy as np
        B, N, D = (16, 4096, 256)
        NUM_EXPERTS, TOP_K, HEADS = (4, 2, 4)
        N_EDGES = 1048576
        LN_EPS = 1e-05

        def _layernorm(x, g, b):
            mu = x.mean(-1, keepdims=True)
            var = ((x - mu) ** 2).mean(-1, keepdims=True)
            return (x - mu) * jax.lax.rsqrt(var + LN_EPS) * g + b

        def _forward(x, edge_index, W_gat, att_src, att_dst, b_gat, ln_gamma, ln_beta, W1, b1, W2, b2):
            Bc, Nc, Dc = x.shape
            M = Bc * Nc
            x_flat = x.reshape(M, Dc)
            h = (x_flat @ W_gat).reshape(M, HEADS, NUM_EXPERTS)
            loops = jnp.arange(M, dtype=edge_index.dtype)
            src = jnp.concatenate([edge_index[0], loops])
            dst = jnp.concatenate([edge_index[1], loops])
            a_src = (h * att_src).sum(-1)
            a_dst = (h * att_dst).sum(-1)
            e = jax.nn.leaky_relu(a_src[src] + a_dst[dst], negative_slope=0.2)
            e_max = jax.ops.segment_max(e, dst, num_segments=M)
            ee = jnp.exp(e - e_max[dst])
            denom = jax.ops.segment_sum(ee, dst, num_segments=M)
            alpha = ee / (denom[dst] + 1e-16)
            msg = h[src] * alpha[:, :, None]
            agg = jax.ops.segment_sum(msg, dst, num_segments=M).reshape(M, HEADS * NUM_EXPERTS) + b_gat
            scores = _layernorm(agg, ln_gamma, ln_beta).reshape(M, HEADS, NUM_EXPERTS).mean(1)
            scores = scores.reshape(Bc, Nc, NUM_EXPERTS)
            topk_s, topk_i = jax.lax.top_k(scores, TOP_K)
            w = jax.nn.softmax(topk_s, axis=-1)
            out = jnp.zeros_like(x)
            for ei in range(NUM_EXPERTS):
                g = jnp.where(topk_i == ei, w, 0.0).sum(-1)
                hh = jax.nn.gelu(x @ W1[ei] + b1[ei], approximate=False)
                out = out + g[..., None] * (hh @ W2[ei] + b2[ei])
            return out
        return _forward(x, edge_index, W_gat, att_src, att_dst, b_gat, ln_gamma, ln_beta, W1, b1, W2, b2)

    def _gn(v, G=32, eps=1e-5):
        B_, H_, W_, C_ = v.shape
        g = v.reshape(B_, H_, W_, G, C_ // G)
        m = jnp.mean(g, axis=(1, 2, 4), keepdims=True)
        s = jnp.var(g, axis=(1, 2, 4), keepdims=True)
        return ((g - m) / jnp.sqrt(s + eps)).reshape(v.shape)

    def _ln_c(v, eps=1e-6):
        m = jnp.mean(v, axis=-1, keepdims=True)
        s = jnp.var(v, axis=-1, keepdims=True)
        return (v - m) / jnp.sqrt(s + eps)

    def _ln_t(v, eps=1e-5):
        m = jnp.mean(v, axis=-1, keepdims=True)
        s = jnp.var(v, axis=-1, keepdims=True)
        return (v - m) / jnp.sqrt(s + eps)

    def _to_tokens(v):
        B_, H_, W_, C_ = v.shape
        return v.reshape(B_, H_ * W_, C_)
    def _from_tokens(t, like):
        return t.reshape(like.shape)

    x = x + _L0_conv_ref(_ln_c(x), L0_conv_Wq, L0_conv_Wk, L0_conv_Wv, L0_conv_Wo, L0_conv_ln_g, L0_conv_ln_b)
    t = _to_tokens(x)
    t = t + _L0_ffn_ref(_ln_t(t), L0_ffn_W_gat, L0_ffn_att_src, L0_ffn_att_dst, L0_ffn_b_gat, L0_ffn_ln_gamma, L0_ffn_ln_beta, L0_ffn_W1, L0_ffn_b1, L0_ffn_W2, L0_ffn_b2, L0_ffn_edge_index)
    x = _from_tokens(t, x)
    x = x + _L1_conv_ref(_ln_c(x), L1_conv_rhs)
    t = _to_tokens(x)
    t = t + _L1_ffn_ref(_ln_t(t), L1_ffn_W_gat, L1_ffn_att_src, L1_ffn_att_dst, L1_ffn_b_gat, L1_ffn_ln_gamma, L1_ffn_ln_beta, L1_ffn_W1, L1_ffn_b1, L1_ffn_W2, L1_ffn_b2, L1_ffn_edge_index)
    x = _from_tokens(t, x)
    return x


_drawn_inputs = setup_inputs


def setup_inputs(seed=0):
    import zlib

    import numpy as np

    out = dict(_drawn_inputs(seed))
    spreads = {'L0_conv_ln_g': (1.0, 0.2),
     'L0_conv_ln_b': (0.0, 0.1),
     'L0_ffn_b_gat': (0.0, 0.1),
     'L0_ffn_ln_gamma': (1.0, 0.2),
     'L0_ffn_ln_beta': (0.0, 0.1),
     'L0_ffn_b1': (0.0, 0.1),
     'L0_ffn_b2': (0.0, 0.1),
     'L1_ffn_b_gat': (0.0, 0.8),
     'L1_ffn_ln_gamma': (1.0, 0.6),
     'L1_ffn_ln_beta': (0.0, 0.8),
     'L1_ffn_b1': (0.0, 0.8),
     'L1_ffn_b2': (0.0, 2.0)}
    factors = {'L1_ffn_W_gat': 7.956,
     'L1_ffn_att_src': 8.0,
     'L1_ffn_att_dst': 8.0,
     'L1_ffn_W1': 6.559,
     'L1_ffn_W2': 5.956}
    for name, (base, spread) in spreads.items():
        noise = np.random.default_rng([zlib.crc32(name.encode()), seed]).standard_normal(out[name].shape)
        drawn = base * np.exp(spread * noise) if base else spread * noise
        out[name] = jnp.asarray(drawn.astype(out[name].dtype))
    for name, factor in factors.items():
        out[name] = (out[name] * factor).astype(out[name].dtype)
    return out
```

```python
import numpy as np
import concourse.bass as bass
from concourse import mybir
from concourse.alu_op_type import AluOpType as ALU
from contextlib import ExitStack

F32 = mybir.dt.float32
BF16 = mybir.dt.bfloat16
I32 = mybir.dt.int32
U32 = mybir.dt.uint32
ACT = mybir.ActivationFunctionType
AX = mybir.AxisListType

B, N1, N2, C = 8, 32, 32, 256
L = N1 * N2
M = B * L
P = 128
TPB = L // P
NT = M // P
KK = C // P
H, KD = 8, C // 8
HPQ = P // KD
HALF = 512
MROW = (2 * N1 - 4) * N2


class Semaphores:

    def __init__(self, nc, ctx):
        self.nc, self.own = nc, []
        ctx.callback(self.clear)

    def new(self, name):
        self.own.append(self.nc.alloc_semaphore(name))
        return self.own[-1]

    def clear(self):
        self.nc.clear_and_free_semaphores(self.own)
        self.nc.all_engine_barrier()


def attention_layer(nc, x_in, x_out, w, cos_t, sin_t, qscale_t, decay_t, ln_g, ln_b, ident_in, blk_in):
    with ExitStack() as ctx:
        def sb(name, shape, dt=F32):
            return ctx.enter_context(nc.sbuf_tensor("at_" + name, shape, dt))

        semaphores = Semaphores(nc, ctx)

        def sem(name):
            return semaphores.new("at_" + name)

        decay = sb("decay", [P, H, MROW])
        cos = sb("cos", [P, L])
        sin = sb("sin", [P, L])
        qscale = sb("qscale", [P, KK, L])
        wt = sb("wt", [P, 6, KK, C])
        ident = sb("ident", [P, P])
        blk = sb("blk", [P, P])
        ones = sb("ones", [P, KD])
        gb = sb("gb", [P, 2])
        eps6 = sb("eps6", [P, TPB])
        nhalf = sb("nhalf", [P, TPB])
        eps5 = sb("eps5", [P, 1])
        xt = sb("xt", [P, TPB, C])
        xn = sb("xn", [P, TPB, C])
        g_t = xn[:, :, :].rearrange("p t c -> p (t c)").rearrange("p (k l) -> p k l", k=KK)
        xnT = sb("xnT", [P, KK, L])
        qr = sb("qr", [P, KK, L])
        kz = sb("kz", [P, H, L])
        v = sb("v", [P, TPB, C])
        kr = sb("kr", [P, 2, HALF])
        t1 = sb("t1", [P, HALF])
        t2 = sb("t2", [P, HALF])
        stats = sb("stats", [P, TPB, 6])
        mv = sb("mv", [P, TPB, 2])
        ve = sb("ve", [P, TPB])
        rstd = sb("rstd", [P, TPB])
        pr = sb("pr", [P, 3, 2, HALF])
        ab = sb("ab", [P, 3, 2, HALF])
        dn = sb("dn", [P, HALF])
        rdn = sb("rdn", [P, HALF])
        o = sb("o", [P, HALF])
        oc = sb("oc", [P, HALF])
        sq = sb("sq", [P, HALF])
        sd = sb("sd", [P, HALF])
        rsd = sb("rsd", [P, HALF])
        ps_s = [ctx.enter_context(nc.psum_tensor(f"at_ps_s{i}", [P, 2, HALF], F32)) for i in range(2)]
        ps_av = ctx.enter_context(nc.psum_tensor("at_ps_av", [P, HALF], F32))
        ps_dn = ctx.enter_context(nc.psum_tensor("at_ps_dn", [P, HALF], F32))
        ps_m = [ctx.enter_context(nc.psum_tensor(f"at_ps_m{i}", [P, HALF], F32)) for i in range(2)]

        s_const, s_cst, s_x, s_out = sem("const"), sem("cst"), sem("x"), sem("out")
        s_mv, s_ve, s_vec = sem("mv"), sem("ve"), sem("vec")
        s_rstd, s_pool = sem("rstd"), sem("pool")
        s_xn, s_tr, s_xnT = sem("xn"), sem("tr"), sem("xnT")
        s_proj, s_rot, s_kr, s_kz = sem("proj"), sem("rot"), sem("kr"), sem("kz")
        s_vps, s_v = sem("vps"), sem("v")
        s_sc, s_p, s_a, s_av = sem("sc"), sem("p"), sem("a"), sem("av")
        s_o, s_mu, s_oc, s_sq, s_var, s_sd, s_y, s_g = (sem(k) for k in ("o", "mu", "oc", "sq", "var", "sd", "y", "g"))
        s_op, s_x1 = sem("op"), sem("x1")

        NU = 64
        NG = NU // 16
        NCONST = 10

        def unit(u):
            return u // 32, (u // 16) % 2, (u // 2) % 8, u % 2

        s_turn = sem("turn")
        block = ctx.enter_context(nc.Block())

        @block.sync
        def _(sp):
            sp.dma_start(ident[:, :], ident_in).then_inc(s_const, 16)
            sp.dma_start(blk[:, :], blk_in).then_inc(s_const, 16)
            sp.dma_start(wt[:, :, :, :], w).then_inc(s_const, 16)
            sp.dma_start(cos[:, :], cos_t).then_inc(s_const, 16)
            sp.dma_start(sin[:, :], sin_t).then_inc(s_const, 16)
            sp.dma_start(qscale[:, :, :], qscale_t).then_inc(s_const, 16)
            sp.dma_start(decay[:, :, :], decay_t).then_inc(s_const, 16)
            for j in range(HPQ):
                if j == 0:
                    sp.dma_start(gb[0:KD, 0:1], ln_g).then_inc(s_const, 16)
                else:
                    sp.dma_start(gb[KD * j:KD * j + KD, 0:1], ln_g).then_inc(s_const, 16)
                sp.dma_start(gb[KD * j:KD * j + KD, 1:2], ln_b).then_inc(s_const, 16)
            with sp.Fori(0, B) as b:
                sp.dma_start(xt[:, :, :], x_in[bass.ds(b * L, L), :].rearrange("(t p) c -> p t c", p=P)).then_inc(s_x, 16)
                sp.wait_ge(s_x1, b * TPB + TPB)
                sp.sem_inc(s_turn, 1)
                sp.dma_start(x_out[bass.ds(b * L, L), :].rearrange("(t p) c -> p t c", p=P), xt[:, :, :]).then_inc(s_out, 16)
                sp.wait_ge(s_out, b * 16 + 16)
                sp.sem_inc(s_turn, 1)
            sp.wait_ge(s_out, B * 16)

        @block.gpsimd
        def _(pool):
            pool.memset(kz[:, :, :], 0.0).then_inc(s_cst, 1)
            pool.memset(ones[:, :], 1.0).then_inc(s_cst, 1)
            pool.memset(nhalf[:, :], -0.5).then_inc(s_cst, 1)
            pool.memset(eps5[:, :], 1e-5).then_inc(s_cst, 1)
            pool.wait_ge(s_cst, 4)
            with pool.Fori(0, B) as b:
                pool.wait_ge(s_ve, b + 1)
                pool.tensor_tensor(rstd[:, :], ve[:, :], nhalf[:, :], ALU.pow).then_inc(s_rstd, 1)
                for g in range(4):
                    pool.wait_ge(s_kr, b * 4 + (g + 1))
                    pool.sem_inc(s_pool, 1)
                    hq, n = g // 2, g % 2
                    for j in range(HPQ):
                        last = pool.tensor_copy(kz[KD * j:KD * j + KD, HPQ * hq + j, HALF * n:HALF * n + HALF],
                                                kr[KD * j:KD * j + KD, g % 2, :])
                    last.then_inc(s_kz, 1)
                for g in range(NG):
                    pool.wait_ge(s_oc, b * NG + (g + 1))
                    pool.tensor_tensor(sq[:, :], oc[:, :], oc[:, :], ALU.mult).then_inc(s_sq, 1)

        @block.scalar
        def _(act):
            act.wait_ge(s_const, 16 * (7 + 2 * HPQ))
            act.wait_ge(s_cst, 4)
            with act.Fori(0, B) as b:
                for t in range(TPB // 2):
                    act.wait_ge(s_tr, b * 4 + (t + 1))
                    act.activation(xnT[:, :, 2 * P * t:2 * P * t + 2 * P],
                                   ps_m[t % 2][:, :].rearrange("p (k c) -> p k c", k=KK), ACT.Copy).then_inc(s_xnT, 1)
                for t in range(TPB // 2):
                    act.wait_ge(s_vps, b * 4 + (t + 1))
                    act.activation(v[:, 2 * t:2 * t + 2, :], ps_m[t % 2][:, :].rearrange("p (k c) -> p k c", k=2),
                                   ACT.Copy).then_inc(s_v, 1)

                def head_sd(g):
                    act.wait_ge(s_var, b * NG + (g + 1))
                    act.activation(sd[:, :], ps_m[1][:, :], ACT.Sqrt, bias=eps5[:, 0:1]).then_inc(s_sd, 1)

                for u in range(NU):
                    act.wait_ge(s_p, b * NU + (u + 1))
                    if u >= 3:
                        act.wait_ge(s_av, b * NU + (u - 2))
                    act.activation(ab[:, u % 3, :, :], pr[:, u % 3, :, :], ACT.Abs).then_inc(s_a, 1)
                    if u >= 24 and (u - 24) % 16 == 0:
                        head_sd((u - 24) // 16)
                head_sd(NG - 1)
                for g in range(NG):
                    act.wait_ge(s_y, b * NG + (g + 1))
                    dst = g_t[:, g // 2, HALF * (g % 2):HALF * (g % 2) + HALF]
                    act.activation(dst, dst, ACT.Gelu, bias=gb[:, 1:2], scale=gb[:, 0:1]).then_inc(s_g, 1)

        @block.vector
        def _(dve):
            steps = [0]

            def then(ins):
                steps[0] += 1
                ins.then_inc(s_vec, 1)
                dve.wait_ge(s_vec, steps[0])

            dve.wait_ge(s_const, 16 * (7 + 2 * HPQ))
            dve.wait_ge(s_cst, 4)
            with dve.Fori(0, B) as b:
                dve.wait_ge(s_x, b * 16 + 16)
                for t in range(TPB):
                    ins = dve.bn_stats(stats[:, t, :], xt[:, t, :])
                then(ins)
                for t in range(TPB):
                    ins = dve.bn_aggr(mv[:, t, :], stats[:, t, :])
                then(ins)
                dve.tensor_scalar(ve[:, :], mv[:, :, 1], 1e-6, None, ALU.add).then_inc(s_ve, 1)
                dve.wait_ge(s_rstd, b + 1)
                for t in range(TPB):
                    dve.tensor_scalar(xn[:, t, :], xt[:, t, :], mv[:, t, 0:1], rstd[:, t:t + 1],
                                      ALU.subtract, ALU.mult).then_inc(s_xn, 1)
                for g in range(8):
                    hq, n = (g // 2) % 2, g % 2
                    cols = slice(HALF * n, HALF * n + HALF)
                    dve.wait_ge(s_proj, b * 8 + (g + 1))
                    if g > 0:
                        if g <= 4:
                            dve.wait_ge(s_rot, b * 4 + g)
                        else:
                            dve.wait_ge(s_kr, b * 4 + (g - 4))
                    dve.tensor_tensor(t1[:, :], ps_s[g % 2][:, 0, :], cos[:, cols], ALU.mult)
                    then(dve.tensor_tensor(t2[:, :], ps_s[g % 2][:, 1, :], sin[:, cols], ALU.mult))
                    if g < 4:
                        then(dve.tensor_tensor(t1[:, :], t1[:, :], t2[:, :], ALU.add))
                        ins = dve.tensor_tensor(qr[:, hq, cols], t1[:, :], qscale[:, hq, cols], ALU.mult)
                        ins.then_inc(s_rot, 1)
                    else:
                        if g >= 6:
                            dve.wait_ge(s_kz, b * 4 + (g - 5))
                        dve.tensor_tensor(kr[:, g % 2, :], t1[:, :], t2[:, :], ALU.add).then_inc(s_kr, 1)

                def take_output(g):
                    dve.wait_ge(s_av, b * NU + (16 * g + 16))
                    then(dve.tensor_scalar(dn[:, :], ps_dn[:, :], 1.0, 50000.0, ALU.max, ALU.min))
                    then(dve.reciprocal(rdn[:, :], dn[:, :]))
                    dve.tensor_tensor(o[:, :], ps_av[:, :], rdn[:, :], ALU.mult).then_inc(s_o, 1)

                def centre(g):
                    dve.wait_ge(s_o, b * NG + (g + 1))
                    dve.wait_ge(s_mu, b * NG + (g + 1))
                    dve.tensor_tensor(oc[:, :], o[:, :], ps_m[0][:, :], ALU.subtract).then_inc(s_oc, 1)

                def scale(g):
                    dve.wait_ge(s_oc, b * NG + (g + 1))
                    dve.wait_ge(s_sd, b * NG + (g + 1))
                    then(dve.reciprocal(rsd[:, :], sd[:, :]))
                    dve.tensor_tensor(g_t[:, g // 2, HALF * (g % 2):HALF * (g % 2) + HALF],
                                      oc[:, :], rsd[:, :], ALU.mult).then_inc(s_y, 1)

                for u in range(NU):
                    hq, qn, kb, jp = unit(u)
                    h = HPQ * hq + 2 * jp
                    first = (N1 - 4 + (N1 // 2) * qn - 4 * kb) * N2
                    dve.wait_ge(s_sc, b * NU + (u + 1))
                    if u >= 3:
                        dve.wait_ge(s_av, b * NU + (u - 2))
                        dve.wait_ge(s_a, b * NU + (u - 2))
                    dve.tensor_tensor(pr[:, u % 3, :, :], ps_s[u % 2][:, :, :],
                                      decay[:, h:h + 2, first:first + HALF], ALU.mult).then_inc(s_p, 1)
                    if u >= 17 and (u - 17) % 16 == 0:
                        take_output((u - 17) // 16)
                    if u >= 20 and (u - 20) % 16 == 0:
                        centre((u - 20) // 16)
                    if u >= 25 and (u - 25) % 16 == 0:
                        scale((u - 25) // 16)
                take_output(NG - 1)
                centre(NG - 1)
                scale(NG - 1)
                for t in range(TPB):
                    dve.wait_ge(s_op, b * TPB + (t + 1))
                    dve.tensor_tensor(xt[:, t, :], ps_m[t % 2][:, 0:C], xt[:, t, :], ALU.add).then_inc(s_x1, 1)
                dve.sem_clear(s_vec)

        @block.tensor
        def _(pe):
            pe.wait_ge(s_const, 16 * (7 + 2 * HPQ))
            pe.wait_ge(s_cst, 4)
            with pe.Fori(0, B) as b:
                for t in range(TPB // 2):
                    pe.wait_ge(s_xn, b * TPB + (2 * t + 2))
                    if t >= 2:
                        pe.wait_ge(s_xnT, b * 4 + (t - 1))
                    for k in range(KK):
                        for s in range(2):
                            at = (2 * k + s) * P
                            ins = pe.transpose(ps_m[t % 2][:, at:at + P], xn[:, 2 * t + s, P * k:P * k + P], ident[:, :])
                    ins.then_inc(s_tr, 1)
                for g in range(8):
                    which, hq, n = 2 * (g // 4), (g // 2) % 2, g % 2
                    pe.wait_ge(s_xnT, b * 4 + 4)
                    if g >= 2:
                        if g - 2 < 4:
                            pe.wait_ge(s_rot, b * 4 + (g - 1))
                        else:
                            pe.wait_ge(s_kr, b * 4 + (g - 5))
                    for s in range(2):
                        for k in range(KK):
                            ins = pe.matmul(ps_s[g % 2][:, s, :], wt[:, which + s, k, P * hq:P * hq + P],
                                            xnT[:, k, HALF * n:HALF * n + HALF], start=(k == 0), stop=(k == KK - 1))
                    ins.then_inc(s_proj, 1)
                for t in range(TPB // 2):
                    if t >= 2:
                        pe.wait_ge(s_v, b * 4 + (t - 1))
                    for s in range(2):
                        for k in range(KK):
                            ins = pe.matmul(ps_m[t % 2][:, C * s:C * s + C], xnT[:, k, (2 * t + s) * P:(2 * t + s + 1) * P],
                                            wt[:, 4, k, :], start=(k == 0), stop=(k == KK - 1))
                    ins.then_inc(s_vps, 1)

                pe.wait_ge(s_kr, b * 4 + 4)
                pe.wait_ge(s_rot, b * 4 + 4)
                pe.wait_ge(s_kz, b * 4 + 4)
                pe.wait_ge(s_v, b * 4 + 4)

                def scores(u):
                    hq, qn, kb, jp = unit(u)
                    if u >= 2:
                        pe.wait_ge(s_p, b * NU + (u - 1))
                    for jj in range(2):
                        h = HPQ * hq + 2 * jp + jj
                        ins = pe.matmul(ps_s[u % 2][:, jj, :], kz[:, h, P * kb:P * kb + P],
                                        qr[:, hq, HALF * qn:HALF * qn + HALF], start=True, stop=True)
                    ins.then_inc(s_sc, 1)

                def products(u):
                    hq, qn, kb, jp = unit(u)
                    if u % 16 == 0 and u > 0:
                        pe.wait_ge(s_o, b * NG + u // 16)
                    pe.wait_ge(s_a, b * NU + (u + 1))
                    for jj in range(2):
                        j = 2 * jp + jj
                        h = HPQ * hq + j
                        pe.matmul(ps_av[KD * j:KD * j + KD, :], v[:, kb, KD * h:KD * h + KD], pr[:, u % 3, jj, :],
                                  start=(kb == 0), stop=(kb == 7), tile_position=(0, KD * j), skip_group_check=True)
                        ins = pe.matmul(ps_dn[KD * j:KD * j + KD, :], ones[:, :], ab[:, u % 3, jj, :],
                                        start=(kb == 0), stop=(kb == 7), tile_position=(0, KD * j), skip_group_check=True)
                    ins.then_inc(s_av, 1)

                def mean(g):
                    pe.wait_ge(s_o, b * NG + (g + 1))
                    pe.matmul(ps_m[0][:, :], blk[:, :], o[:, :], start=True, stop=True).then_inc(s_mu, 1)

                def variance(g):
                    pe.wait_ge(s_sq, b * NG + (g + 1))
                    pe.matmul(ps_m[1][:, :], blk[:, :], sq[:, :], start=True, stop=True).then_inc(s_var, 1)

                for u in range(NU + 2):
                    if u < NU:
                        scores(u)
                    if u >= 2:
                        products(u - 2)
                    if u >= 19 and (u - 19) % 16 == 0:
                        mean((u - 19) // 16)
                    if u >= 23 and (u - 23) % 16 == 0:
                        variance((u - 23) // 16)
                mean(NG - 1)
                variance(NG - 1)
                pe.wait_ge(s_g, b * NG + NG)
                for t in range(TPB):
                    if t >= 2:
                        pe.wait_ge(s_x1, b * TPB + (t - 1))
                    for k in range(KK):
                        ins = pe.matmul(ps_m[t % 2][:, 0:C], g_t[:, k, P * t:P * t + P], wt[:, 5, k, :],
                                        start=(k == 0), stop=(k == KK - 1))
                    ins.then_inc(s_op, 1)


def attention_constants():
    half = (1.0 / 10000.0 ** np.linspace(0.0, 1.0, KD // 2).astype(np.float32)).astype(np.float32)
    angle = np.repeat(half, 2)
    index = (np.arange(N1)[:, None] + np.arange(N2)[None, :]).reshape(L).astype(np.float32)
    phase = (index[:, None] * angle[None, :]).astype(np.float32).astype(np.float64)
    sign = np.where(np.arange(KD) % 2 == 0, -1.0, 1.0)
    cos = np.tile(np.cos(phase).T, (HPQ, 1)).astype(np.float32)
    sin = np.tile((np.sin(phase) * sign).T, (HPQ, 1)).astype(np.float32)
    decay = np.log(1.0 - 2.0 ** (-2.0 - 5.0 * np.arange(H) / H))
    d1 = np.abs(np.arange(N1)[:, None] - np.arange(N1)[None, :])
    line = np.exp(d1[None] * decay[:, None, None]).sum(-1)
    total = (line[:, :, None] * line[:, None, :]).reshape(H, L)
    r = KD ** -0.5 / np.sqrt(total)
    qscale = np.repeat(r, KD, axis=0).reshape(KK, P, L).transpose(1, 0, 2).astype(np.float32)
    part = np.arange(P)
    delta = np.arange(2 * N1 - 4) - (N1 - 4)
    dist = (np.abs(delta[None, :, None] - (part // N2)[:, None, None])
            + np.abs(np.arange(N2)[None, None, :] - (part % N2)[:, None, None]))
    table = np.exp(dist[:, None] * decay[None, :, None, None]).reshape(P, H, MROW).astype(np.float32)
    blk = np.kron(np.eye(HPQ), np.full((KD, KD), 1.0 / KD)).astype(np.float32)
    return cos, sin, np.ascontiguousarray(qscale), table, blk, np.eye(P, dtype=np.float32)
GH, GE = 4, 4
GF = GH * GE
HSW = GF + GH
STW = GH + GH + GH + GF
NE = 1048576
EC = NE // P
ECH = 2048
TABLES = 4
HIST = 32
CODE_BASE = 0x10000000


def edge_lists(nc, tag, edges, iota_in, codes, count, edges_left):
    with ExitStack() as ctx:
        def sb(name, shape, dt=F32):
            return ctx.enter_context(nc.sbuf_tensor(f"{tag}el_{name}", shape, dt))

        semaphores = Semaphores(nc, ctx)

        def sem(name):
            return semaphores.new(f"{tag}el_s_{name}")

        src = sb("src", [P, 2, ECH], I32)
        dst = sb("dst", [P, 2, ECH], I32)
        sf = sb("sf", [P, ECH])
        df = sb("df", [P, ECH])
        fa = sb("fa", [P, ECH])
        fb = sb("fb", [P, ECH])
        ia = sb("ia", [P, ECH], I32)
        ib = sb("ib", [P, ECH], I32)
        code = sb("code", [P, EC], I32)
        lo = sb("lo", [P, EC], BF16)
        hi = sb("hi", [P, EC], BF16)
        iota = sb("iota", [P, P], BF16)
        one_lo = sb("one_lo", [P, 2, HIST, P], BF16)
        one_hi = sb("one_hi", [P, 2, HIST, NT], BF16)
        zero = sb("zero", [P, P], BF16)
        part = sb("part", [P, EC // ECH])
        tot = sb("tot", [P, 1])
        top = sb("top", [P, 1])
        m8 = sb("m8", [P, 8], F32)
        ps = ctx.enter_context(nc.psum_tensor(f"{tag}el_ps", [P, NT], F32))
        s_in, s_vec, s_free, s_tot, s_top, s_zero = (
            sem("iota"), sem("vec"), sem("free"), sem("tot"), sem("top"), sem("zero"))
        s_edges = [sem("edges0"), sem("edges1")]
        s_one, s_hist, s_left, s_loop = (sem(k) for k in ("one", "hist", "left", "loop"))
        NCH = EC // ECH
        NH = EC // HIST // 2
        edges_v = edges.rearrange("a (p n) -> a p n", p=P)
        block = ctx.enter_context(nc.Block())

        @block.sync
        def _(sp):
            sp.dma_start(iota[:, :], iota_in).then_inc(s_in, 16)
            for c in range(NCH):
                if c >= 2:
                    sp.wait_ge(s_free, c - 1)
                sp.dma_start(src[:, c % 2, :], edges_v[0, :, ECH * c:ECH * c + ECH]).then_inc(s_edges[c % 2], 16)
                sp.dma_start(dst[:, c % 2, :], edges_v[1, :, ECH * c:ECH * c + ECH]).then_inc(s_edges[c % 2], 16)

        @block.gpsimd
        def _(pool):
            pool.memset(zero[:, :], 0.0).then_inc(s_zero, 1)
            pool.wait_ge(s_tot, 1)
            pool.partition_all_reduce(top[:, :], tot[:, :], P, bass.bass_isa.ReduceOp.max).then_inc(s_top, 1)

        @block.tensor
        def _(pe):
            pe.wait_ge(s_zero, 1)
            pe.matmul(ps[:, :], zero[:, :], zero[:, 0:NT], start=True, stop=False, skip_group_check=True)
            with pe.Fori(0, NH) as i:
                for s in range(2):
                    pe.wait_ge(s_one, i * 2 + (s + 1))
                    for j in range(HIST):
                        ins = pe.matmul(ps[:, :], one_lo[:, s, j, :], one_hi[:, s, j, :], start=False, stop=False,
                                        skip_group_check=True)
                    ins.then_inc(s_hist, 1)
            pe.matmul(ps[:, :], zero[:, :], zero[:, 0:NT], start=False, stop=True, skip_group_check=True).then_inc(s_hist, 1)

        @block.vector
        def _(dve):
            steps = [0]

            def then(ins):
                steps[0] += 1
                ins.then_inc(s_vec, 1)
                dve.wait_ge(s_vec, steps[0])

            dve.wait_ge(s_in, 16)
            for c in range(NCH):
                dve.wait_ge(s_edges[c % 2], 32 * (c // 2 + 1))
                s, cols = c % 2, slice(ECH * c, ECH * c + ECH)
                then(dve.tensor_scalar(sf[:, :], src[:, s, :], float(-M), float(M - 1), ALU.max, ALU.min))
                then(dve.tensor_scalar(fa[:, :], sf[:, :], 0.0, float(M), ALU.is_lt, ALU.mult))
                then(dve.tensor_tensor(sf[:, :], sf[:, :], fa[:, :], ALU.add))
                then(dve.tensor_scalar(df[:, :], dst[:, s, :], -1.0, float(M), ALU.max, ALU.min))
                then(dve.tensor_scalar(fa[:, :], df[:, :], 0.0, None, ALU.is_ge))
                then(dve.scalar_tensor_tensor(fb[:, :], df[:, :], float(M), fa[:, :], ALU.is_lt, ALU.mult))
                then(dve.scalar_tensor_tensor(fa[:, :], sf[:, :], float(M - 1), fb[:, :], ALU.is_lt, ALU.mult))
                then(dve.tensor_reduce(part[:, c:c + 1], fa[:, :], AX.X, ALU.add))
                then(dve.tensor_copy(ia[:, :], sf[:, :]))
                then(dve.tensor_copy(ib[:, :], df[:, :]))
                then(dve.tensor_scalar(code[:, cols], ib[:, :], 13, CODE_BASE, ALU.logical_shift_left, ALU.bitwise_or))
                then(dve.tensor_tensor(ia[:, :], ia[:, :], code[:, cols], ALU.bitwise_or))
                ins = dve.tensor_scalar(code[:, cols], fa[:, :], -1.0, None, ALU.mult)
                then(ins)
                then(dve.tensor_tensor(code[:, cols], code[:, cols], ia[:, :], ALU.bitwise_and))
                then(dve.tensor_tensor(fb[:, :], fb[:, :], fa[:, :], ALU.subtract))
                then(dve.tensor_scalar(ia[:, :], ib[:, :], P - 1, None, ALU.bitwise_and))
                then(dve.tensor_copy(lo[:, cols], ia[:, :]))
                then(dve.tensor_scalar(ia[:, :], ib[:, :], 7, None, ALU.arith_shift_right))
                then(dve.tensor_copy(df[:, :], ia[:, :]))
                then(dve.scalar_tensor_tensor(fa[:, :], df[:, :], 1.0, fb[:, :], ALU.add, ALU.mult))
                then(dve.tensor_scalar(hi[:, cols], fa[:, :], -1.0, None, ALU.add))
                dve.nop().then_inc(s_free, 1)
            dve.tensor_reduce(tot[:, :], part[:, :], AX.X, ALU.add).then_inc(s_tot, 1)
            with dve.Fori(0, NH) as i:
                for s in range(2):
                    dve.wait_ge(s_loop, i * 2 + (s + 1))
                    cols = bass.ds(i * (2 * HIST) + s * HIST, HIST)
                    dve.tensor_tensor(one_lo[:, s, :, :], iota[:, :].unsqueeze(1).to_broadcast([P, HIST, P]),
                                      lo[:, cols].unsqueeze(2).to_broadcast([P, HIST, P]), ALU.is_equal)
                    dve.tensor_tensor(one_hi[:, s, :, :], iota[:, 0:NT].unsqueeze(1).to_broadcast([P, HIST, NT]),
                                      hi[:, cols].unsqueeze(2).to_broadcast([P, HIST, NT]), ALU.is_equal).then_inc(s_one, 1)
            dve.wait_ge(s_hist, 2 * NH + 1)
            then(dve.tensor_copy(count[:, :], ps[:, :]))
            dve.wait_ge(s_top, 1)
            then(dve.tensor_scalar(ia[:, 0:1], top[:, :], 7.0, 8.0, ALU.add, ALU.max))
            then(dve.tensor_scalar(edges_left[:, 0:1], ia[:, 0:1], 3, None, ALU.logical_shift_right))
            n = dve.value_load(edges_left[0:1, 0:1], min_val=1, max_val=EC // 8)
            steps_before = steps[0]
            dve.sem_clear(s_vec)
            codef = code[:, :].bitcast(F32)
            with dve.Fori(0, n) as i:
                steps[0] = 0
                then(dve.max(m8[:, :], codef))
                then(dve.tensor_copy(codes[:, bass.ds(i * 8, 8)], m8[:, :].bitcast(I32)))
                then(dve.match_replace(codef, m8[:, :], codef, 0.0))
                dve.sem_clear(s_vec)

        @block.scalar
        def _(act):
            act.sem_inc(s_loop, 2)
            with act.Fori(0, NH) as i:
                for s in range(2):
                    act.wait_ge(s_hist, i * 2 + (s + 1))
                    act.sem_inc(s_loop, 1)
GTOK = 1024
NGT = M // GTOK


def normalised_nodes(nc, tag, x_in, tT, hs_rows, ad, w_gat, att_src, att_dst, ident_in):
    with ExitStack() as ctx:
        def sb(name, shape, dt=F32):
            return ctx.enter_context(nc.sbuf_tensor(f"{tag}nn_{name}", shape, dt))

        semaphores = Semaphores(nc, ctx)

        def sem(name):
            return semaphores.new(f"{tag}nn_s_{name}")

        ident = sb("ident", [P, P])
        wg = sb("wg", [P, KK, GF])
        a_s = sb("a_s", [P, GF])
        a_d = sb("a_d", [P, GF])
        xt = sb("xt", [P, 2, TPB, C])
        xn = sb("xn", [P, 2, TPB, C])
        xnT = sb("xnT", [P, 2, KK, L])
        stats = sb("stats", [P, TPB, 6])
        mv = sb("mv", [P, TPB, 2])
        ve = sb("ve", [P, TPB])
        nhalf = sb("nhalf", [P, TPB])
        rstd = sb("rstd", [P, TPB])
        hs = sb("hs", [P, 2, TPB, HSW])
        tmp = sb("tmp", [P, TPB, GF])
        tmp2 = sb("tmp2", [P, TPB, GF])
        ps = [ctx.enter_context(nc.psum_tensor(f"{tag}nn_ps{i}", [P, 512], F32)) for i in range(2)]
        ps_h = [ctx.enter_context(nc.psum_tensor(f"{tag}nn_psh{i}", [P, TPB, GF], F32)) for i in range(2)]
        s_const, s_half = sem("const"), sem("half")
        s_x = [sem("x0"), sem("x1")]
        s_tT = [sem("tT0"), sem("tT1")]
        s_hs = [sem("hs0"), sem("hs1")]
        s_vec, s_ve, s_rstd, s_xn, s_tr, s_xnT, s_h, s_hsb, s_left = (
            sem(k) for k in ("vec", "ve", "rstd", "xn", "tr", "xnT", "h", "hsb", "left"))
        HALFG = NGT // 2
        s_turn = sem("turn")
        block = ctx.enter_context(nc.Block())

        @block.sync
        def _(sp):
            sp.dma_start(ident[:, :], ident_in).then_inc(s_const, 16)
            sp.dma_start(wg[:, :, :], w_gat).then_inc(s_const, 16)
            sp.dma_start(a_s[:, :], att_src.to_broadcast([P, GF])).then_inc(s_const, 16)
            sp.dma_start(a_d[:, :], att_dst.to_broadcast([P, GF])).then_inc(s_const, 16)
            with sp.Fori(0, HALFG) as i:
                for s in range(2):
                    sp.wait_ge(s_xn, i * (2 * TPB) + (s * TPB + TPB))
                    sp.sem_inc(s_turn, 1)
                    sp.dma_start(xt[:, s, :, :], x_in[bass.ds(i * (2 * L) + s * L, L), :]
                                 .rearrange("(t p) c -> p t c", p=P)).then_inc(s_x[s], 16)

        @block.gpsimd
        def _(pool):
            pool.memset(nhalf[:, :], -0.5).then_inc(s_half, 1)
            pool.sem_inc(s_xn, 2 * TPB)
            pool.wait_ge(s_half, 1)
            with pool.Fori(0, HALFG) as i:
                for s in range(2):
                    pool.wait_ge(s_ve, i * 2 + (s + 1))
                    pool.tensor_tensor(rstd[:, :], ve[:, :], nhalf[:, :], ALU.pow).then_inc(s_rstd, 1)

        @block.vector
        def _(dve):
            steps = [0]

            def then(ins):
                steps[0] += 1
                ins.then_inc(s_vec, 1)
                dve.wait_ge(s_vec, steps[0])

            dve.wait_ge(s_const, 64)
            with dve.Fori(0, HALFG) as i:
                steps[0] = 0
                for s in range(2):
                    dve.wait_ge(s_x[s], i * 16 + 16)
                    for t in range(TPB):
                        ins = dve.bn_stats(stats[:, t, :], xt[:, s, t, :])
                    then(ins)
                    for t in range(TPB):
                        ins = dve.bn_aggr(mv[:, t, :], stats[:, t, :])
                    then(ins)
                    dve.tensor_scalar(ve[:, :], mv[:, :, 1], 1e-5, None, ALU.add).then_inc(s_ve, 1)
                    dve.wait_ge(s_rstd, i * 2 + (s + 1))
                    dve.wait_ge(s_tr, i * 8 + (4 * s + 4))
                    for t in range(TPB):
                        dve.tensor_scalar(xn[:, s, t, :], xt[:, s, t, :], mv[:, t, 0:1], rstd[:, t:t + 1],
                                          ALU.subtract, ALU.mult).then_inc(s_xn, 1)
                    dve.wait_ge(s_h, i * 2 + (s + 1))
                    dve.wait_ge(s_left, i + 1)
                    f = ps_h[s][:, :, :]
                    then(dve.tensor_copy(hs[:, s, :, 0:GF], f))
                    then(dve.tensor_tensor(tmp[:, :, :], f, a_s[:, :].unsqueeze(1).to_broadcast([P, TPB, GF]), ALU.mult))
                    then(dve.tensor_tensor(tmp2[:, :, :], f, a_d[:, :].unsqueeze(1).to_broadcast([P, TPB, GF]), ALU.mult))
                    dve.tensor_reduce(hs[:, s, :, GF:HSW], tmp[:, :, :].rearrange("p t (h e) -> p t h e", e=GE),
                                      AX.X, ALU.add).then_inc(s_hsb, 1)
                    then(dve.tensor_reduce(ad[:, bass.ds(i * (2 * TPB) + s * TPB, TPB), :],
                                           tmp2[:, :, :].rearrange("p t (h e) -> p t h e", e=GE), AX.X, ALU.add))
                dve.sem_clear(s_vec)

        @block.tensor
        def _(pe):
            pe.wait_ge(s_const, 64)
            pe.sem_inc(s_tr, 8)
            with pe.Fori(0, HALFG) as i:
                for s in range(2):
                    for t in range(TPB // 2):
                        pe.wait_ge(s_xn, i * (2 * TPB) + (2 * TPB + s * TPB + 2 * t + 2))
                        pe.wait_ge(s_xnT, i * 8 + (4 * s + t + 1))
                        for k in range(KK):
                            for q in range(2):
                                at = (2 * k + q) * P
                                ins = pe.transpose(ps[t % 2][:, at:at + P], xn[:, s, 2 * t + q, P * k:P * k + P], ident[:, :])
                        ins.then_inc(s_tr, 1)
                    pe.wait_ge(s_xnT, i * 8 + (4 * s + 6))
                    pe.wait_ge(s_hsb, i * 2 + (s + 1))
                    for t in range(TPB):
                        for k in range(KK):
                            ins = pe.matmul(ps_h[s][:, t, :], xnT[:, s, k, P * t:P * t + P], wg[:, k, :],
                                            start=(k == 0), stop=(k == KK - 1))
                    ins.then_inc(s_h, 1)

        @block.scalar
        def _(act):
            act.sem_inc(s_xnT, 2)
            act.sem_inc(s_hsb, 2)
            act.sem_inc(s_left, 1)
            with act.Fori(0, HALFG) as i:
                for s in range(2):
                    act.wait_ge(s_hsb, i * 2 + (s + 1))
                    for t in range(TPB // 2):
                        act.wait_ge(s_tr, i * 8 + (8 + 4 * s + t + 1))
                        act.activation(xnT[:, s, :, 2 * P * t:2 * P * t + 2 * P],
                                       ps[t % 2][:, :].rearrange("p (k c) -> p k c", k=KK), ACT.Copy).then_inc(s_xnT, 1)
                    act.wait_ge(s_xnT, i * 8 + (4 * s + 6))
                    act.dma_start(tT[bass.ds(i * 2 + s, 1), :, :, :].rearrange("a p k l -> p (a k l)"),
                                  xnT[:, s, :, :].rearrange("p k l -> p (k l)")).then_inc(s_tT[s], 16)
                    act.wait_ge(s_hsb, i * 2 + (s + 3))
                    act.dma_start(hs_rows[bass.ds(i * (2 * L) + s * L, L), :].rearrange("(t p) c -> p t c", p=P),
                                  hs[:, s, :, :]).then_inc(s_hs[s], 16)
                for s in range(2):
                    act.wait_ge(s_tT[s], i * 16 + 16)
                    act.wait_ge(s_hs[s], i * 16 + 16)
                act.sem_inc(s_left, 1)
            for s in range(2):
                act.wait_ge(s_tT[s], 16 * HALFG)
                act.wait_ge(s_hs[s], 16 * HALFG)


def target_rows(nc, tag, hs_rows, ad, count, st):
    with ExitStack() as ctx:
        def sb(name, shape, dt=F32):
            return ctx.enter_context(nc.sbuf_tensor(f"{tag}tr_{name}", shape, dt))

        semaphores = Semaphores(nc, ctx)

        def sem(name):
            return semaphores.new(f"{tag}tr_s_{name}")

        hs = sb("hs", [P, NT, HSW])
        last = sb("last", [P, HSW])
        row = sb("row", [P, NT, STW])
        row0 = sb("row0", [P, NT, STW])
        es = sb("es", [P, NT, GH])
        el = sb("el", [P, NT, GH])
        tm = sb("tm", [P, NT, GH])
        cz = sb("cz", [P, NT])
        ps_, pl = sb("ps", [P, NT, GH]), sb("pl", [P, NT, GH])
        acc = sb("acc", [P, NT, GF])
        acc2 = sb("acc2", [P, NT, GF])
        s_in, s_vec, s_e, s_p, s_done, s_out = (sem(k) for k in ("in", "vec", "e", "p", "done", "out"))
        s_turn = sem("turn")
        block = ctx.enter_context(nc.Block())

        @block.sync
        def _(sp):
            sp.dma_start(hs[:, :, :], hs_rows[:, :].rearrange("(t p) c -> p t c", p=P)).then_inc(s_in, 16)
            sp.dma_start(last[:, :], hs_rows[M - 1:M, :].to_broadcast([P, HSW])).then_inc(s_in, 16)
            sp.wait_ge(s_done, 1)
            sp.dma_start(st[0, :, :].rearrange("(t p) c -> p t c", p=P), row0[:, :, :]).then_inc(s_out, 16)
            for k in range(1, TABLES):
                sp.dma_start(st[k, :, :].rearrange("(t p) c -> p t c", p=P), row[:, :, :]).then_inc(s_out, 16)
            sp.wait_ge(s_out, 16 * TABLES)

        @block.scalar
        def _(act):
            act.wait_ge(s_e, 1)
            act.activation(ps_[:, :, :], es[:, :, :], ACT.Exp).then_inc(s_p, 1)
            act.activation(pl[:, :, :], el[:, :, :], ACT.Exp).then_inc(s_p, 1)

        @block.vector
        def _(dve):
            steps = [0]

            def then(ins):
                steps[0] += 1
                ins.then_inc(s_vec, 1)
                dve.wait_ge(s_vec, steps[0])

            def leaky(out, z, t):
                then(dve.tensor_scalar(t, z, 0.2, None, ALU.mult))
                then(dve.tensor_tensor(out, z, t, ALU.max))

            dve.wait_ge(s_in, 32)
            then(dve.tensor_tensor(es[:, :, :], hs[:, :, GF:HSW], ad[:, :, :], ALU.add))
            leaky(es[:, :, :], es[:, :, :], tm[:, :, :])
            then(dve.tensor_tensor(el[:, :, :], ad[:, :, :], last[:, GF:HSW].unsqueeze(1).to_broadcast([P, NT, GH]), ALU.add))
            leaky(el[:, :, :], el[:, :, :], tm[:, :, :])
            m = row[:, :, GH:2 * GH]
            then(dve.tensor_scalar(cz[:, :], count[:, :], 1.0, None, ALU.min))
            then(dve.tensor_tensor(tm[:, :, :], el[:, :, :], es[:, :, :], ALU.subtract))
            then(dve.tensor_scalar(tm[:, :, :], tm[:, :, :], 0.0, None, ALU.max))
            then(dve.tensor_tensor(tm[:, :, :], tm[:, :, :], cz[:, :].unsqueeze(2).to_broadcast([P, NT, GH]), ALU.mult))
            then(dve.tensor_tensor(m, es[:, :, :], tm[:, :, :], ALU.add))
            then(dve.tensor_tensor(es[:, :, :], es[:, :, :], m, ALU.subtract))
            then(dve.tensor_tensor(el[:, :, :], el[:, :, :], m, ALU.subtract))
            dve.tensor_scalar(el[:, :, :], el[:, :, :], 0.0, None, ALU.min).then_inc(s_e, 1)
            dve.memset(row[:, :, 2 * GH:STW], 0.0)
            then(dve.tensor_copy(row[:, :, 0:GH], ad[:, :, :]))
            then(dve.tensor_copy(row0[:, :, 0:2 * GH], row[:, :, 0:2 * GH]))
            dve.wait_ge(s_p, 2)
            then(dve.tensor_tensor(pl[:, :, :], pl[:, :, :], count[:, :].unsqueeze(2).to_broadcast([P, NT, GH]), ALU.mult))
            then(dve.tensor_tensor(row0[:, :, 2 * GH:3 * GH], ps_[:, :, :], pl[:, :, :], ALU.add))
            for h in range(GH):
                own = hs[:, :, GE * h:GE * h + GE]
                then(dve.tensor_tensor(acc[:, :, GE * h:GE * h + GE], own,
                                       ps_[:, :, h:h + 1].to_broadcast([P, NT, GE]), ALU.mult))
                then(dve.tensor_tensor(acc2[:, :, GE * h:GE * h + GE],
                                       last[:, GE * h:GE * h + GE].unsqueeze(1).to_broadcast([P, NT, GE]),
                                       pl[:, :, h:h + 1].to_broadcast([P, NT, GE]), ALU.mult))
            dve.tensor_tensor(row0[:, :, 3 * GH:STW], acc[:, :, :], acc2[:, :, :], ALU.add).then_inc(s_done, 1)


def edge_sums(nc, tag, hs_rows, st, codes, edges_left, ident_in, iota_f_in):
    with ExitStack() as ctx:
        def sb(name, shape, dt=F32):
            return ctx.enter_context(nc.sbuf_tensor(f"{tag}es_{name}", shape, dt))

        semaphores = Semaphores(nc, ctx)

        def sem(name):
            return semaphores.new(f"{tag}es_s_{name}")

        K = TABLES
        ident = sb("ident", [P, P])
        below = sb("below", [P, P])
        i_src = sb("i_src", [P, K], I32)
        i_dst = sb("i_dst", [P, K], I32)
        i_out = sb("i_out", [P, K], I32)
        code = sb("code", [P, K], I32)
        d = sb("d", [P, K])
        vd = sb("vd", [P, K])
        g = sb("g", [P, K, HSW])
        r = sb("r", [P, K, STW])
        nr = sb("nr", [P, K, STW])
        same = sb("same", [P, K, P])
        far = sb("far", [P, K, P])
        rk = sb("rk", [P, K, P])
        rank = sb("rank", [P, K])
        e = sb("e", [P, K, GH])
        et = sb("et", [P, K, GH])
        big = sb("big", [P, GH, P])
        gm = sb("gm", [P, K, GH])
        xm = sb("xm", [P, 2, K, GH])
        xe = sb("xe", [P, 2, K, GH])
        pay = sb("pay", [P, K, HSW])
        sc = sb("sc", [P, K, HSW])
        ps_d = ctx.enter_context(nc.psum_tensor(f"{tag}es_psd", [P, K, P], F32))
        ps_e = [ctx.enter_context(nc.psum_tensor(f"{tag}es_pse{k}", [P, GH, P], F32)) for k in range(K)]
        ps_g = ctx.enter_context(nc.psum_tensor(f"{tag}es_psg", [P, K, HSW], F32))
        s_const, s_vec, s_idx, s_dd, s_d, s_e, s_eb, s_x, s_xe, s_pay, s_gs, s_new, s_io, s_free = (
            sem(k) for k in ("const", "vec", "idx", "dd", "d", "e", "eb", "x", "xe", "pay", "gs", "new", "io", "free"))
        s_src = [sem(f"src{k}") for k in range(K)]
        s_dst = [sem(f"dst{k}") for k in range(K)]
        s_wr = [sem(f"wr{k}") for k in range(K)]
        s_turn = sem("turn")
        block = ctx.enter_context(nc.Block())

        def steps_of(eng):
            n = eng.value_load(edges_left[0:1, 0:1], min_val=1, max_val=EC // 8)
            return n * (8 // K)

        @block.sync
        def _(sp):
            sp.dma_start(ident[:, :], ident_in).then_inc(s_const, 16)
            sp.dma_start(below[:, :], iota_f_in).then_inc(s_const, 16)

        @block.gpsimd
        def _(pool):
            pool.sem_inc(s_free, 1)
            with pool.Fori(0, steps_of(pool)) as i:
                pool.wait_ge(s_idx, i + 1)
                pool.sem_inc(s_io, 1)
                for k in range(K):
                    pool.indirect_dma_start(g[:, k, :], None, hs_rows[:, :],
                                            bass.IndirectOffsetOnAxis(ap=i_src[:, k:k + 1].bitcast(U32), axis=0)).then_inc(s_src[k], 16)
                for k in range(K):
                    pool.indirect_dma_start(r[:, k, :], None, st[k],
                                            bass.IndirectOffsetOnAxis(ap=i_dst[:, k:k + 1].bitcast(U32), axis=0)).then_inc(s_dst[k], 16)
                pool.wait_ge(s_new, i + 1)
                pool.sem_inc(s_io, 1)
                for k in range(K):
                    pool.indirect_dma_start(st[k], bass.IndirectOffsetOnAxis(ap=i_out[:, k:k + 1].bitcast(U32), axis=0),
                                            nr[:, k, :], None, bounds_check=M - 1, oob_is_err=False).then_inc(s_wr[k], 16)
                for k in range(K):
                    pool.wait_ge(s_wr[k], i * 16 + 16)
                pool.sem_inc(s_free, 1)

        @block.vector
        def _(dve):
            steps = [0]

            def then(ins):
                steps[0] += 1
                ins.then_inc(s_vec, 1)
                dve.wait_ge(s_vec, steps[0])

            dve.wait_ge(s_const, 32)
            with dve.Fori(0, steps_of(dve)) as i:
                steps[0] = 0
                dve.wait_ge(s_free, i + 1)
                then(dve.tensor_copy(code[:, :], codes[:, bass.ds(i * K, K)]))
                then(dve.tensor_scalar(i_src[:, :], code[:, :], M - 1, None, ALU.bitwise_and))
                dve.tensor_scalar(i_dst[:, :], code[:, :], 13, M - 1, ALU.logical_shift_right, ALU.bitwise_and).then_inc(s_idx, 1)
                then(dve.tensor_scalar(i_out[:, :], code[:, :], 28, 1, ALU.logical_shift_right, ALU.bitwise_xor))
                then(dve.tensor_copy(vd[:, :], i_out[:, :]))
                dve.wait_ge(s_idx, i + 1)
                then(dve.tensor_copy(d[:, :], i_dst[:, :]))
                then(dve.scalar_tensor_tensor(d[:, :], vd[:, :], float(M), d[:, :], ALU.mult, ALU.add))
                dve.nop().then_inc(s_dd, 1)
                dve.wait_ge(s_d, i + 1)
                for k in range(K):
                    dve.tensor_scalar(same[:, k, :], ps_d[:, k, :], d[:, k:k + 1], None, ALU.is_equal)
                    ins = dve.tensor_scalar(far[:, k, :], ps_d[:, k, :], d[:, k:k + 1], -1e30, ALU.not_equal, ALU.mult)
                then(ins)
                then(dve.tensor_tensor(rk[:, :, :], same[:, :, :], below[:, :].unsqueeze(1).to_broadcast([P, K, P]), ALU.mult))
                then(dve.tensor_reduce(rank[:, :], rk[:, :, :], AX.X, ALU.max))
                then(dve.scalar_tensor_tensor(vd[:, :], rank[:, :], float(M), d[:, :], ALU.mult, ALU.add))
                then(dve.tensor_copy(i_out[:, :], vd[:, :]))
                for k in range(K):
                    dve.wait_ge(s_src[k], i * 16 + 16)
                    dve.wait_ge(s_dst[k], i * 16 + 16)
                then(dve.tensor_tensor(e[:, :, :], g[:, :, GF:HSW], r[:, :, 0:GH], ALU.add))
                then(dve.tensor_scalar(et[:, :, :], e[:, :, :], 0.2, None, ALU.mult))
                then(dve.tensor_tensor(e[:, :, :], e[:, :, :], et[:, :, :], ALU.max))
                dve.nop().then_inc(s_e, 1)
                for k in range(K):
                    dve.wait_ge(s_eb, i * K + (k + 1))
                    then(dve.tensor_tensor(big[:, :, :], ps_e[k][:, :, :], far[:, k:k + 1, :].to_broadcast([P, GH, P]), ALU.add))
                    then(dve.tensor_reduce(gm[:, k, :], big[:, :, :], AX.X, ALU.max))
                m_old, m_new = r[:, :, GH:2 * GH], nr[:, :, GH:2 * GH]
                then(dve.tensor_tensor(m_new, m_old, gm[:, :, :], ALU.max))
                then(dve.tensor_tensor(xm[:, 0, :, :], m_old, m_new, ALU.subtract))
                then(dve.tensor_tensor(xm[:, 1, :, :], e[:, :, :], m_new, ALU.subtract))
                then(dve.tensor_scalar(xm[:, :, :, :], xm[:, :, :, :], 0.0, None, ALU.min))
                dve.nop().then_inc(s_x, 1)
                dve.wait_ge(s_xe, i + 1)
                then(dve.tensor_copy(pay[:, :, 0:GH], xe[:, 1, :, :]))
                then(dve.tensor_copy(sc[:, :, 0:GH], xe[:, 0, :, :]))
                for k in range(K):
                    ins = dve.tensor_tensor(pay[:, k, GH:HSW].rearrange("p (h e) -> p h e", e=GE),
                                      g[:, k, 0:GF].rearrange("p (h e) -> p h e", e=GE),
                                      xe[:, 1, k, :].unsqueeze(2).to_broadcast([P, GH, GE]), ALU.mult)
                then(ins)
                dve.nop().then_inc(s_pay, 1)
                for k in range(K):
                    dve.tensor_tensor(sc[:, k, GH:HSW].rearrange("p (h e) -> p h e", e=GE),
                                      r[:, k, 3 * GH:STW].rearrange("p (h e) -> p h e", e=GE),
                                      xe[:, 0, k, :].unsqueeze(2).to_broadcast([P, GH, GE]), ALU.mult)
                dve.tensor_copy(nr[:, :, 0:GH], r[:, :, 0:GH])
                then(dve.tensor_tensor(sc[:, :, 0:GH], sc[:, :, 0:GH], r[:, :, 2 * GH:3 * GH], ALU.mult))
                dve.wait_ge(s_gs, i + 1)
                then(dve.tensor_tensor(nr[:, :, 2 * GH:STW], sc[:, :, :], ps_g[:, :, :], ALU.add))
                dve.nop().then_inc(s_new, 1)
                dve.sem_clear(s_vec)

        @block.scalar
        def _(act):
            with act.Fori(0, steps_of(act)) as i:
                act.wait_ge(s_x, i + 1)
                act.activation(xe[:, :, :, :], xm[:, :, :, :], ACT.Exp).then_inc(s_xe, 1)

        @block.tensor
        def _(pe):
            pe.wait_ge(s_const, 32)
            with pe.Fori(0, steps_of(pe)) as i:
                pe.wait_ge(s_dd, i + 1)
                for k in range(K):
                    ins = pe.matmul(ps_d[:, k, :], d[:, k:k + 1].to_broadcast([P, P]), ident[:, :], start=True, stop=True)
                ins.then_inc(s_d, 1)
                pe.wait_ge(s_e, i + 1)
                for k in range(K):
                    for h in range(GH):
                        ins = pe.matmul(ps_e[k][:, h, :], e[:, k, h:h + 1].to_broadcast([P, P]), ident[:, :], start=True, stop=True)
                    ins.then_inc(s_eb, 1)
                pe.wait_ge(s_pay, i + 1)
                for k in range(K):
                    ins = pe.matmul(ps_g[:, k, :], same[:, k, :], pay[:, k, :], start=True, stop=True)
                ins.then_inc(s_gs, 1)


def expert_gates(nc, tag, st, gates, b_gat, ln_g, ln_b):
    with ExitStack() as ctx:
        def sb(name, shape, dt=F32):
            return ctx.enter_context(nc.sbuf_tensor(f"{tag}eg_{name}", shape, dt))

        semaphores = Semaphores(nc, ctx)

        def sem(name):
            return semaphores.new(f"{tag}eg_s_{name}")

        K = TABLES
        row = sb("row", [P, K, NT, STW])
        m = sb("m", [P, NT, GH])
        x = sb("x", [P, K, NT, GH])
        w = sb("w", [P, K, NT, GH])
        acc = sb("acc", [P, NT, GF])
        t16 = sb("t16", [P, NT, GF])
        den = sb("den", [P, NT, GH])
        t4 = sb("t4", [P, NT, GH])
        vec = sb("vec", [P, 3, GF])
        mean = sb("mean", [P, NT])
        var = sb("var", [P, NT])
        rstd = sb("rstd", [P, NT])
        nhalf = sb("nhalf", [P, NT])
        s = sb("s", [P, NT, GE])
        beats = sb("beats", [P, NT, GE])
        b1 = sb("b1", [P, NT])
        b2 = sb("b2", [P, NT])
        top, second, w1, w2 = sb("top", [P, NT]), sb("second", [P, NT]), sb("w1", [P, NT]), sb("w2", [P, NT])
        is1 = sb("is1", [P, NT, GE])
        is2 = sb("is2", [P, NT, GE])
        s_in, s_vec, s_x, s_w, s_var, s_rstd, s_dif, s_ex = (sem(k) for k in ("in", "vec", "x", "w", "var", "rstd", "dif", "ex"))
        s_turn = sem("turn")
        block = ctx.enter_context(nc.Block())

        @block.sync
        def _(sp):
            for k in range(K):
                sp.dma_start(row[:, k, :, :], st[k, :, :].rearrange("(t p) c -> p t c", p=P)).then_inc(s_in, 16)
            for k, v_ in enumerate((b_gat, ln_g, ln_b)):
                sp.dma_start(vec[:, k, :], v_.to_broadcast([P, GF])).then_inc(s_in, 16)

        @block.scalar
        def _(act):
            act.wait_ge(s_x, 1)
            act.activation(w[:, :, :, :], x[:, :, :, :], ACT.Exp).then_inc(s_w, 1)
            act.wait_ge(s_dif, 1)
            act.activation(w2[:, :], w1[:, :], ACT.Exp).then_inc(s_ex, 1)

        @block.gpsimd
        def _(pool):
            pool.memset(nhalf[:, :], -0.5).then_inc(s_in, 1)
            pool.wait_ge(s_in, 16 * (K + 3) + 1)
            pool.wait_ge(s_var, 1)
            pool.tensor_tensor(rstd[:, :], var[:, :], nhalf[:, :], ALU.pow).then_inc(s_rstd, 1)

        @block.vector
        def _(dve):
            steps = [0]

            def then(ins):
                steps[0] += 1
                ins.then_inc(s_vec, 1)
                dve.wait_ge(s_vec, steps[0])

            def over(a, n):
                return a.unsqueeze(2).to_broadcast([P, NT, n])

            dve.wait_ge(s_in, 16 * (K + 3) + 1)
            then(dve.tensor_tensor(m[:, :, :], row[:, 0, :, GH:2 * GH], row[:, 1, :, GH:2 * GH], ALU.max))
            for k in range(2, K):
                then(dve.tensor_tensor(m[:, :, :], m[:, :, :], row[:, k, :, GH:2 * GH], ALU.max))
            for k in range(K):
                ins = dve.tensor_tensor(x[:, k, :, :], row[:, k, :, GH:2 * GH], m[:, :, :], ALU.subtract)
            ins.then_inc(s_x, 1)
            dve.wait_ge(s_w, 1)
            for k in range(K):
                out4, out16 = (den, acc) if k == 0 else (t4, t16)
                then(dve.tensor_tensor(out4[:, :, :], row[:, k, :, 2 * GH:3 * GH], w[:, k, :, :], ALU.mult))
                for h in range(GH):
                    then(dve.tensor_tensor(out16[:, :, GE * h:GE * h + GE], row[:, k, :, 3 * GH + GE * h:3 * GH + GE * h + GE],
                                           w[:, k, :, h:h + 1].to_broadcast([P, NT, GE]), ALU.mult))
                if k:
                    then(dve.tensor_tensor(den[:, :, :], den[:, :, :], t4[:, :, :], ALU.add))
                    then(dve.tensor_tensor(acc[:, :, :], acc[:, :, :], t16[:, :, :], ALU.add))
            then(dve.tensor_scalar(den[:, :, :], den[:, :, :], 1e-16, None, ALU.add))
            then(dve.reciprocal(t4[:, :, :], den[:, :, :]))
            for h in range(GH):
                then(dve.tensor_tensor(acc[:, :, GE * h:GE * h + GE], acc[:, :, GE * h:GE * h + GE],
                                       t4[:, :, h:h + 1].to_broadcast([P, NT, GE]), ALU.mult))
            then(dve.tensor_tensor(acc[:, :, :], acc[:, :, :], vec[:, 0:1, :].to_broadcast([P, NT, GF]), ALU.add))
            then(dve.tensor_reduce(mean[:, :], acc[:, :, :], AX.X, ALU.add))
            then(dve.tensor_scalar(mean[:, :], mean[:, :], 1.0 / GF, None, ALU.mult))
            then(dve.tensor_tensor(acc[:, :, :], acc[:, :, :], over(mean[:, :], GF), ALU.subtract))
            then(dve.tensor_tensor(t16[:, :, :], acc[:, :, :], acc[:, :, :], ALU.mult))
            then(dve.tensor_reduce(var[:, :], t16[:, :, :], AX.X, ALU.add))
            then(dve.tensor_scalar(var[:, :], var[:, :], 1.0 / GF, 1e-5, ALU.mult, ALU.add))
            dve.nop().then_inc(s_var, 1)
            dve.wait_ge(s_rstd, 1)
            then(dve.tensor_tensor(acc[:, :, :], acc[:, :, :], over(rstd[:, :], GF), ALU.mult))
            then(dve.tensor_tensor(acc[:, :, :], acc[:, :, :], vec[:, 1:2, :].to_broadcast([P, NT, GF]), ALU.mult))
            then(dve.tensor_tensor(acc[:, :, :], acc[:, :, :], vec[:, 2:3, :].to_broadcast([P, NT, GF]), ALU.add))
            then(dve.tensor_reduce(s[:, :, :], acc[:, :, :].rearrange("p t (h e) -> p t e h", e=GE), AX.X, ALU.add))
            then(dve.tensor_scalar(s[:, :, :], s[:, :, :], 1.0 / GH, None, ALU.mult))
            for e in range(GE):
                for f in range(GE):
                    if f == e:
                        continue
                    op = ALU.is_ge if f < e else ALU.is_gt
                    first = f == (1 if e == 0 else 0)
                    then(dve.tensor_tensor(b1[:, :], s[:, :, f], s[:, :, e], op))
                    if first:
                        then(dve.tensor_copy(beats[:, :, e], b1[:, :]))
                    else:
                        then(dve.tensor_tensor(beats[:, :, e], beats[:, :, e], b1[:, :], ALU.add))
            then(dve.tensor_scalar(is1[:, :, :], beats[:, :, :], 0.0, None, ALU.is_equal))
            then(dve.tensor_scalar(is2[:, :, :], beats[:, :, :], 1.0, None, ALU.is_equal))
            then(dve.tensor_tensor(t4[:, :, :], is1[:, :, :], s[:, :, :], ALU.mult))
            then(dve.tensor_reduce(top[:, :], t4[:, :, :], AX.X, ALU.add))
            then(dve.tensor_tensor(t4[:, :, :], is2[:, :, :], s[:, :, :], ALU.mult))
            then(dve.tensor_reduce(second[:, :], t4[:, :, :], AX.X, ALU.add))
            then(dve.tensor_tensor(w1[:, :], second[:, :], top[:, :], ALU.subtract))
            dve.nop().then_inc(s_dif, 1)
            dve.wait_ge(s_ex, 1)
            then(dve.tensor_scalar(b1[:, :], w2[:, :], 1.0, None, ALU.add))
            then(dve.reciprocal(w1[:, :], b1[:, :]))
            then(dve.tensor_tensor(b2[:, :], w2[:, :], w1[:, :], ALU.mult))
            then(dve.tensor_tensor(is1[:, :, :], is1[:, :, :], over(w1[:, :], GE), ALU.mult))
            then(dve.tensor_tensor(is2[:, :, :], is2[:, :, :], over(b2[:, :], GE), ALU.mult))
            then(dve.tensor_tensor(gates[:, :, :], is1[:, :, :], is2[:, :, :], ALU.add))
MT = 512
MTT = MT // P
HID = 512
MB = HID // P


def experts(nc, tag, x_in, x_out, tT, gates, w1_in, b1_in, w2_in, b2_in):
    with ExitStack() as ctx:
        def sb(name, shape, dt=F32):
            return ctx.enter_context(nc.sbuf_tensor(f"{tag}ex_{name}", shape, dt))

        semaphores = Semaphores(nc, ctx)

        def sem(name):
            return semaphores.new(f"{tag}ex_s_{name}")

        w1 = sb("w1", [P, GE, KK, HID])
        w2 = sb("w2", [P, GE, MB, C])
        b1 = sb("b1", [P, GE, MB])
        b2 = sb("b2", [P, GE, C])
        tt = sb("tt", [P, 2, KK, MT])
        xt = sb("xt", [P, 2, MTT, C])
        g4 = sb("g4", [P, 2, MTT, GE])
        hid = sb("hid", [P, 2, MB, MT])
        ps1 = [ctx.enter_context(nc.psum_tensor(f"{tag}ex_p{i}", [P, MT], F32)) for i in range(4)]
        ps2 = [ctx.enter_context(nc.psum_tensor(f"{tag}ex_q{i}", [P, 2, C], F32)) for i in range(4)]
        s_const = sem("const")
        s_t = [sem("t0"), sem("t1")]
        s_out = [sem("out0"), sem("out1")]
        s_up, s_act, s_down, s_add, s_vec, s_free = (sem(k) for k in ("up", "act", "down", "add", "vec", "free"))
        NS = M // MT
        UP, DN = GE * MB, GE * 2
        s_turn = sem("turn")
        block = ctx.enter_context(nc.Block())

        @block.sync
        def _(sp):
            sp.dma_start(w1[:, :, :, :], w1_in).then_inc(s_const, 16)
            sp.dma_start(w2[:, :, :, :], w2_in).then_inc(s_const, 16)
            sp.dma_start(b1[:, :, :], b1_in).then_inc(s_const, 16)
            for e in range(GE):
                sp.dma_start(b2[:, e, :], b2_in[e:e + 1, :].to_broadcast([P, C])).then_inc(s_const, 16)
            with sp.Fori(0, NS // 2) as i:
                for s in range(2):
                    sp.wait_ge(s_free, i * 2 + (s + 1))
                    sp.sem_inc(s_turn, 1)
                    sp.dma_start(xt[:, s, :, :], x_in[bass.ds(i * (2 * MT) + s * MT, MT), :]
                                 .rearrange("(t p) c -> p t c", p=P)).then_inc(s_t[s], 16)
                    sp.dma_start(tt[:, s, :, :].rearrange("p k l -> p (k l)").rearrange("p (k l) -> p k l", k=KK),
                                 tT[bass.ds(i, 1), :, :, MT * s:MT * s + MT].rearrange("a p k l -> p (a k) l")).then_inc(s_t[s], 16)

        @block.tensor
        def _(pe):
            pe.wait_ge(s_const, 16 * (3 + GE))
            with pe.Fori(0, NS // 2) as i:
                def up(n):
                    s, e = n // GE, n % GE
                    if e == 0:
                        pe.wait_ge(s_t[s], i * 32 + 32)
                    for m in range(MB):
                        pe.wait_ge(s_act, i * (2 * UP) + (n * MB + m + 1))
                        for k in range(KK):
                            ins = pe.matmul(ps1[m][:, :], w1[:, e, k, P * m:P * m + P], tt[:, s, k, :],
                                            start=(k == 0), stop=(k == KK - 1))
                        ins.then_inc(s_up, 1)

                def down(n):
                    e = n % GE
                    pe.wait_ge(s_act, i * (2 * UP) + (n * MB + 2 * MB))
                    for q in range(2):
                        pe.wait_ge(s_add, i * (2 * DN) + (2 * n + q + 1))
                        bank = (2 * n + q) % 4
                        for r in range(2):
                            t = 2 * q + r
                            for m in range(MB):
                                ins = pe.matmul(ps2[bank][:, r, :], hid[:, n % 2, m, P * t:P * t + P], w2[:, e, m, :],
                                                start=(m == 0), stop=(m == MB - 1))
                        ins.then_inc(s_down, 1)

                for n in range(2 * GE):
                    up(n)
                    if n:
                        down(n - 1)
                down(2 * GE - 1)

        @block.scalar
        def _(act):
            act.wait_ge(s_const, 16 * (3 + GE))
            act.sem_inc(s_act, MB)
            with act.Fori(0, NS // 2) as i:
                for n in range(2 * GE):
                    act.wait_ge(s_down, i * (2 * DN) + (2 * n + 1))
                    for m in range(MB):
                        act.wait_ge(s_up, i * (2 * UP) + (n * MB + m + 1))
                        act.activation(hid[:, n % 2, m, :], ps1[m][:, :], ACT.Gelu,
                                       bias=b1[:, n % GE, m:m + 1]).then_inc(s_act, 1)

        @block.gpsimd
        def _(pool):
            pool.sem_inc(s_down, 3)
            with pool.Fori(0, NS // 2) as i:
                for s in range(2):
                    pool.wait_ge(s_add, i * (2 * DN) + (4 + s * DN + DN))
                    pool.dma_start(x_out[bass.ds(i * (2 * MT) + s * MT, MT), :].rearrange("(t p) c -> p t c", p=P),
                                   xt[:, s, :, :]).then_inc(s_out[s], 16)
                for s in range(2):
                    pool.wait_ge(s_out[s], i * 16 + 16)
                    pool.sem_inc(s_free, 1)
            for s in range(2):
                pool.wait_ge(s_out[s], 16 * (NS // 2))

        @block.vector
        def _(dve):
            dve.wait_ge(s_const, 16 * (3 + GE))
            dve.sem_inc(s_add, 4)
            dve.sem_inc(s_free, 2)
            with dve.Fori(0, NS // 2) as i:
                done = 0
                for s in range(2):
                    dve.wait_ge(s_t[s], i * 32 + 32)
                    dve.tensor_copy(g4[:, s, :, :], gates[:, bass.ds(i * (2 * MTT) + s * MTT, MTT), :]).then_inc(s_vec, 1)
                    done += 1
                    dve.wait_ge(s_vec, done)
                    for e in range(GE):
                        for t in range(MTT):
                            ins = dve.scalar_tensor_tensor(xt[:, s, t, :], b2[:, e, :], g4[:, s, t, e:e + 1],
                                                           xt[:, s, t, :], ALU.mult, ALU.add)
                        ins.then_inc(s_vec, 1)
                        done += 1
                        dve.wait_ge(s_vec, done)
                    for e in range(GE):
                        n = s * GE + e
                        for q in range(2):
                            dve.wait_ge(s_down, i * (2 * DN) + (3 + 2 * n + q + 1))
                            if e > 0:
                                dve.wait_ge(s_add, i * (2 * DN) + (4 + 2 * n + q - 1))
                            for r in range(2):
                                t = 2 * q + r
                                ins = dve.scalar_tensor_tensor(xt[:, s, t, :], ps2[(2 * n + q) % 4][:, r, :],
                                                               g4[:, s, t, e:e + 1], xt[:, s, t, :], ALU.mult, ALU.add)
                            ins.then_inc(s_add, 1)
                dve.sem_clear(s_vec)


ROUND = 12582912.0
QMAX = 127.0
TAPS = 9
PADR = N1 + 2


def conv_layer(nc, x_in, x_out, rhs_in, ident_in):
    with ExitStack() as ctx:
        def sb(name, shape, dt=F32):
            return ctx.enter_context(nc.sbuf_tensor(f"cv_{name}", shape, dt))

        semaphores = Semaphores(nc, ctx)

        def sem(name):
            return semaphores.new(f"cv_s_{name}")

        ident = sb("ident", [P, P])
        identb = sb("identb", [P, P], BF16)
        w = sb("w", [P, KK, TAPS, C])
        qw = sb("qw", [P, KK, TAPS, C], BF16)
        wmax = sb("wmax", [P, C])
        wall = sb("wall", [P, C])
        s_rhs = sb("s_rhs", [P, C])
        r_rhs = sb("r_rhs", [P, C])
        xt = sb("xt", [P, 2, TPB, C])
        xn = sb("xn", [P, TPB, C])
        q = sb("q", [P, 2, TPB, C], BF16)
        pad = sb("pad", [P, 2, KK, 3, PADR, N2], BF16)
        y = sb("y", [P, 2, C])
        stats = sb("stats", [P, TPB, 6])
        mv = sb("mv", [P, TPB, 2])
        ve = sb("ve", [P, TPB])
        nhalf = sb("nhalf", [P, TPB])
        rstd = sb("rstd", [P, TPB])
        amax = sb("amax", [P, 1])
        aall = sb("aall", [P, 1])
        s_lhs = sb("s_lhs", [P, 2])
        r_lhs = sb("r_lhs", [P, 2])
        ps_t = [ctx.enter_context(nc.psum_tensor(f"cv_pt{i}", [P, KK, P], BF16)) for i in range(2)]
        ps_o = [ctx.enter_context(nc.psum_tensor(f"cv_po{i}", [P, C], F32)) for i in range(4)]
        s_const, s_mem, s_wm, s_wa, s_w, s_vec = (sem(k) for k in ("const", "mem", "wm", "wa", "w", "vec"))
        s_x = [sem("x0"), sem("x1")]
        s_out = [sem("out0"), sem("out1")]
        s_ve, s_rstd, s_am, s_aa, s_q, s_tr, s_pad, s_o, s_y, s_free = (
            sem(k) for k in ("ve", "rstd", "am", "aa", "q", "tr", "pad", "o", "y", "free"))
        NB = B // 2
        s_turn = sem("turn")
        block = ctx.enter_context(nc.Block())

        @block.sync
        def _(sp):
            sp.dma_start(ident[:, :], ident_in).then_inc(s_const, 16)
            sp.dma_start(w[:, :, :, :], rhs_in).then_inc(s_const, 16)
            with sp.Fori(0, NB) as i:
                for s in range(2):
                    sp.wait_ge(s_free, i * 2 + (s + 1))
                    sp.sem_inc(s_turn, 1)
                    sp.dma_start(xt[:, s, :, :], x_in[bass.ds(i * (2 * L) + s * L, L), :]
                                 .rearrange("(t p) c -> p t c", p=P)).then_inc(s_x[s], 16)

        @block.gpsimd
        def _(pool):
            pool.memset(nhalf[:, :], -0.5)
            pool.memset(pad[:, :, :, :, :, :], 0.0).then_inc(s_mem, 1)
            pool.wait_ge(s_mem, 1)
            pool.wait_ge(s_wm, 1)
            pool.partition_all_reduce(wall[:, :], wmax[:, :], P, bass.bass_isa.ReduceOp.max).then_inc(s_wa, 1)
            pool.sem_inc(s_free, 2)
            with pool.Fori(0, NB) as i:
                for s in range(2):
                    pool.wait_ge(s_ve, i * 2 + (s + 1))
                    pool.tensor_tensor(rstd[:, :], ve[:, :], nhalf[:, :], ALU.pow).then_inc(s_rstd, 1)
                    pool.wait_ge(s_am, i * 2 + (s + 1))
                    pool.sem_inc(s_mem, 1)
                    pool.partition_all_reduce(aall[:, :], amax[:, :], P, bass.bass_isa.ReduceOp.max).then_inc(s_aa, 1)

        @block.scalar
        def _(act):
            act.wait_ge(s_mem, 1)
            with act.Fori(0, NB) as i:
                for s in range(2):
                    for t in range(TPB):
                        act.wait_ge(s_tr, i * (2 * TPB) + (s * TPB + t + 1))
                        if t == 0:
                            act.wait_ge(s_o, i * (2 * TPB) + (s * TPB + TPB))
                        tile = ps_t[t % 2][:, :, :].rearrange("p k (r c) -> p k r c", c=N2)
                        rows = slice(1 + 4 * t, 5 + 4 * t)
                        for dx in range(3):
                            to, of = max(0, 1 - dx), max(0, dx - 1)
                            n = N2 - abs(dx - 1)
                            ins = act.activation(pad[:, s, :, dx, rows, to:to + n], tile[:, :, :, of:of + n], ACT.Copy)
                        ins.then_inc(s_pad, 1)
                for s in range(2):
                    act.wait_ge(s_y, i * (2 * TPB) + (4 + s * TPB + TPB))
                    act.dma_start(x_out[bass.ds(i * (2 * L) + s * L, L), :].rearrange("(t p) c -> p t c", p=P),
                                  xt[:, s, :, :]).then_inc(s_out[s], 16)
                for s in range(2):
                    act.wait_ge(s_out[s], i * 16 + 16)
                    act.sem_inc(s_free, 1)
            for s in range(2):
                act.wait_ge(s_out[s], 16 * NB)

        @block.vector
        def _(dve):
            steps = [0]

            def then(ins):
                steps[0] += 1
                ins.then_inc(s_vec, 1)
                dve.wait_ge(s_vec, steps[0])

            dve.wait_ge(s_const, 32)
            dve.wait_ge(s_mem, 1)
            dve.tensor_reduce(wmax[:, :], w[:, :, :, :].rearrange("p k t c -> p c (k t)"), AX.X, ALU.max,
                              apply_absolute_value=True).then_inc(s_wm, 1)
            dve.tensor_copy(identb[:, :], ident[:, :])
            dve.wait_ge(s_wa, 1)
            then(dve.tensor_scalar(s_rhs[:, :], wall[:, :], 1e-6, 1.0 / QMAX, ALU.max, ALU.mult))
            then(dve.reciprocal(r_rhs[:, :], s_rhs[:, :]))
            for k in range(KK):
                wk = w[:, k, :, :]
                then(dve.tensor_tensor(wk, wk, r_rhs[:, :].unsqueeze(1).to_broadcast([P, TAPS, C]), ALU.mult))
                then(dve.tensor_scalar(wk, wk, QMAX, -QMAX, ALU.min, ALU.max))
                then(dve.tensor_scalar(wk, wk, ROUND, None, ALU.add))
                then(dve.tensor_scalar(qw[:, k, :, :], wk, ROUND, None, ALU.subtract))
            dve.nop().then_inc(s_w, 1)
            dve.sem_clear(s_vec)
            dve.sem_inc(s_o, 2 * TPB)
            with dve.Fori(0, NB) as i:
                steps[0] = 0

                def prepare(s):
                    dve.wait_ge(s_x[s], i * 16 + 16)
                    for t in range(TPB):
                        ins = dve.bn_stats(stats[:, t, :], xt[:, s, t, :])
                    then(ins)
                    for t in range(TPB):
                        ins = dve.bn_aggr(mv[:, t, :], stats[:, t, :])
                    then(ins)
                    dve.tensor_scalar(ve[:, :], mv[:, :, 1], 1e-6, None, ALU.add).then_inc(s_ve, 1)
                    dve.wait_ge(s_rstd, i * 2 + (s + 1))
                    for t in range(TPB):
                        ins = dve.tensor_scalar(xn[:, t, :], xt[:, s, t, :], mv[:, t, 0:1], rstd[:, t:t + 1],
                                                ALU.subtract, ALU.mult)
                    then(ins)
                    dve.tensor_reduce(amax[:, :], xn[:, :, :], AX.XY, ALU.max, apply_absolute_value=True).then_inc(s_am, 1)
                    dve.wait_ge(s_aa, i * 2 + (s + 1))
                    then(dve.tensor_scalar(s_lhs[:, s:s + 1], aall[:, :], 1e-6, 1.0 / QMAX, ALU.max, ALU.mult))
                    then(dve.reciprocal(r_lhs[:, s:s + 1], s_lhs[:, s:s + 1]))
                    then(dve.tensor_scalar(xn[:, :, :], xn[:, :, :], r_lhs[:, s:s + 1], QMAX, ALU.mult, ALU.min))
                    then(dve.tensor_scalar(xn[:, :, :], xn[:, :, :], -QMAX, ROUND, ALU.max, ALU.add))
                    then(dve.tensor_scalar(q[:, s, :, :], xn[:, :, :], ROUND, None, ALU.subtract))
                    dve.nop().then_inc(s_q, 1)

                def finish(s):
                    for t in range(TPB):
                        n = s * TPB + t
                        dve.wait_ge(s_o, i * (2 * TPB) + (2 * TPB + n + 1))
                        then(dve.scalar_tensor_tensor(y[:, t % 2, :], ps_o[t % 4][:, :], s_lhs[:, s:s + 1],
                                                      s_rhs[:, :], ALU.mult, ALU.mult))
                        dve.tensor_tensor(xt[:, s, t, :], y[:, t % 2, :], xt[:, s, t, :], ALU.add).then_inc(s_y, 1)

                prepare(0)
                prepare(1)
                finish(0)
                finish(1)
                dve.sem_clear(s_vec)

        @block.tensor
        def _(pe):
            pe.wait_ge(s_w, 1)
            pe.sem_inc(s_pad, 2)
            pe.sem_inc(s_y, 4)
            with pe.Fori(0, NB) as i:
                for s in range(2):
                    pe.wait_ge(s_q, i * 2 + (s + 1))
                    for t in range(TPB):
                        n = s * TPB + t
                        pe.wait_ge(s_pad, i * (2 * TPB) + (n + 1))
                        for k in range(KK):
                            ins = pe.transpose(ps_t[t % 2][:, k, :], q[:, s, t, P * k:P * k + P], identb[:, :])
                        ins.then_inc(s_tr, 1)
                for s in range(2):
                    pe.wait_ge(s_pad, i * (2 * TPB) + (2 + s * TPB + TPB))
                    for t in range(TPB):
                        n = s * TPB + t
                        pe.wait_ge(s_y, i * (2 * TPB) + (n + 1))
                        for a in range(KK * TAPS):
                            k, tap = a // TAPS, a % TAPS
                            dy, dx = tap // 3, tap % 3
                            ins = pe.matmul(ps_o[t % 4][:, :], pad[:, s, k, dx, 4 * t + dy:4 * t + dy + 4, :].rearrange("p r c -> p (r c)"),
                                            qw[:, k, tap, :], start=(a == 0), stop=(a == KK * TAPS - 1))
                        ins.then_inc(s_o, 1)

def build(nc, a, out):
    def dram(name, shape):
        return nc.dram_tensor(name, shape, F32).ap()

    x1, x2, x3 = (dram(n, (M, C)) for n in ("x1", "x2", "x3"))
    tT = dram("tT", (NGT, P, KK, GTOK))
    hs_rows = dram("hs_rows", (M, HSW))
    st = StateTables([dram(f"target_rows{k}", (M, STW)) for k in range(TABLES)])

    def gated_experts(layer, x_in, x_out):
        w = {n: a[f"L{layer}_{n}"] for n in ("w_gat", "att_src", "att_dst", "b_gat", "ln_gamma", "ln_beta",
                                            "w1", "b1", "w2", "b2", "edges")}
        tag = f"l{layer}"
        with ExitStack() as ctx:
            def sb(name, shape, dt=F32):
                return ctx.enter_context(nc.sbuf_tensor(f"{tag}_{name}", shape, dt))

            codes = sb("codes", [P, EC], I32)
            count = sb("count", [P, NT])
            left = sb("left", [P, 1], I32)
            ad = sb("ad", [P, NT, GH])
            gates = sb("gates", [P, NT, GE])
            edge_lists(nc, tag, w["edges"], a["iota"], codes, count, left)
            normalised_nodes(nc, tag, x_in, tT, hs_rows, ad, w["w_gat"], w["att_src"], w["att_dst"], a["ident"])
            target_rows(nc, tag, hs_rows, ad, count, st)
            edge_sums(nc, tag, hs_rows, st, codes, left, a["ident"], a["below"])
            expert_gates(nc, tag, st, gates, w["b_gat"], w["ln_gamma"], w["ln_beta"])
            experts(nc, tag, x_in, x_out, tT, gates, w["w1"], w["b1"], w["w2"], w["b2"])

    attention_layer(nc, a["x"], x1, a["w_att"], a["cos"], a["sin"], a["qscale"], a["decay"], a["ln_g"], a["ln_b"],
                    a["ident"], a["blk"])
    gated_experts(0, x1, x2)
    conv_layer(nc, x2, x3, a["rhs"], a["ident"])
    gated_experts(1, x3, out)


class StateTables:

    def __init__(self, tables):
        self.tables = tables

    def __getitem__(self, at):
        if isinstance(at, tuple):
            return self.tables[at[0]][at[1:]]
        return self.tables[at]


def kernel(**inputs):
    import concourse.bacc as bacc
    from concourse.bass_utils import run_bass_kernel_spmd

    def rows_first(w, *lead):
        k = w.shape[-2] // P
        v = w.reshape(*w.shape[:-2], k, P, w.shape[-1])
        return np.ascontiguousarray(np.moveaxis(v, -2, 0))

    inputs = {k: np.asarray(v) for k, v in inputs.items()}
    cos, sin, qscale, decay, blk, eye = attention_constants()
    swapped = np.arange(C) ^ 1
    wq, wk, wv, wo = (inputs[f"L0_conv_W{k}"] for k in "qkvo")
    arrays = {
        "x": np.ascontiguousarray(inputs["x"].reshape(M, C)),
        "w_att": np.ascontiguousarray(np.stack([rows_first(w.T) for w in (wq, wq[swapped], wk, wk[swapped], wv, wo)], axis=1)),
        "cos": cos, "sin": sin, "qscale": qscale, "decay": decay, "blk": blk, "ident": eye,
        "ln_g": inputs["L0_conv_ln_g"].reshape(KD, 1),
        "ln_b": inputs["L0_conv_ln_b"].reshape(KD, 1),
        "below": np.tril(np.ones((P, P), np.float32), -1),
        "iota": np.tile(np.arange(P), (P, 1)).astype(mybir.dt.np(BF16)),
        "rhs": np.ascontiguousarray(inputs["L1_conv_rhs"].reshape(TAPS, KK, P, C).transpose(2, 1, 0, 3)),
    }
    for layer in range(2):
        f, t = f"L{layer}_ffn_", f"L{layer}_"
        arrays[t + "w_gat"] = rows_first(inputs[f + "W_gat"])
        arrays[t + "w1"] = rows_first(inputs[f + "W1"])
        arrays[t + "w2"] = rows_first(inputs[f + "W2"])
        arrays[t + "b1"] = np.ascontiguousarray(inputs[f + "b1"].reshape(GE, MB, P).transpose(2, 0, 1))
        arrays[t + "b2"] = inputs[f + "b2"]
        arrays[t + "edges"] = inputs[f + "edge_index"]
        for name in ("att_src", "att_dst", "b_gat", "ln_gamma", "ln_beta"):
            arrays[t + name] = inputs[f + name].reshape(1, GF)
    nc = bacc.Bacc("TRN2", target_bir_lowering=False, num_devices=1)
    aps = {n: nc.dram_tensor("in_" + n, v.shape, mybir.dt.from_np(v.dtype), kind="ExternalInput").ap() for n, v in arrays.items()}
    out = nc.dram_tensor("out", (M, C), F32, kind="ExternalOutput").ap()
    build(nc, aps, out)
    r = run_bass_kernel_spmd(nc, [{"in_" + n: v for n, v in arrays.items()}], core_ids=[0])
    return r.results[0]["out"].reshape(B, N1, N2, C)
```

```python
import numpy as np
import concourse.bass as bass
from concourse import mybir
from concourse.alu_op_type import AluOpType as ALU
from contextlib import ExitStack

F32 = mybir.dt.float32
BF16 = mybir.dt.bfloat16
I32 = mybir.dt.int32
U32 = mybir.dt.uint32
ACT = mybir.ActivationFunctionType
AX = mybir.AxisListType

B, N1, N2, C = 8, 32, 32, 256
L = N1 * N2
M = B * L
P = 128
TPB = L // P
NT = M // P
KK = C // P
H, KD = 8, C // 8
HPQ = P // KD
HALF = 512
MROW = (2 * N1 - 4) * N2


class Semaphores:

    def __init__(self, nc, ctx):
        self.nc, self.own = nc, []
        ctx.callback(self.clear)

    def new(self, name):
        self.own.append(self.nc.alloc_semaphore(name))
        return self.own[-1]

    def clear(self):
        self.nc.clear_and_free_semaphores(self.own)
        self.nc.all_engine_barrier()


def attention_layer(nc, x_in, x_out, w, cos_t, sin_t, qscale_t, decay_t, ln_g, ln_b, ident_in, blk_in):
    with ExitStack() as ctx:
        def sb(name, shape, dt=F32):
            return ctx.enter_context(nc.sbuf_tensor("at_" + name, shape, dt))

        semaphores = Semaphores(nc, ctx)

        def sem(name):
            return semaphores.new("at_" + name)

        decay = sb("decay", [P, H, MROW])
        cos = sb("cos", [P, L])
        sin = sb("sin", [P, L])
        qscale = sb("qscale", [P, KK, L])
        wt = sb("wt", [P, 6, KK, C])
        ident = sb("ident", [P, P])
        blk = sb("blk", [P, P])
        ones = sb("ones", [P, KD])
        gb = sb("gb", [P, 2])
        nhalf = sb("nhalf", [P, TPB])
        xt = sb("xt", [P, TPB, C])
        xn = sb("xn", [P, TPB, C])
        g_t = xn[:, :, :].rearrange("p t c -> p (t c)").rearrange("p (k l) -> p k l", k=KK)
        xnT = sb("xnT", [P, KK, L])
        qr = sb("qr", [P, KK, L])
        kz = sb("kz", [P, H, L])
        v = sb("v", [P, TPB, C])
        kr = sb("kr", [P, 2, HALF])
        t1 = sb("t1", [P, HALF])
        t2 = sb("t2", [P, HALF])
        stats = sb("stats", [P, TPB, 6])
        mv = sb("mv", [P, TPB, 2])
        ve = sb("ve", [P, TPB])
        rstd = sb("rstd", [P, TPB])
        pr = sb("pr", [P, 3, 2, HALF])
        ab = sb("ab", [P, 3, 2, HALF])
        dn = sb("dn", [P, HALF])
        o = sb("o", [P, HALF])
        oc = sb("oc", [P, HALF])
        sq = sb("sq", [P, HALF])
        vq = sb("vq", [P, HALF])
        sd = sb("sd", [P, HALF])
        rsd = sb("rsd", [P, HALF])
        ps_s = [ctx.enter_context(nc.psum_tensor(f"at_ps_s{i}", [P, 2, HALF], F32)) for i in range(2)]
        ps_av = ctx.enter_context(nc.psum_tensor("at_ps_av", [P, HALF], F32))
        ps_dn = ctx.enter_context(nc.psum_tensor("at_ps_dn", [P, HALF], F32))
        ps_m = [ctx.enter_context(nc.psum_tensor(f"at_ps_m{i}", [P, HALF], F32)) for i in range(2)]

        s_const, s_cst, s_x, s_out = sem("const"), sem("cst"), sem("x"), sem("out")
        s_mv, s_ve, s_vec = sem("mv"), sem("ve"), sem("vec")
        s_rstd, s_pool = sem("rstd"), sem("pool")
        s_xn, s_tr, s_xnT = sem("xn"), sem("tr"), sem("xnT")
        s_proj, s_rot, s_kr, s_kz = sem("proj"), sem("rot"), sem("kr"), sem("kz")
        s_vps, s_v = sem("vps"), sem("v")
        s_sc, s_p, s_a, s_av = sem("sc"), sem("p"), sem("a"), sem("av")
        s_o, s_mu, s_oc, s_sq, s_var, s_sd, s_y, s_g = (sem(k) for k in ("o", "mu", "oc", "sq", "var", "sd", "y", "g"))
        s_op, s_x1, s_vq = sem("op"), sem("x1"), sem("vq")

        NU = 64
        NG = NU // 16

        def unit(u):
            return u // 32, (u // 16) % 2, (u // 2) % 8, u % 2

        s_turn = sem("turn")
        block = ctx.enter_context(nc.Block())

        @block.sync
        def _(sp):
            sp.dma_start(ident[:, :], ident_in).then_inc(s_const, 16)
            sp.dma_start(blk[:, :], blk_in).then_inc(s_const, 16)
            sp.dma_start(wt[:, :, :, :], w).then_inc(s_const, 16)
            sp.dma_start(cos[:, :], cos_t).then_inc(s_const, 16)
            sp.dma_start(sin[:, :], sin_t).then_inc(s_const, 16)
            sp.dma_start(qscale[:, :, :], qscale_t).then_inc(s_const, 16)
            sp.dma_start(decay[:, :, :], decay_t).then_inc(s_const, 16)
            for j in range(HPQ):
                if j == 0:
                    sp.dma_start(gb[0:KD, 0:1], ln_g).then_inc(s_const, 16)
                else:
                    sp.dma_start(gb[KD * j:KD * j + KD, 0:1], ln_g).then_inc(s_const, 16)
                sp.dma_start(gb[KD * j:KD * j + KD, 1:2], ln_b).then_inc(s_const, 16)
            with sp.Fori(0, B) as b:
                sp.dma_start(xt[:, :, :], x_in[bass.ds(b * L, L), :].rearrange("(t p) c -> p t c", p=P)).then_inc(s_x, 16)
                sp.wait_ge(s_x1, b * TPB + TPB)
                sp.sem_inc(s_turn, 1)
                sp.dma_start(x_out[bass.ds(b * L, L), :].rearrange("(t p) c -> p t c", p=P), xt[:, :, :]).then_inc(s_out, 16)
                sp.wait_ge(s_out, b * 16 + 16)
                sp.sem_inc(s_turn, 1)
            sp.wait_ge(s_out, B * 16)

        @block.gpsimd
        def _(pool):
            pool.memset(kz[:, :, :], 0.0).then_inc(s_cst, 1)
            pool.memset(ones[:, :], 1.0).then_inc(s_cst, 1)
            pool.memset(nhalf[:, :], -0.5).then_inc(s_cst, 1)
            pool.wait_ge(s_cst, 3)
            with pool.Fori(0, B) as b:
                pool.wait_ge(s_ve, b + 1)
                pool.tensor_tensor(rstd[:, :], ve[:, :], nhalf[:, :], ALU.pow).then_inc(s_rstd, 1)
                for g in range(4):
                    pool.wait_ge(s_kr, b * 4 + (g + 1))
                    pool.sem_inc(s_pool, 1)
                    hq, n = g // 2, g % 2
                    for j in range(HPQ):
                        last = pool.tensor_copy(kz[KD * j:KD * j + KD, HPQ * hq + j, HALF * n:HALF * n + HALF],
                                                kr[KD * j:KD * j + KD, g % 2, :])
                    last.then_inc(s_kz, 1)
                for g in range(NG):
                    pool.wait_ge(s_oc, b * NG + (g + 1))
                    pool.tensor_tensor(sq[:, :], oc[:, :], oc[:, :], ALU.mult).then_inc(s_sq, 1)

        @block.scalar
        def _(act):
            act.wait_ge(s_const, 16 * (7 + 2 * HPQ))
            act.wait_ge(s_cst, 3)
            with act.Fori(0, B) as b:
                for t in range(TPB // 2):
                    act.wait_ge(s_tr, b * 4 + (t + 1))
                    act.activation(xnT[:, :, 2 * P * t:2 * P * t + 2 * P],
                                   ps_m[t % 2][:, :].rearrange("p (k c) -> p k c", k=KK), ACT.Copy).then_inc(s_xnT, 1)
                for t in range(TPB // 2):
                    act.wait_ge(s_vps, b * 4 + (t + 1))
                    act.activation(v[:, 2 * t:2 * t + 2, :], ps_m[t % 2][:, :].rearrange("p (k c) -> p k c", k=2),
                                   ACT.Copy).then_inc(s_v, 1)

                def head_sd(g):
                    act.wait_ge(s_vq, b * NG + (g + 1))
                    act.activation(sd[:, :], vq[:, :], ACT.Sqrt).then_inc(s_sd, 1)

                for u in range(NU):
                    act.wait_ge(s_p, b * NU + (u + 1))
                    if u >= 3:
                        act.wait_ge(s_av, b * NU + (u - 2))
                    act.activation(ab[:, u % 3, :, :], pr[:, u % 3, :, :], ACT.Abs).then_inc(s_a, 1)
                    if u >= 25 and (u - 25) % 16 == 0:
                        head_sd((u - 25) // 16)
                head_sd(NG - 1)
                for g in range(NG):
                    act.wait_ge(s_y, b * NG + (g + 1))
                    dst = g_t[:, g // 2, HALF * (g % 2):HALF * (g % 2) + HALF]
                    act.activation(dst, dst, ACT.Gelu, bias=gb[:, 1:2], scale=gb[:, 0:1]).then_inc(s_g, 1)

        @block.vector
        def _(dve):
            steps = [0]

            def then(ins):
                steps[0] += 1
                ins.then_inc(s_vec, 1)
                dve.wait_ge(s_vec, steps[0])

            dve.wait_ge(s_const, 16 * (7 + 2 * HPQ))
            dve.wait_ge(s_cst, 3)
            with dve.Fori(0, B) as b:
                dve.wait_ge(s_x, b * 16 + 16)
                for t in range(TPB):
                    ins = dve.bn_stats(stats[:, t, :], xt[:, t, :])
                then(ins)
                for t in range(TPB):
                    ins = dve.bn_aggr(mv[:, t, :], stats[:, t, :])
                then(ins)
                dve.tensor_scalar(ve[:, :], mv[:, :, 1], 1e-6, None, ALU.add).then_inc(s_ve, 1)
                dve.wait_ge(s_rstd, b + 1)
                for t in range(TPB):
                    dve.tensor_scalar(xn[:, t, :], xt[:, t, :], mv[:, t, 0:1], rstd[:, t:t + 1],
                                      ALU.subtract, ALU.mult).then_inc(s_xn, 1)
                for g in range(8):
                    hq, n = (g // 2) % 2, g % 2
                    cols = slice(HALF * n, HALF * n + HALF)
                    dve.wait_ge(s_proj, b * 8 + (g + 1))
                    if g > 0:
                        if g <= 4:
                            dve.wait_ge(s_rot, b * 4 + g)
                        else:
                            dve.wait_ge(s_kr, b * 4 + (g - 4))
                    dve.tensor_tensor(t1[:, :], ps_s[g % 2][:, 0, :], cos[:, cols], ALU.mult)
                    then(dve.tensor_tensor(t2[:, :], ps_s[g % 2][:, 1, :], sin[:, cols], ALU.mult))
                    if g < 4:
                        then(dve.tensor_tensor(t1[:, :], t1[:, :], t2[:, :], ALU.add))
                        ins = dve.tensor_tensor(qr[:, hq, cols], t1[:, :], qscale[:, hq, cols], ALU.mult)
                        ins.then_inc(s_rot, 1)
                    else:
                        if g >= 6:
                            dve.wait_ge(s_kz, b * 4 + (g - 5))
                        dve.tensor_tensor(kr[:, g % 2, :], t1[:, :], t2[:, :], ALU.add).then_inc(s_kr, 1)

                def take_output(g):
                    dve.wait_ge(s_av, b * NU + (16 * g + 16))
                    dve.tensor_copy(o[:, :], ps_av[:, :])
                    then(dve.tensor_scalar(dn[:, :], ps_dn[:, :], 1.0, 50000.0, ALU.max, ALU.min))
                    dve.nop().then_inc(s_o, 1)
                    then(dve.scalar_tensor_tensor(dn[:, :], dn[:, :], 1e-5, dn[:, :], ALU.mult, ALU.mult))

                def add_eps(g):
                    dve.wait_ge(s_var, b * NG + (g + 1))
                    dve.tensor_tensor(vq[:, :], ps_m[1][:, :], dn[:, :], ALU.add).then_inc(s_vq, 1)

                def centre(g):
                    dve.wait_ge(s_o, b * NG + (g + 1))
                    dve.wait_ge(s_mu, b * NG + (g + 1))
                    dve.tensor_tensor(oc[:, :], o[:, :], ps_m[0][:, :], ALU.subtract).then_inc(s_oc, 1)

                def scale(g):
                    dve.wait_ge(s_oc, b * NG + (g + 1))
                    dve.wait_ge(s_sd, b * NG + (g + 1))
                    then(dve.reciprocal(rsd[:, :], sd[:, :]))
                    dve.tensor_tensor(g_t[:, g // 2, HALF * (g % 2):HALF * (g % 2) + HALF],
                                      oc[:, :], rsd[:, :], ALU.mult).then_inc(s_y, 1)

                for u in range(NU):
                    hq, qn, kb, jp = unit(u)
                    h = HPQ * hq + 2 * jp
                    first = (N1 - 4 + (N1 // 2) * qn - 4 * kb) * N2
                    dve.wait_ge(s_sc, b * NU + (u + 1))
                    if u >= 3:
                        dve.wait_ge(s_av, b * NU + (u - 2))
                        dve.wait_ge(s_a, b * NU + (u - 2))
                    dve.tensor_tensor(pr[:, u % 3, :, :], ps_s[u % 2][:, :, :],
                                      decay[:, h:h + 2, first:first + HALF], ALU.mult).then_inc(s_p, 1)
                    if u >= 17 and (u - 17) % 16 == 0:
                        take_output((u - 17) // 16)
                    if u >= 20 and (u - 20) % 16 == 0:
                        centre((u - 20) // 16)
                    if u >= 24 and (u - 24) % 16 == 0:
                        add_eps((u - 24) // 16)
                    if u >= 27 and (u - 27) % 16 == 0:
                        scale((u - 27) // 16)
                take_output(NG - 1)
                centre(NG - 1)
                add_eps(NG - 1)
                scale(NG - 1)
                for t in range(TPB):
                    dve.wait_ge(s_op, b * TPB + (t + 1))
                    dve.tensor_tensor(xt[:, t, :], ps_m[t % 2][:, 0:C], xt[:, t, :], ALU.add).then_inc(s_x1, 1)
                dve.sem_clear(s_vec)

        @block.tensor
        def _(pe):
            pe.wait_ge(s_const, 16 * (7 + 2 * HPQ))
            pe.wait_ge(s_cst, 3)
            with pe.Fori(0, B) as b:
                for t in range(TPB // 2):
                    pe.wait_ge(s_xn, b * TPB + (2 * t + 2))
                    if t >= 2:
                        pe.wait_ge(s_xnT, b * 4 + (t - 1))
                    for k in range(KK):
                        for s in range(2):
                            at = (2 * k + s) * P
                            ins = pe.transpose(ps_m[t % 2][:, at:at + P], xn[:, 2 * t + s, P * k:P * k + P], ident[:, :])
                    ins.then_inc(s_tr, 1)
                for g in range(8):
                    which, hq, n = 2 * (g // 4), (g // 2) % 2, g % 2
                    pe.wait_ge(s_xnT, b * 4 + 4)
                    if g >= 2:
                        if g - 2 < 4:
                            pe.wait_ge(s_rot, b * 4 + (g - 1))
                        else:
                            pe.wait_ge(s_kr, b * 4 + (g - 5))
                    for s in range(2):
                        for k in range(KK):
                            ins = pe.matmul(ps_s[g % 2][:, s, :], wt[:, which + s, k, P * hq:P * hq + P],
                                            xnT[:, k, HALF * n:HALF * n + HALF], start=(k == 0), stop=(k == KK - 1))
                    ins.then_inc(s_proj, 1)
                for t in range(TPB // 2):
                    if t >= 2:
                        pe.wait_ge(s_v, b * 4 + (t - 1))
                    for s in range(2):
                        for k in range(KK):
                            ins = pe.matmul(ps_m[t % 2][:, C * s:C * s + C], xnT[:, k, (2 * t + s) * P:(2 * t + s + 1) * P],
                                            wt[:, 4, k, :], start=(k == 0), stop=(k == KK - 1))
                    ins.then_inc(s_vps, 1)

                pe.wait_ge(s_kr, b * 4 + 4)
                pe.wait_ge(s_rot, b * 4 + 4)
                pe.wait_ge(s_kz, b * 4 + 4)
                pe.wait_ge(s_v, b * 4 + 4)

                def scores(u):
                    hq, qn, kb, jp = unit(u)
                    if u >= 2:
                        pe.wait_ge(s_p, b * NU + (u - 1))
                    for jj in range(2):
                        h = HPQ * hq + 2 * jp + jj
                        ins = pe.matmul(ps_s[u % 2][:, jj, :], kz[:, h, P * kb:P * kb + P],
                                        qr[:, hq, HALF * qn:HALF * qn + HALF], start=True, stop=True)
                    ins.then_inc(s_sc, 1)

                def products(u):
                    hq, qn, kb, jp = unit(u)
                    if u % 16 == 0 and u > 0:
                        pe.wait_ge(s_o, b * NG + u // 16)
                    pe.wait_ge(s_a, b * NU + (u + 1))
                    for jj in range(2):
                        j = 2 * jp + jj
                        h = HPQ * hq + j
                        pe.matmul(ps_av[KD * j:KD * j + KD, :], v[:, kb, KD * h:KD * h + KD], pr[:, u % 3, jj, :],
                                  start=(kb == 0), stop=(kb == 7), tile_position=(0, KD * j), skip_group_check=True)
                        ins = pe.matmul(ps_dn[KD * j:KD * j + KD, :], ones[:, :], ab[:, u % 3, jj, :],
                                        start=(kb == 0), stop=(kb == 7), tile_position=(0, KD * j), skip_group_check=True)
                    ins.then_inc(s_av, 1)

                def mean(g):
                    pe.wait_ge(s_o, b * NG + (g + 1))
                    pe.matmul(ps_m[0][:, :], blk[:, :], o[:, :], start=True, stop=True).then_inc(s_mu, 1)

                def variance(g):
                    pe.wait_ge(s_sq, b * NG + (g + 1))
                    pe.matmul(ps_m[1][:, :], blk[:, :], sq[:, :], start=True, stop=True).then_inc(s_var, 1)

                for u in range(NU + 2):
                    if u < NU:
                        scores(u)
                    if u >= 2:
                        products(u - 2)
                    if u >= 19 and (u - 19) % 16 == 0:
                        mean((u - 19) // 16)
                    if u >= 23 and (u - 23) % 16 == 0:
                        variance((u - 23) // 16)
                mean(NG - 1)
                variance(NG - 1)
                pe.wait_ge(s_g, b * NG + NG)
                for t in range(TPB):
                    if t >= 2:
                        pe.wait_ge(s_x1, b * TPB + (t - 1))
                    for k in range(KK):
                        ins = pe.matmul(ps_m[t % 2][:, 0:C], g_t[:, k, P * t:P * t + P], wt[:, 5, k, :],
                                        start=(k == 0), stop=(k == KK - 1))
                    ins.then_inc(s_op, 1)


def attention_constants():
    half = (1.0 / 10000.0 ** np.linspace(0.0, 1.0, KD // 2).astype(np.float32)).astype(np.float32)
    angle = np.repeat(half, 2)
    index = (np.arange(N1)[:, None] + np.arange(N2)[None, :]).reshape(L).astype(np.float32)
    phase = (index[:, None] * angle[None, :]).astype(np.float32).astype(np.float64)
    sign = np.where(np.arange(KD) % 2 == 0, -1.0, 1.0)
    cos = np.tile(np.cos(phase).T, (HPQ, 1)).astype(np.float32)
    sin = np.tile((np.sin(phase) * sign).T, (HPQ, 1)).astype(np.float32)
    decay = np.log(1.0 - 2.0 ** (-2.0 - 5.0 * np.arange(H) / H))
    d1 = np.abs(np.arange(N1)[:, None] - np.arange(N1)[None, :])
    line = np.exp(d1[None] * decay[:, None, None]).sum(-1)
    total = (line[:, :, None] * line[:, None, :]).reshape(H, L)
    r = KD ** -0.5 / np.sqrt(total)
    qscale = np.repeat(r, KD, axis=0).reshape(KK, P, L).transpose(1, 0, 2).astype(np.float32)
    part = np.arange(P)
    delta = np.arange(2 * N1 - 4) - (N1 - 4)
    dist = (np.abs(delta[None, :, None] - (part // N2)[:, None, None])
            + np.abs(np.arange(N2)[None, None, :] - (part % N2)[:, None, None]))
    table = np.exp(dist[:, None] * decay[None, :, None, None]).reshape(P, H, MROW).astype(np.float32)
    blk = np.kron(np.eye(HPQ), np.full((KD, KD), 1.0 / KD)).astype(np.float32)
    return cos, sin, np.ascontiguousarray(qscale), table, blk, np.eye(P, dtype=np.float32)
GH, GE = 4, 4
GF = GH * GE
HSW = GF + GH
STW = GH + GH + GH + GF
NE = 1048576
EC = NE // P
ECH = 1024
TABLES = 8
HIST = 32
LSEG = 512
LROUNDS = 4
LPASS = LSEG // (8 * LROUNDS)
SEG = 256
CODE_BASE = 0x10000000


def edge_lists(nc, tag, edges, iota_in, codes, count, edges_left):
    with ExitStack() as ctx:
        def sb(name, shape, dt=F32):
            return ctx.enter_context(nc.sbuf_tensor(f"{tag}el_{name}", shape, dt))

        semaphores = Semaphores(nc, ctx)

        def sem(name):
            return semaphores.new(f"{tag}el_s_{name}")

        RC = EC // SEG * 8
        LC = EC // LSEG * 8
        src = sb("src", [P, 2, ECH], I32)
        dst = sb("dst", [P, 2, ECH], I32)
        sf = sb("sf", [P, ECH])
        df = sb("df", [P, ECH])
        fa = sb("fa", [P, ECH])
        fb = sb("fb", [P, ECH])
        ia = sb("ia", [P, ECH], I32)
        ib = sb("ib", [P, ECH], I32)
        code = sb("code", [P, EC], I32)
        key = sb("key", [P, EC])
        lo = sb("lo", [P, RC], BF16)
        hi = sb("hi", [P, RC], BF16)
        cand = sb("cand", [P, RC])
        segs = sb("segs", [P, EC // SEG])
        iota = sb("iota", [P, P, HIST], BF16)
        one_lo = sb("one_lo", [P, 2, P, HIST], BF16)
        one_hi = sb("one_hi", [P, 2, NT, HIST], BF16)
        zero = sb("zero", [P, P], BF16)
        tot = sb("tot", [P, 2])
        top = sb("top", [P, 2])
        rounds = sb("rounds", [P, 1], I32)
        m8 = sb("m8", [P, 8], F32)
        lsegs = sb("lsegs", [P, EC // LSEG])
        picked = sb("picked", [P, LROUNDS * LC])
        n_own = sb("n_own", [P, 1])
        n_all = sb("n_all", [P, 1])
        blocks = sb("blocks", [P, 1], I32)
        passes = sb("passes", [P, 1], I32)
        ps = ctx.enter_context(nc.psum_tensor(f"{tag}el_ps", [P, NT], F32))
        s_in, s_vec, s_free, s_tot, s_top, s_zero = (
            sem("iota"), sem("vec"), sem("free"), sem("tot"), sem("top"), sem("zero"))
        s_edges = [sem("edges0"), sem("edges1")]
        s_one, s_hist, s_left, s_loop, s_own, s_all, s_turn = (
            sem(k) for k in ("one", "hist", "left", "loop", "own", "all", "turn_p"))
        NCH = EC // ECH
        edges_v = edges.rearrange("a (p n) -> a p n", p=P)
        block = ctx.enter_context(nc.Block())

        @block.sync
        def _(sp):
            sp.dma_start(iota[:, :, :], iota_in).then_inc(s_in, 16)
            for c in range(NCH):
                if c >= 2:
                    sp.wait_ge(s_free, c - 1)
                sp.dma_start(src[:, c % 2, :], edges_v[0, :, ECH * c:ECH * c + ECH]).then_inc(s_edges[c % 2], 16)
                sp.dma_start(dst[:, c % 2, :], edges_v[1, :, ECH * c:ECH * c + ECH]).then_inc(s_edges[c % 2], 16)

        @block.gpsimd
        def _(pool):
            pool.memset(zero[:, :], 0.0).then_inc(s_zero, 1)
            pool.wait_ge(s_tot, 1)
            pool.partition_all_reduce(top[:, :], tot[:, :], P, bass.bass_isa.ReduceOp.max).then_inc(s_top, 1)
            pool.wait_ge(s_left, 1)
            n_passes = pool.value_load(passes[0:1, 0:1], min_val=1, max_val=LPASS)
            with pool.Fori(0, n_passes) as i:
                pool.wait_ge(s_own, i + 1)
                pool.sem_inc(s_turn, 1)
                pool.partition_all_reduce(n_all[:, :], n_own[:, :], P, bass.bass_isa.ReduceOp.max).then_inc(s_all, 1)

        @block.tensor
        def _(pe):
            pe.wait_ge(s_zero, 1)
            pe.matmul(ps[:, :], zero[:, :], zero[:, 0:NT], start=True, stop=False, skip_group_check=True)
            pe.sem_inc(s_hist, 2)
            pe.wait_ge(s_left, 1)
            n_rounds = pe.value_load(rounds[0:1, 0:1], min_val=1, max_val=SEG // 8)
            with pe.Fori(0, n_rounds) as i:
                for q in range(RC // HIST):
                    pe.wait_ge(s_one, i * (RC // HIST) + (q + 1))
                    for j in range(HIST):
                        ins = pe.matmul(ps[:, :], one_lo[:, q % 2, :, j], one_hi[:, q % 2, :, j], start=False, stop=False,
                                        skip_group_check=True)
                    ins.then_inc(s_hist, 1)
            pe.matmul(ps[:, :], zero[:, :], zero[:, 0:NT], start=False, stop=True, skip_group_check=True).then_inc(s_loop, 1)

        @block.vector
        def _(dve):
            steps = [0]

            def then(ins):
                steps[0] += 1
                ins.then_inc(s_vec, 1)
                dve.wait_ge(s_vec, steps[0])

            dve.wait_ge(s_in, 16)
            for c in range(NCH):
                dve.wait_ge(s_edges[c % 2], 32 * (c // 2 + 1))
                s, cols = c % 2, slice(ECH * c, ECH * c + ECH)
                then(dve.tensor_scalar(sf[:, :], src[:, s, :], float(-M), float(M - 1), ALU.max, ALU.min))
                then(dve.tensor_scalar(fa[:, :], sf[:, :], 0.0, float(M), ALU.is_lt, ALU.mult))
                then(dve.tensor_tensor(sf[:, :], sf[:, :], fa[:, :], ALU.add))
                then(dve.tensor_scalar(df[:, :], dst[:, s, :], -1.0, float(M), ALU.max, ALU.min))
                then(dve.tensor_scalar(fa[:, :], df[:, :], 0.0, None, ALU.is_ge))
                then(dve.scalar_tensor_tensor(fb[:, :], df[:, :], float(M), fa[:, :], ALU.is_lt, ALU.mult))
                then(dve.scalar_tensor_tensor(fa[:, :], sf[:, :], float(M - 1), fb[:, :], ALU.is_lt, ALU.mult))
                then(dve.tensor_reduce(lsegs[:, c * (ECH // LSEG):(c + 1) * (ECH // LSEG)],
                                       fa[:, :].rearrange("p (s w) -> p s w", w=LSEG), AX.X, ALU.add))
                then(dve.tensor_copy(ia[:, :], sf[:, :]))
                then(dve.tensor_copy(ib[:, :], df[:, :]))
                then(dve.tensor_scalar(code[:, cols], ib[:, :], 13, CODE_BASE, ALU.logical_shift_left, ALU.bitwise_or))
                then(dve.tensor_tensor(ia[:, :], ia[:, :], code[:, cols], ALU.bitwise_or))
                ins = dve.tensor_scalar(code[:, cols], fa[:, :], -1.0, None, ALU.mult)
                then(ins)
                then(dve.tensor_tensor(code[:, cols], code[:, cols], ia[:, :], ALU.bitwise_and))
                then(dve.tensor_tensor(fb[:, :], fb[:, :], fa[:, :], ALU.subtract))
                then(dve.scalar_tensor_tensor(key[:, cols], df[:, :], 1.0, fb[:, :], ALU.add, ALU.mult))
                then(dve.tensor_reduce(segs[:, c * (ECH // SEG):(c + 1) * (ECH // SEG)],
                                       fb[:, :].rearrange("p (s w) -> p s w", w=SEG), AX.X, ALU.add))
                dve.nop().then_inc(s_free, 1)
            then(dve.tensor_reduce(tot[:, 0:1], lsegs[:, :], AX.X, ALU.max))
            dve.tensor_reduce(tot[:, 1:2], segs[:, :], AX.X, ALU.max).then_inc(s_tot, 1)
            dve.wait_ge(s_top, 1)
            then(dve.tensor_scalar(ia[:, 0:1], top[:, 0:1], 8.0 * LROUNDS - 1.0, 8.0 * LROUNDS, ALU.add, ALU.max))
            then(dve.tensor_scalar(ia[:, 1:2], top[:, 1:2], 7.0, 8.0, ALU.add, ALU.max))
            then(dve.tensor_scalar(passes[:, 0:1], ia[:, 0:1], 5, None, ALU.logical_shift_right))
            then(dve.tensor_scalar(rounds[:, 0:1], ia[:, 1:2], 3, None, ALU.logical_shift_right))
            dve.nop().then_inc(s_left, 1)
            n_rounds = dve.value_load(rounds[0:1, 0:1], min_val=1, max_val=SEG // 8)
            dve.sem_clear(s_vec)
            with dve.Fori(0, n_rounds) as i:
                steps[0] = 0
                for g in range(EC // SEG):
                    ins = dve.max(cand[:, 8 * g:8 * g + 8], key[:, SEG * g:SEG * g + SEG])
                then(ins)
                for g in range(EC // SEG):
                    part_of = key[:, SEG * g:SEG * g + SEG]
                    ins = dve.match_replace(part_of, cand[:, 8 * g:8 * g + 8], part_of, 0.0)
                then(ins)
                then(dve.tensor_scalar(ia[:, 0:RC], cand[:, :], -1.0, None, ALU.add))
                then(dve.tensor_scalar(ib[:, 0:RC], ia[:, 0:RC], P - 1, None, ALU.bitwise_and))
                then(dve.tensor_copy(lo[:, :], ib[:, 0:RC]))
                then(dve.tensor_scalar(ia[:, 0:RC], ia[:, 0:RC], 7, None, ALU.arith_shift_right))
                then(dve.tensor_copy(hi[:, :], ia[:, 0:RC]))
                for q in range(RC // HIST):
                    dve.wait_ge(s_hist, i * (RC // HIST) + (q + 1))
                    cols = slice(HIST * q, HIST * q + HIST)
                    dve.tensor_tensor(one_lo[:, q % 2, :, :], iota[:, :, :],
                                      lo[:, cols].unsqueeze(1).to_broadcast([P, P, HIST]), ALU.is_equal)
                    dve.tensor_tensor(one_hi[:, q % 2, :, :], iota[:, 0:NT, :],
                                      hi[:, cols].unsqueeze(1).to_broadcast([P, NT, HIST]), ALU.is_equal).then_inc(s_one, 1)
                dve.sem_clear(s_vec)
            steps[0] = 0
            dve.wait_ge(s_loop, 1)
            then(dve.tensor_copy(count[:, :], ps[:, :]))
            n_passes = dve.value_load(passes[0:1, 0:1], min_val=1, max_val=LPASS)
            codef = code[:, :].bitcast(F32)
            then(dve.memset(codes[:, :], 0))
            then(dve.memset(edges_left[:, :], 0))
            dve.sem_clear(s_vec)
            with dve.Fori(0, n_passes) as i:
                steps[0] = 0
                for q in range(LROUNDS):
                    for g in range(EC // LSEG):
                        to = LC * q + 8 * g
                        ins = dve.max(picked[:, to:to + 8], codef[:, LSEG * g:LSEG * g + LSEG])
                    then(ins)
                    for g in range(EC // LSEG):
                        to = LC * q + 8 * g
                        part_of = codef[:, LSEG * g:LSEG * g + LSEG]
                        ins = dve.match_replace(part_of, picked[:, to:to + 8], part_of, 0.0)
                    then(ins)
                then(dve.tensor_scalar(fa[:, 0:LROUNDS * LC], picked[:, :], 0.0, None, ALU.is_gt))
                dve.tensor_reduce(n_own[:, :], fa[:, 0:LROUNDS * LC], AX.X, ALU.add).then_inc(s_own, 1)
                dve.wait_ge(s_all, i + 1)
                then(dve.tensor_scalar(ia[:, 0:1], n_all[:, :], 7.0, 8.0, ALU.add, ALU.max))
                then(dve.tensor_scalar(blocks[:, 0:1], ia[:, 0:1], 3, None, ALU.logical_shift_right))
                n = dve.value_load(blocks[0:1, 0:1], min_val=1, max_val=LROUNDS * LC // 8)
                base = dve.value_load(edges_left[0:1, 0:1], min_val=0, max_val=(LPASS - 1) * (LROUNDS * LC // 8))
                dve.sem_clear(s_vec)
                with dve.Fori(0, n) as j:
                    steps[0] = 0
                    then(dve.max(m8[:, :], picked[:, :]))
                    then(dve.tensor_copy(codes[:, bass.ds((base + j) * 8, 8)], m8[:, :].bitcast(I32)))
                    then(dve.match_replace(picked[:, :], m8[:, :], picked[:, :], 0.0))
                    dve.sem_clear(s_vec)
                steps[0] = 0
                then(dve.tensor_tensor(edges_left[:, :], edges_left[:, :], blocks[:, :], ALU.add))
                dve.sem_clear(s_vec)


GTOK = 1024
NGT = M // GTOK


def normalised_nodes(nc, tag, x_in, tT, hs_rows, ad, w_gat, att_src, att_dst, ident_in):
    with ExitStack() as ctx:
        def sb(name, shape, dt=F32):
            return ctx.enter_context(nc.sbuf_tensor(f"{tag}nn_{name}", shape, dt))

        semaphores = Semaphores(nc, ctx)

        def sem(name):
            return semaphores.new(f"{tag}nn_s_{name}")

        ident = sb("ident", [P, P])
        wg = sb("wg", [P, KK, GF])
        a_s = sb("a_s", [P, GF])
        a_d = sb("a_d", [P, GF])
        xt = sb("xt", [P, 2, TPB, C])
        xn = sb("xn", [P, 2, TPB, C])
        xnT = sb("xnT", [P, 2, KK, L])
        stats = sb("stats", [P, TPB, 6])
        mv = sb("mv", [P, TPB, 2])
        ve = sb("ve", [P, TPB])
        nhalf = sb("nhalf", [P, TPB])
        rstd = sb("rstd", [P, TPB])
        hs = sb("hs", [P, 2, TPB, HSW])
        tmp = sb("tmp", [P, TPB, GF])
        tmp2 = sb("tmp2", [P, TPB, GF])
        ps = [ctx.enter_context(nc.psum_tensor(f"{tag}nn_ps{i}", [P, 512], F32)) for i in range(2)]
        ps_h = [ctx.enter_context(nc.psum_tensor(f"{tag}nn_psh{i}", [P, TPB, GF], F32)) for i in range(2)]
        s_const, s_half = sem("const"), sem("half")
        s_x = [sem("x0"), sem("x1")]
        s_tT = [sem("tT0"), sem("tT1")]
        s_hs = [sem("hs0"), sem("hs1")]
        s_vec, s_ve, s_rstd, s_xn, s_tr, s_xnT, s_h, s_hsb, s_left = (
            sem(k) for k in ("vec", "ve", "rstd", "xn", "tr", "xnT", "h", "hsb", "left"))
        HALFG = NGT // 2
        s_turn = sem("turn")
        block = ctx.enter_context(nc.Block())

        @block.sync
        def _(sp):
            sp.dma_start(ident[:, :], ident_in).then_inc(s_const, 16)
            sp.dma_start(wg[:, :, :], w_gat).then_inc(s_const, 16)
            sp.dma_start(a_s[:, :], att_src.to_broadcast([P, GF])).then_inc(s_const, 16)
            sp.dma_start(a_d[:, :], att_dst.to_broadcast([P, GF])).then_inc(s_const, 16)
            with sp.Fori(0, HALFG) as i:
                for s in range(2):
                    sp.wait_ge(s_xn, i * (2 * TPB) + (s * TPB + TPB))
                    sp.sem_inc(s_turn, 1)
                    sp.dma_start(xt[:, s, :, :], x_in[bass.ds(i * (2 * L) + s * L, L), :]
                                 .rearrange("(t p) c -> p t c", p=P)).then_inc(s_x[s], 16)

        @block.gpsimd
        def _(pool):
            pool.memset(nhalf[:, :], -0.5).then_inc(s_half, 1)
            pool.sem_inc(s_xn, 2 * TPB)
            pool.wait_ge(s_half, 1)
            with pool.Fori(0, HALFG) as i:
                for s in range(2):
                    pool.wait_ge(s_ve, i * 2 + (s + 1))
                    pool.tensor_tensor(rstd[:, :], ve[:, :], nhalf[:, :], ALU.pow).then_inc(s_rstd, 1)

        @block.vector
        def _(dve):
            steps = [0]

            def then(ins):
                steps[0] += 1
                ins.then_inc(s_vec, 1)
                dve.wait_ge(s_vec, steps[0])

            dve.wait_ge(s_const, 64)
            with dve.Fori(0, HALFG) as i:
                steps[0] = 0
                for s in range(2):
                    dve.wait_ge(s_x[s], i * 16 + 16)
                    for t in range(TPB):
                        ins = dve.bn_stats(stats[:, t, :], xt[:, s, t, :])
                    then(ins)
                    for t in range(TPB):
                        ins = dve.bn_aggr(mv[:, t, :], stats[:, t, :])
                    then(ins)
                    dve.tensor_scalar(ve[:, :], mv[:, :, 1], 1e-5, None, ALU.add).then_inc(s_ve, 1)
                    dve.wait_ge(s_rstd, i * 2 + (s + 1))
                    dve.wait_ge(s_tr, i * 8 + (4 * s + 4))
                    for t in range(TPB):
                        dve.tensor_scalar(xn[:, s, t, :], xt[:, s, t, :], mv[:, t, 0:1], rstd[:, t:t + 1],
                                          ALU.subtract, ALU.mult).then_inc(s_xn, 1)
                    dve.wait_ge(s_h, i * 2 + (s + 1))
                    dve.wait_ge(s_left, i + 1)
                    f = ps_h[s][:, :, :]
                    then(dve.tensor_copy(hs[:, s, :, 0:GF], f))
                    then(dve.tensor_tensor(tmp[:, :, :], f, a_s[:, :].unsqueeze(1).to_broadcast([P, TPB, GF]), ALU.mult))
                    then(dve.tensor_tensor(tmp2[:, :, :], f, a_d[:, :].unsqueeze(1).to_broadcast([P, TPB, GF]), ALU.mult))
                    dve.tensor_reduce(hs[:, s, :, GF:HSW], tmp[:, :, :].rearrange("p t (h e) -> p t h e", e=GE),
                                      AX.X, ALU.add).then_inc(s_hsb, 1)
                    then(dve.tensor_reduce(ad[:, bass.ds(i * (2 * TPB) + s * TPB, TPB), :],
                                           tmp2[:, :, :].rearrange("p t (h e) -> p t h e", e=GE), AX.X, ALU.add))
                dve.sem_clear(s_vec)

        @block.tensor
        def _(pe):
            pe.wait_ge(s_const, 64)
            pe.sem_inc(s_tr, 8)
            with pe.Fori(0, HALFG) as i:
                for s in range(2):
                    for t in range(TPB // 2):
                        pe.wait_ge(s_xn, i * (2 * TPB) + (2 * TPB + s * TPB + 2 * t + 2))
                        pe.wait_ge(s_xnT, i * 8 + (4 * s + t + 1))
                        for k in range(KK):
                            for q in range(2):
                                at = (2 * k + q) * P
                                ins = pe.transpose(ps[t % 2][:, at:at + P], xn[:, s, 2 * t + q, P * k:P * k + P], ident[:, :])
                        ins.then_inc(s_tr, 1)
                    pe.wait_ge(s_xnT, i * 8 + (4 * s + 6))
                    pe.wait_ge(s_hsb, i * 2 + (s + 1))
                    for t in range(TPB):
                        for k in range(KK):
                            ins = pe.matmul(ps_h[s][:, t, :], xnT[:, s, k, P * t:P * t + P], wg[:, k, :],
                                            start=(k == 0), stop=(k == KK - 1))
                    ins.then_inc(s_h, 1)

        @block.scalar
        def _(act):
            act.sem_inc(s_xnT, 2)
            act.sem_inc(s_hsb, 2)
            act.sem_inc(s_left, 1)
            with act.Fori(0, HALFG) as i:
                for s in range(2):
                    act.wait_ge(s_hsb, i * 2 + (s + 1))
                    for t in range(TPB // 2):
                        act.wait_ge(s_tr, i * 8 + (8 + 4 * s + t + 1))
                        act.activation(xnT[:, s, :, 2 * P * t:2 * P * t + 2 * P],
                                       ps[t % 2][:, :].rearrange("p (k c) -> p k c", k=KK), ACT.Copy).then_inc(s_xnT, 1)
                    act.wait_ge(s_xnT, i * 8 + (4 * s + 6))
                    act.dma_start(tT[bass.ds(i * 2 + s, 1), :, :, :].rearrange("a p k l -> p (a k l)"),
                                  xnT[:, s, :, :].rearrange("p k l -> p (k l)")).then_inc(s_tT[s], 16)
                    act.wait_ge(s_hsb, i * 2 + (s + 3))
                    act.dma_start(hs_rows[bass.ds(i * (2 * L) + s * L, L), :].rearrange("(t p) c -> p t c", p=P),
                                  hs[:, s, :, :]).then_inc(s_hs[s], 16)
                for s in range(2):
                    act.wait_ge(s_tT[s], i * 16 + 16)
                    act.wait_ge(s_hs[s], i * 16 + 16)
                act.sem_inc(s_left, 1)
            for s in range(2):
                act.wait_ge(s_tT[s], 16 * HALFG)
                act.wait_ge(s_hs[s], 16 * HALFG)


def target_rows(nc, tag, hs_rows, ad, count, st):
    with ExitStack() as ctx:
        def sb(name, shape, dt=F32):
            return ctx.enter_context(nc.sbuf_tensor(f"{tag}tr_{name}", shape, dt))

        semaphores = Semaphores(nc, ctx)

        def sem(name):
            return semaphores.new(f"{tag}tr_s_{name}")

        hs = sb("hs", [P, NT, HSW])
        last = sb("last", [P, HSW])
        row = sb("row", [P, NT, STW])
        row0 = sb("row0", [P, NT, STW])
        es = sb("es", [P, NT, GH])
        el = sb("el", [P, NT, GH])
        tm = sb("tm", [P, NT, GH])
        cz = sb("cz", [P, NT])
        ps_, pl = sb("ps", [P, NT, GH]), sb("pl", [P, NT, GH])
        acc = sb("acc", [P, NT, GF])
        acc2 = sb("acc2", [P, NT, GF])
        s_in, s_vec, s_e, s_p, s_done, s_out = (sem(k) for k in ("in", "vec", "e", "p", "done", "out"))
        s_turn = sem("turn")
        block = ctx.enter_context(nc.Block())

        @block.sync
        def _(sp):
            sp.dma_start(hs[:, :, :], hs_rows[:, :].rearrange("(t p) c -> p t c", p=P)).then_inc(s_in, 16)
            sp.dma_start(last[:, :], hs_rows[M - 1:M, :].to_broadcast([P, HSW])).then_inc(s_in, 16)
            sp.wait_ge(s_done, 1)
            sp.dma_start(st[0, :, :].rearrange("(t p) c -> p t c", p=P), row0[:, :, :]).then_inc(s_out, 16)
            for k in range(1, TABLES):
                sp.dma_start(st[k, :, :].rearrange("(t p) c -> p t c", p=P), row[:, :, :]).then_inc(s_out, 16)
            sp.wait_ge(s_out, 16 * TABLES)

        @block.scalar
        def _(act):
            act.wait_ge(s_e, 1)
            act.activation(ps_[:, :, :], es[:, :, :], ACT.Exp).then_inc(s_p, 1)
            act.activation(pl[:, :, :], el[:, :, :], ACT.Exp).then_inc(s_p, 1)

        @block.vector
        def _(dve):
            steps = [0]

            def then(ins):
                steps[0] += 1
                ins.then_inc(s_vec, 1)
                dve.wait_ge(s_vec, steps[0])

            def leaky(out, z, t):
                then(dve.tensor_scalar(t, z, 0.2, None, ALU.mult))
                then(dve.tensor_tensor(out, z, t, ALU.max))

            dve.wait_ge(s_in, 32)
            then(dve.tensor_tensor(es[:, :, :], hs[:, :, GF:HSW], ad[:, :, :], ALU.add))
            leaky(es[:, :, :], es[:, :, :], tm[:, :, :])
            then(dve.tensor_tensor(el[:, :, :], ad[:, :, :], last[:, GF:HSW].unsqueeze(1).to_broadcast([P, NT, GH]), ALU.add))
            leaky(el[:, :, :], el[:, :, :], tm[:, :, :])
            m = row[:, :, GH:2 * GH]
            then(dve.tensor_scalar(cz[:, :], count[:, :], 1.0, None, ALU.min))
            then(dve.tensor_tensor(tm[:, :, :], el[:, :, :], es[:, :, :], ALU.subtract))
            then(dve.tensor_scalar(tm[:, :, :], tm[:, :, :], 0.0, None, ALU.max))
            then(dve.tensor_tensor(tm[:, :, :], tm[:, :, :], cz[:, :].unsqueeze(2).to_broadcast([P, NT, GH]), ALU.mult))
            then(dve.tensor_tensor(m, es[:, :, :], tm[:, :, :], ALU.add))
            then(dve.tensor_tensor(es[:, :, :], es[:, :, :], m, ALU.subtract))
            then(dve.tensor_tensor(el[:, :, :], el[:, :, :], m, ALU.subtract))
            dve.tensor_scalar(el[:, :, :], el[:, :, :], 0.0, None, ALU.min).then_inc(s_e, 1)
            dve.memset(row[:, :, 2 * GH:STW], 0.0)
            then(dve.tensor_copy(row[:, :, 0:GH], ad[:, :, :]))
            then(dve.tensor_copy(row0[:, :, 0:2 * GH], row[:, :, 0:2 * GH]))
            dve.wait_ge(s_p, 2)
            then(dve.tensor_tensor(pl[:, :, :], pl[:, :, :], count[:, :].unsqueeze(2).to_broadcast([P, NT, GH]), ALU.mult))
            then(dve.tensor_tensor(row0[:, :, 2 * GH:3 * GH], ps_[:, :, :], pl[:, :, :], ALU.add))
            for h in range(GH):
                own = hs[:, :, GE * h:GE * h + GE]
                then(dve.tensor_tensor(acc[:, :, GE * h:GE * h + GE], own,
                                       ps_[:, :, h:h + 1].to_broadcast([P, NT, GE]), ALU.mult))
                then(dve.tensor_tensor(acc2[:, :, GE * h:GE * h + GE],
                                       last[:, GE * h:GE * h + GE].unsqueeze(1).to_broadcast([P, NT, GE]),
                                       pl[:, :, h:h + 1].to_broadcast([P, NT, GE]), ALU.mult))
            dve.tensor_tensor(row0[:, :, 3 * GH:STW], acc[:, :, :], acc2[:, :, :], ALU.add).then_inc(s_done, 1)


def edge_sums(nc, tag, hs_rows, st, codes, edges_left, ident_in, iota_f_in):
    with ExitStack() as ctx:
        def sb(name, shape, dt=F32):
            return ctx.enter_context(nc.sbuf_tensor(f"{tag}es_{name}", shape, dt))

        semaphores = Semaphores(nc, ctx)

        def sem(name):
            return semaphores.new(f"{tag}es_s_{name}")

        K = TABLES // 2
        ident = sb("ident", [P, P])
        below = sb("below", [P, P])
        i_src2 = sb("i_src", [P, 2, K], I32)
        i_dst2 = sb("i_dst", [P, 2, K], I32)
        i_out2 = sb("i_out", [P, 2, K], I32)
        code = sb("code", [P, K], I32)
        flag = sb("flag", [P, K], I32)
        vo2 = sb("vo", [P, 2, K])
        d2 = sb("d", [P, 2, K])
        vd = sb("vd", [P, K])
        g2 = sb("g", [P, 2, K, HSW])
        r2 = sb("r", [P, 2, K, STW])
        nr2 = sb("nr", [P, 2, K, STW])
        same2 = sb("same", [P, 2, K, P])
        far2 = sb("far", [P, 2, K, P])
        rk = sb("rk", [P, K, P])
        rank = sb("rank", [P, K])
        e = sb("e", [P, K, GH])
        et = sb("et", [P, K, GH])
        big = sb("big", [P, GH, P])
        gm = sb("gm", [P, K, GH])
        xm = sb("xm", [P, 2, K, GH])
        xe = sb("xe", [P, 2, K, GH])
        pay = sb("pay", [P, K, HSW])
        sc = sb("sc", [P, K, HSW])
        ps_d = ctx.enter_context(nc.psum_tensor(f"{tag}es_psd", [P, K, P], F32))
        ps_e = [ctx.enter_context(nc.psum_tensor(f"{tag}es_pse{k}", [P, GH, P], F32)) for k in range(K)]
        ps_g = ctx.enter_context(nc.psum_tensor(f"{tag}es_psg", [P, K, HSW], F32))
        s_const, s_vec, s_idx, s_dd, s_d, s_e, s_eb, s_x, s_xe, s_pay, s_gs, s_new, s_io = (
            sem(k) for k in ("const", "vec", "idx", "dd", "d", "e", "eb", "x", "xe", "pay", "gs", "new", "io"))
        s_free = [sem("free0"), sem("free1")]
        s_src = [[sem(f"src{s}{k}") for k in range(K)] for s in range(2)]
        s_dst = [[sem(f"dst{s}{k}") for k in range(K)] for s in range(2)]
        s_wr = [[sem(f"wr{s}{k}") for k in range(K)] for s in range(2)]
        block = ctx.enter_context(nc.Block())

        def steps_of(eng):
            n = eng.value_load(edges_left[0:1, 0:1], min_val=1, max_val=EC // 8)
            return n

        @block.sync
        def _(sp):
            sp.dma_start(ident[:, :], ident_in).then_inc(s_const, 16)
            sp.dma_start(below[:, :], iota_f_in).then_inc(s_const, 16)

        @block.gpsimd
        def _(pool):
            def read_targets(s):
                for k in range(K):
                    pool.indirect_dma_start(r2[:, s, k, :], None, st[K * s + k],
                                            bass.IndirectOffsetOnAxis(ap=i_dst2[:, s, k:k + 1].bitcast(U32), axis=0)).then_inc(s_dst[s][k], 16)

            def read_sources(s, call):
                pool.wait_ge(s_idx, call)
                pool.sem_inc(s_io, 1)
                for k in range(K):
                    pool.indirect_dma_start(g2[:, s, k, :], None, hs_rows[:, :],
                                            bass.IndirectOffsetOnAxis(ap=i_src2[:, s, k:k + 1].bitcast(U32), axis=0)).then_inc(s_src[s][k], 16)

            for s in range(2):
                pool.sem_inc(s_free[s], 1)
                read_sources(s, s + 1)
                read_targets(s)
            with pool.Fori(0, steps_of(pool)) as i:
                for s in range(2):
                    pool.wait_ge(s_new, i * 2 + (s + 1))
                    pool.sem_inc(s_io, 1)
                    for k in range(K):
                        pool.indirect_dma_start(st[K * s + k], bass.IndirectOffsetOnAxis(ap=i_out2[:, s, k:k + 1].bitcast(U32), axis=0),
                                                nr2[:, s, k, :], None, bounds_check=M - 1, oob_is_err=False).then_inc(s_wr[s][k], 16)
                    read_sources(s, i * 2 + (s + 3))
                    for k in range(K):
                        pool.wait_ge(s_wr[s][k], i * 16 + 16)
                    pool.sem_inc(s_free[s], 1)
                    read_targets(s)
            n = steps_of(pool)
            for s in range(2):
                for k in range(K):
                    pool.wait_ge(s_src[s][k], n * 16 + 16)
                    pool.wait_ge(s_dst[s][k], n * 16 + 16)
            pool.sem_inc(s_io, 1)

        @block.vector
        def _(dve):
            steps = [0]

            def then(ins):
                steps[0] += 1
                ins.then_inc(s_vec, 1)
                dve.wait_ge(s_vec, steps[0])

            dve.wait_ge(s_const, 32)
            def indices(s, step, call):
                i_src, i_dst, i_out, d = i_src2[:, s, :], i_dst2[:, s, :], i_out2[:, s, :], d2[:, s, :]
                g, r, nr, same, far = g2[:, s, :, :], r2[:, s, :, :], nr2[:, s, :, :], same2[:, s, :, :], far2[:, s, :, :]
                then(dve.tensor_copy(code[:, :], codes[:, bass.ds(step * (2 * K) + K * s, K)]))
                then(dve.tensor_scalar(i_src[:, :], code[:, :], M - 1, None, ALU.bitwise_and))
                dve.tensor_scalar(i_dst[:, :], code[:, :], 13, M - 1, ALU.logical_shift_right, ALU.bitwise_and).then_inc(s_idx, 1)
                then(dve.tensor_scalar(flag[:, :], code[:, :], 28, 1, ALU.logical_shift_right, ALU.bitwise_xor))
                then(dve.tensor_copy(vd[:, :], flag[:, :]))
                dve.wait_ge(s_idx, call)
                then(dve.tensor_copy(d[:, :], i_dst[:, :]))
                then(dve.scalar_tensor_tensor(d[:, :], vd[:, :], float(M), d[:, :], ALU.mult, ALU.add))
                dve.nop().then_inc(s_dd, 1)
                dve.wait_ge(s_d, call)
                for k in range(K):
                    dve.tensor_scalar(same[:, k, :], ps_d[:, k, :], d[:, k:k + 1], None, ALU.is_equal)
                    ins = dve.tensor_scalar(far[:, k, :], ps_d[:, k, :], d[:, k:k + 1], -1e30, ALU.not_equal, ALU.mult)
                then(ins)
                then(dve.tensor_tensor(rk[:, :, :], same[:, :, :], below[:, :].unsqueeze(1).to_broadcast([P, K, P]), ALU.mult))
                then(dve.tensor_reduce(rank[:, :], rk[:, :, :], AX.X, ALU.max))
                then(dve.scalar_tensor_tensor(vo2[:, s, :], rank[:, :], float(M), d[:, :], ALU.mult, ALU.add))

            def take_up(s, i):
                i_src, i_dst, i_out, d = i_src2[:, s, :], i_dst2[:, s, :], i_out2[:, s, :], d2[:, s, :]
                g, r, nr, same, far = g2[:, s, :, :], r2[:, s, :, :], nr2[:, s, :, :], same2[:, s, :, :], far2[:, s, :, :]
                dve.wait_ge(s_free[s], i + 1)
                then(dve.tensor_copy(i_out[:, :], vo2[:, s, :]))
                for k in range(K):
                    dve.wait_ge(s_src[s][k], i * 16 + 16)
                    dve.wait_ge(s_dst[s][k], i * 16 + 16)
                then(dve.tensor_tensor(e[:, :, :], g[:, :, GF:HSW], r[:, :, 0:GH], ALU.add))
                then(dve.tensor_scalar(et[:, :, :], e[:, :, :], 0.2, None, ALU.mult))
                then(dve.tensor_tensor(e[:, :, :], e[:, :, :], et[:, :, :], ALU.max))
                dve.nop().then_inc(s_e, 1)
                for k in range(K):
                    dve.wait_ge(s_eb, i * (2 * K) + (K * s + k + 1))
                    then(dve.tensor_tensor(big[:, :, :], ps_e[k][:, :, :], far[:, k:k + 1, :].to_broadcast([P, GH, P]), ALU.add))
                    then(dve.tensor_reduce(gm[:, k, :], big[:, :, :], AX.X, ALU.max))
                m_old, m_new = r[:, :, GH:2 * GH], nr[:, :, GH:2 * GH]
                then(dve.tensor_tensor(m_new, m_old, gm[:, :, :], ALU.max))
                then(dve.tensor_tensor(xm[:, 0, :, :], m_old, m_new, ALU.subtract))
                then(dve.tensor_tensor(xm[:, 1, :, :], e[:, :, :], m_new, ALU.subtract))
                then(dve.tensor_scalar(xm[:, :, :, :], xm[:, :, :, :], 0.0, None, ALU.min))
                dve.nop().then_inc(s_x, 1)
                dve.wait_ge(s_xe, i * 2 + (s + 1))
                then(dve.tensor_copy(pay[:, :, 0:GH], xe[:, 1, :, :]))
                then(dve.tensor_copy(sc[:, :, 0:GH], xe[:, 0, :, :]))
                for k in range(K):
                    ins = dve.tensor_tensor(pay[:, k, GH:HSW].rearrange("p (h e) -> p h e", e=GE),
                                      g[:, k, 0:GF].rearrange("p (h e) -> p h e", e=GE),
                                      xe[:, 1, k, :].unsqueeze(2).to_broadcast([P, GH, GE]), ALU.mult)
                then(ins)
                dve.nop().then_inc(s_pay, 1)
                for k in range(K):
                    dve.tensor_tensor(sc[:, k, GH:HSW].rearrange("p (h e) -> p h e", e=GE),
                                      r[:, k, 3 * GH:STW].rearrange("p (h e) -> p h e", e=GE),
                                      xe[:, 0, k, :].unsqueeze(2).to_broadcast([P, GH, GE]), ALU.mult)
                dve.tensor_copy(nr[:, :, 0:GH], r[:, :, 0:GH])
                then(dve.tensor_tensor(sc[:, :, 0:GH], sc[:, :, 0:GH], r[:, :, 2 * GH:3 * GH], ALU.mult))
                dve.wait_ge(s_gs, i * 2 + (s + 1))
                then(dve.tensor_tensor(nr[:, :, 2 * GH:STW], sc[:, :, :], ps_g[:, :, :], ALU.add))
                dve.nop().then_inc(s_new, 1)


            for s in range(2):
                indices(s, 0, s + 1)
            dve.sem_clear(s_vec)
            with dve.Fori(0, steps_of(dve)) as i:
                steps[0] = 0
                for s in range(2):
                    take_up(s, i)
                    indices(s, i + 1, i * 2 + (s + 3))
                dve.sem_clear(s_vec)

        @block.scalar
        def _(act):
            with act.Fori(0, steps_of(act)) as i:
                for s in range(2):
                    act.wait_ge(s_x, i * 2 + (s + 1))
                    act.activation(xe[:, :, :, :], xm[:, :, :, :], ACT.Exp).then_inc(s_xe, 1)

        @block.tensor
        def _(pe):
            pe.wait_ge(s_const, 32)
            def along(s, call):
                pe.wait_ge(s_dd, call)
                for k in range(K):
                    ins = pe.matmul(ps_d[:, k, :], d2[:, s, k:k + 1].to_broadcast([P, P]), ident[:, :], start=True, stop=True)
                ins.then_inc(s_d, 1)

            for s in range(2):
                along(s, s + 1)
            with pe.Fori(0, steps_of(pe)) as i:
                for s in range(2):
                    pe.wait_ge(s_e, i * 2 + (s + 1))
                    for k in range(K):
                        for h in range(GH):
                            ins = pe.matmul(ps_e[k][:, h, :], e[:, k, h:h + 1].to_broadcast([P, P]), ident[:, :], start=True, stop=True)
                        ins.then_inc(s_eb, 1)
                    pe.wait_ge(s_pay, i * 2 + (s + 1))
                    for k in range(K):
                        ins = pe.matmul(ps_g[:, k, :], same2[:, s, k, :], pay[:, k, :], start=True, stop=True)
                    ins.then_inc(s_gs, 1)
                    along(s, i * 2 + (s + 3))


def expert_gates(nc, tag, st, gates, b_gat, ln_g, ln_b):
    with ExitStack() as ctx:
        def sb(name, shape, dt=F32):
            return ctx.enter_context(nc.sbuf_tensor(f"{tag}eg_{name}", shape, dt))

        semaphores = Semaphores(nc, ctx)

        def sem(name):
            return semaphores.new(f"{tag}eg_s_{name}")

        K = TABLES
        row = sb("row", [P, K, NT, STW])
        m = sb("m", [P, NT, GH])
        x = sb("x", [P, K, NT, GH])
        w = sb("w", [P, K, NT, GH])
        acc = sb("acc", [P, NT, GF])
        t16 = sb("t16", [P, NT, GF])
        den = sb("den", [P, NT, GH])
        t4 = sb("t4", [P, NT, GH])
        vec = sb("vec", [P, 3, GF])
        mean = sb("mean", [P, NT])
        var = sb("var", [P, NT])
        rstd = sb("rstd", [P, NT])
        nhalf = sb("nhalf", [P, NT])
        s = sb("s", [P, NT, GE])
        beats = sb("beats", [P, NT, GE])
        b1 = sb("b1", [P, NT])
        b2 = sb("b2", [P, NT])
        top, second, w1, w2 = sb("top", [P, NT]), sb("second", [P, NT]), sb("w1", [P, NT]), sb("w2", [P, NT])
        is1 = sb("is1", [P, NT, GE])
        is2 = sb("is2", [P, NT, GE])
        s_in, s_vec, s_x, s_w, s_var, s_rstd, s_dif, s_ex = (sem(k) for k in ("in", "vec", "x", "w", "var", "rstd", "dif", "ex"))
        s_turn = sem("turn")
        block = ctx.enter_context(nc.Block())

        @block.sync
        def _(sp):
            for k in range(K):
                sp.dma_start(row[:, k, :, :], st[k, :, :].rearrange("(t p) c -> p t c", p=P)).then_inc(s_in, 16)
            for k, v_ in enumerate((b_gat, ln_g, ln_b)):
                sp.dma_start(vec[:, k, :], v_.to_broadcast([P, GF])).then_inc(s_in, 16)

        @block.scalar
        def _(act):
            act.wait_ge(s_x, 1)
            act.activation(w[:, :, :, :], x[:, :, :, :], ACT.Exp).then_inc(s_w, 1)
            act.wait_ge(s_dif, 1)
            act.activation(w2[:, :], w1[:, :], ACT.Exp).then_inc(s_ex, 1)

        @block.gpsimd
        def _(pool):
            pool.memset(nhalf[:, :], -0.5).then_inc(s_in, 1)
            pool.wait_ge(s_in, 16 * (K + 3) + 1)
            pool.wait_ge(s_var, 1)
            pool.tensor_tensor(rstd[:, :], var[:, :], nhalf[:, :], ALU.pow).then_inc(s_rstd, 1)

        @block.vector
        def _(dve):
            steps = [0]

            def then(ins):
                steps[0] += 1
                ins.then_inc(s_vec, 1)
                dve.wait_ge(s_vec, steps[0])

            def over(a, n):
                return a.unsqueeze(2).to_broadcast([P, NT, n])

            dve.wait_ge(s_in, 16 * (K + 3) + 1)
            then(dve.tensor_tensor(m[:, :, :], row[:, 0, :, GH:2 * GH], row[:, 1, :, GH:2 * GH], ALU.max))
            for k in range(2, K):
                then(dve.tensor_tensor(m[:, :, :], m[:, :, :], row[:, k, :, GH:2 * GH], ALU.max))
            for k in range(K):
                ins = dve.tensor_tensor(x[:, k, :, :], row[:, k, :, GH:2 * GH], m[:, :, :], ALU.subtract)
            ins.then_inc(s_x, 1)
            dve.wait_ge(s_w, 1)
            for k in range(K):
                out4, out16 = (den, acc) if k == 0 else (t4, t16)
                then(dve.tensor_tensor(out4[:, :, :], row[:, k, :, 2 * GH:3 * GH], w[:, k, :, :], ALU.mult))
                for h in range(GH):
                    then(dve.tensor_tensor(out16[:, :, GE * h:GE * h + GE], row[:, k, :, 3 * GH + GE * h:3 * GH + GE * h + GE],
                                           w[:, k, :, h:h + 1].to_broadcast([P, NT, GE]), ALU.mult))
                if k:
                    then(dve.tensor_tensor(den[:, :, :], den[:, :, :], t4[:, :, :], ALU.add))
                    then(dve.tensor_tensor(acc[:, :, :], acc[:, :, :], t16[:, :, :], ALU.add))
            then(dve.tensor_scalar(den[:, :, :], den[:, :, :], 1e-16, None, ALU.add))
            then(dve.reciprocal(t4[:, :, :], den[:, :, :]))
            for h in range(GH):
                then(dve.tensor_tensor(acc[:, :, GE * h:GE * h + GE], acc[:, :, GE * h:GE * h + GE],
                                       t4[:, :, h:h + 1].to_broadcast([P, NT, GE]), ALU.mult))
            then(dve.tensor_tensor(acc[:, :, :], acc[:, :, :], vec[:, 0:1, :].to_broadcast([P, NT, GF]), ALU.add))
            then(dve.tensor_reduce(mean[:, :], acc[:, :, :], AX.X, ALU.add))
            then(dve.tensor_scalar(mean[:, :], mean[:, :], 1.0 / GF, None, ALU.mult))
            then(dve.tensor_tensor(acc[:, :, :], acc[:, :, :], over(mean[:, :], GF), ALU.subtract))
            then(dve.tensor_tensor(t16[:, :, :], acc[:, :, :], acc[:, :, :], ALU.mult))
            then(dve.tensor_reduce(var[:, :], t16[:, :, :], AX.X, ALU.add))
            then(dve.tensor_scalar(var[:, :], var[:, :], 1.0 / GF, 1e-5, ALU.mult, ALU.add))
            dve.nop().then_inc(s_var, 1)
            dve.wait_ge(s_rstd, 1)
            then(dve.tensor_tensor(acc[:, :, :], acc[:, :, :], over(rstd[:, :], GF), ALU.mult))
            then(dve.tensor_tensor(acc[:, :, :], acc[:, :, :], vec[:, 1:2, :].to_broadcast([P, NT, GF]), ALU.mult))
            then(dve.tensor_tensor(acc[:, :, :], acc[:, :, :], vec[:, 2:3, :].to_broadcast([P, NT, GF]), ALU.add))
            then(dve.tensor_reduce(s[:, :, :], acc[:, :, :].rearrange("p t (h e) -> p t e h", e=GE), AX.X, ALU.add))
            then(dve.tensor_scalar(s[:, :, :], s[:, :, :], 1.0 / GH, None, ALU.mult))
            for e in range(GE):
                for f in range(GE):
                    if f == e:
                        continue
                    op = ALU.is_ge if f < e else ALU.is_gt
                    first = f == (1 if e == 0 else 0)
                    then(dve.tensor_tensor(b1[:, :], s[:, :, f], s[:, :, e], op))
                    if first:
                        then(dve.tensor_copy(beats[:, :, e], b1[:, :]))
                    else:
                        then(dve.tensor_tensor(beats[:, :, e], beats[:, :, e], b1[:, :], ALU.add))
            then(dve.tensor_scalar(is1[:, :, :], beats[:, :, :], 0.0, None, ALU.is_equal))
            then(dve.tensor_scalar(is2[:, :, :], beats[:, :, :], 1.0, None, ALU.is_equal))
            then(dve.tensor_tensor(t4[:, :, :], is1[:, :, :], s[:, :, :], ALU.mult))
            then(dve.tensor_reduce(top[:, :], t4[:, :, :], AX.X, ALU.add))
            then(dve.tensor_tensor(t4[:, :, :], is2[:, :, :], s[:, :, :], ALU.mult))
            then(dve.tensor_reduce(second[:, :], t4[:, :, :], AX.X, ALU.add))
            then(dve.tensor_tensor(w1[:, :], second[:, :], top[:, :], ALU.subtract))
            dve.nop().then_inc(s_dif, 1)
            dve.wait_ge(s_ex, 1)
            then(dve.tensor_scalar(b1[:, :], w2[:, :], 1.0, None, ALU.add))
            then(dve.reciprocal(w1[:, :], b1[:, :]))
            then(dve.tensor_tensor(b2[:, :], w2[:, :], w1[:, :], ALU.mult))
            then(dve.tensor_tensor(is1[:, :, :], is1[:, :, :], over(w1[:, :], GE), ALU.mult))
            then(dve.tensor_tensor(is2[:, :, :], is2[:, :, :], over(b2[:, :], GE), ALU.mult))
            then(dve.tensor_tensor(gates[:, :, :], is1[:, :, :], is2[:, :, :], ALU.add))
MT = 512
MTT = MT // P
HID = 512
MB = HID // P


def experts(nc, tag, x_in, x_out, tT, gates, w1_in, b1_in, w2_in, b2_in):
    with ExitStack() as ctx:
        def sb(name, shape, dt=F32):
            return ctx.enter_context(nc.sbuf_tensor(f"{tag}ex_{name}", shape, dt))

        semaphores = Semaphores(nc, ctx)

        def sem(name):
            return semaphores.new(f"{tag}ex_s_{name}")

        w1 = sb("w1", [P, GE, KK, HID])
        w2 = sb("w2", [P, GE, MB, C])
        b1 = sb("b1", [P, GE, MB])
        b2 = sb("b2", [P, GE, C])
        tt = sb("tt", [P, 2, KK, MT])
        xt = sb("xt", [P, 2, MTT, C])
        g4 = sb("g4", [P, 2, MTT, GE])
        hid = sb("hid", [P, 2, MB, MT])
        ps1 = [ctx.enter_context(nc.psum_tensor(f"{tag}ex_p{i}", [P, MT], F32)) for i in range(4)]
        ps2 = [ctx.enter_context(nc.psum_tensor(f"{tag}ex_q{i}", [P, 2, C], F32)) for i in range(4)]
        s_const = sem("const")
        s_t = [sem("t0"), sem("t1")]
        s_out = [sem("out0"), sem("out1")]
        s_up, s_act, s_down, s_add, s_vec, s_free = (sem(k) for k in ("up", "act", "down", "add", "vec", "free"))
        NS = M // MT
        UP, DN = GE * MB, GE * 2
        s_turn = sem("turn")
        block = ctx.enter_context(nc.Block())

        @block.sync
        def _(sp):
            sp.dma_start(w1[:, :, :, :], w1_in).then_inc(s_const, 16)
            sp.dma_start(w2[:, :, :, :], w2_in).then_inc(s_const, 16)
            sp.dma_start(b1[:, :, :], b1_in).then_inc(s_const, 16)
            for e in range(GE):
                sp.dma_start(b2[:, e, :], b2_in[e:e + 1, :].to_broadcast([P, C])).then_inc(s_const, 16)
            with sp.Fori(0, NS // 2) as i:
                for s in range(2):
                    sp.wait_ge(s_free, i * 2 + (s + 1))
                    sp.sem_inc(s_turn, 1)
                    sp.dma_start(xt[:, s, :, :], x_in[bass.ds(i * (2 * MT) + s * MT, MT), :]
                                 .rearrange("(t p) c -> p t c", p=P)).then_inc(s_t[s], 16)
                    sp.dma_start(tt[:, s, :, :].rearrange("p k l -> p (k l)").rearrange("p (k l) -> p k l", k=KK),
                                 tT[bass.ds(i, 1), :, :, MT * s:MT * s + MT].rearrange("a p k l -> p (a k) l")).then_inc(s_t[s], 16)

        @block.tensor
        def _(pe):
            pe.wait_ge(s_const, 16 * (3 + GE))
            with pe.Fori(0, NS // 2) as i:
                def up(n):
                    s, e = n // GE, n % GE
                    if e == 0:
                        pe.wait_ge(s_t[s], i * 32 + 32)
                    for m in range(MB):
                        pe.wait_ge(s_act, i * (2 * UP) + (n * MB + m + 1))
                        for k in range(KK):
                            ins = pe.matmul(ps1[m][:, :], w1[:, e, k, P * m:P * m + P], tt[:, s, k, :],
                                            start=(k == 0), stop=(k == KK - 1))
                        ins.then_inc(s_up, 1)

                def down(n):
                    e = n % GE
                    pe.wait_ge(s_act, i * (2 * UP) + (n * MB + 2 * MB))
                    for q in range(2):
                        pe.wait_ge(s_add, i * (2 * DN) + (2 * n + q + 1))
                        bank = (2 * n + q) % 4
                        for r in range(2):
                            t = 2 * q + r
                            for m in range(MB):
                                ins = pe.matmul(ps2[bank][:, r, :], hid[:, n % 2, m, P * t:P * t + P], w2[:, e, m, :],
                                                start=(m == 0), stop=(m == MB - 1))
                        ins.then_inc(s_down, 1)

                for n in range(2 * GE):
                    up(n)
                    if n:
                        down(n - 1)
                down(2 * GE - 1)

        @block.scalar
        def _(act):
            act.wait_ge(s_const, 16 * (3 + GE))
            act.sem_inc(s_act, MB)
            with act.Fori(0, NS // 2) as i:
                for n in range(2 * GE):
                    act.wait_ge(s_down, i * (2 * DN) + (2 * n + 1))
                    for m in range(MB):
                        act.wait_ge(s_up, i * (2 * UP) + (n * MB + m + 1))
                        act.activation(hid[:, n % 2, m, :], ps1[m][:, :], ACT.Gelu,
                                       bias=b1[:, n % GE, m:m + 1]).then_inc(s_act, 1)

        @block.gpsimd
        def _(pool):
            pool.sem_inc(s_down, 3)
            with pool.Fori(0, NS // 2) as i:
                for s in range(2):
                    pool.wait_ge(s_add, i * (2 * DN) + (4 + s * DN + DN))
                    pool.dma_start(x_out[bass.ds(i * (2 * MT) + s * MT, MT), :].rearrange("(t p) c -> p t c", p=P),
                                   xt[:, s, :, :]).then_inc(s_out[s], 16)
                for s in range(2):
                    pool.wait_ge(s_out[s], i * 16 + 16)
                    pool.sem_inc(s_free, 1)
            for s in range(2):
                pool.wait_ge(s_out[s], 16 * (NS // 2))

        @block.vector
        def _(dve):
            dve.wait_ge(s_const, 16 * (3 + GE))
            dve.sem_inc(s_add, 4)
            dve.sem_inc(s_free, 2)
            with dve.Fori(0, NS // 2) as i:
                done = 0
                for s in range(2):
                    dve.wait_ge(s_t[s], i * 32 + 32)
                    dve.tensor_copy(g4[:, s, :, :], gates[:, bass.ds(i * (2 * MTT) + s * MTT, MTT), :]).then_inc(s_vec, 1)
                    done += 1
                    dve.wait_ge(s_vec, done)
                    for e in range(GE):
                        for t in range(MTT):
                            ins = dve.scalar_tensor_tensor(xt[:, s, t, :], b2[:, e, :], g4[:, s, t, e:e + 1],
                                                           xt[:, s, t, :], ALU.mult, ALU.add)
                        ins.then_inc(s_vec, 1)
                        done += 1
                        dve.wait_ge(s_vec, done)
                    for e in range(GE):
                        n = s * GE + e
                        for q in range(2):
                            dve.wait_ge(s_down, i * (2 * DN) + (3 + 2 * n + q + 1))
                            if e > 0:
                                dve.wait_ge(s_add, i * (2 * DN) + (4 + 2 * n + q - 1))
                            for r in range(2):
                                t = 2 * q + r
                                ins = dve.scalar_tensor_tensor(xt[:, s, t, :], ps2[(2 * n + q) % 4][:, r, :],
                                                               g4[:, s, t, e:e + 1], xt[:, s, t, :], ALU.mult, ALU.add)
                            ins.then_inc(s_add, 1)
                dve.sem_clear(s_vec)


ROUND = 12582912.0
QMAX = 127.0
TAPS = 9
PADR = N1 + 2


def conv_layer(nc, x_in, x_out, rhs_in, ident_in):
    with ExitStack() as ctx:
        def sb(name, shape, dt=F32):
            return ctx.enter_context(nc.sbuf_tensor(f"cv_{name}", shape, dt))

        semaphores = Semaphores(nc, ctx)

        def sem(name):
            return semaphores.new(f"cv_s_{name}")

        ident = sb("ident", [P, P])
        identb = sb("identb", [P, P], BF16)
        w = sb("w", [P, KK, TAPS, C])
        qw = sb("qw", [P, KK, TAPS, C], BF16)
        wmax = sb("wmax", [P, C])
        wall = sb("wall", [P, C])
        s_rhs = sb("s_rhs", [P, C])
        r_rhs = sb("r_rhs", [P, C])
        xt = sb("xt", [P, 2, TPB, C])
        xn = sb("xn", [P, TPB, C])
        q = sb("q", [P, 2, TPB, C], BF16)
        pad = sb("pad", [P, 2, KK, 3, PADR, N2], BF16)
        y = sb("y", [P, 2, C])
        stats = sb("stats", [P, TPB, 6])
        mv = sb("mv", [P, TPB, 2])
        ve = sb("ve", [P, TPB])
        nhalf = sb("nhalf", [P, TPB])
        rstd = sb("rstd", [P, TPB])
        amax = sb("amax", [P, 1])
        aall = sb("aall", [P, 1])
        s_lhs = sb("s_lhs", [P, 2])
        r_lhs = sb("r_lhs", [P, 2])
        ps_t = [ctx.enter_context(nc.psum_tensor(f"cv_pt{i}", [P, KK, P], BF16)) for i in range(2)]
        ps_o = [ctx.enter_context(nc.psum_tensor(f"cv_po{i}", [P, C], F32)) for i in range(4)]
        s_const, s_mem, s_wm, s_wa, s_w, s_vec = (sem(k) for k in ("const", "mem", "wm", "wa", "w", "vec"))
        s_x = [sem("x0"), sem("x1")]
        s_out = [sem("out0"), sem("out1")]
        s_ve, s_rstd, s_am, s_aa, s_q, s_tr, s_pad, s_o, s_y, s_free = (
            sem(k) for k in ("ve", "rstd", "am", "aa", "q", "tr", "pad", "o", "y", "free"))
        NB = B // 2
        s_turn = sem("turn")
        block = ctx.enter_context(nc.Block())

        @block.sync
        def _(sp):
            sp.dma_start(ident[:, :], ident_in).then_inc(s_const, 16)
            sp.dma_start(w[:, :, :, :], rhs_in).then_inc(s_const, 16)
            with sp.Fori(0, NB) as i:
                for s in range(2):
                    sp.wait_ge(s_free, i * 2 + (s + 1))
                    sp.sem_inc(s_turn, 1)
                    sp.dma_start(xt[:, s, :, :], x_in[bass.ds(i * (2 * L) + s * L, L), :]
                                 .rearrange("(t p) c -> p t c", p=P)).then_inc(s_x[s], 16)

        @block.gpsimd
        def _(pool):
            pool.memset(nhalf[:, :], -0.5)
            pool.memset(pad[:, :, :, :, :, :], 0.0).then_inc(s_mem, 1)
            pool.wait_ge(s_mem, 1)
            pool.wait_ge(s_wm, 1)
            pool.partition_all_reduce(wall[:, :], wmax[:, :], P, bass.bass_isa.ReduceOp.max).then_inc(s_wa, 1)
            pool.sem_inc(s_free, 2)
            with pool.Fori(0, NB) as i:
                for s in range(2):
                    pool.wait_ge(s_ve, i * 2 + (s + 1))
                    pool.tensor_tensor(rstd[:, :], ve[:, :], nhalf[:, :], ALU.pow).then_inc(s_rstd, 1)
                    pool.wait_ge(s_am, i * 2 + (s + 1))
                    pool.sem_inc(s_mem, 1)
                    pool.partition_all_reduce(aall[:, :], amax[:, :], P, bass.bass_isa.ReduceOp.max).then_inc(s_aa, 1)

        @block.scalar
        def _(act):
            act.wait_ge(s_mem, 1)
            with act.Fori(0, NB) as i:
                for s in range(2):
                    for t in range(TPB):
                        act.wait_ge(s_tr, i * (2 * TPB) + (s * TPB + t + 1))
                        if t == 0:
                            act.wait_ge(s_o, i * (2 * TPB) + (s * TPB + TPB))
                        tile = ps_t[t % 2][:, :, :].rearrange("p k (r c) -> p k r c", c=N2)
                        rows = slice(1 + 4 * t, 5 + 4 * t)
                        for dx in range(3):
                            to, of = max(0, 1 - dx), max(0, dx - 1)
                            n = N2 - abs(dx - 1)
                            ins = act.activation(pad[:, s, :, dx, rows, to:to + n], tile[:, :, :, of:of + n], ACT.Copy)
                        ins.then_inc(s_pad, 1)
                for s in range(2):
                    act.wait_ge(s_y, i * (2 * TPB) + (4 + s * TPB + TPB))
                    act.dma_start(x_out[bass.ds(i * (2 * L) + s * L, L), :].rearrange("(t p) c -> p t c", p=P),
                                  xt[:, s, :, :]).then_inc(s_out[s], 16)
                for s in range(2):
                    act.wait_ge(s_out[s], i * 16 + 16)
                    act.sem_inc(s_free, 1)
            for s in range(2):
                act.wait_ge(s_out[s], 16 * NB)

        @block.vector
        def _(dve):
            steps = [0]

            def then(ins):
                steps[0] += 1
                ins.then_inc(s_vec, 1)
                dve.wait_ge(s_vec, steps[0])

            dve.wait_ge(s_const, 32)
            dve.wait_ge(s_mem, 1)
            dve.tensor_reduce(wmax[:, :], w[:, :, :, :].rearrange("p k t c -> p c (k t)"), AX.X, ALU.max,
                              apply_absolute_value=True).then_inc(s_wm, 1)
            dve.tensor_copy(identb[:, :], ident[:, :])
            dve.wait_ge(s_wa, 1)
            then(dve.tensor_scalar(s_rhs[:, :], wall[:, :], 1e-6, 1.0 / QMAX, ALU.max, ALU.mult))
            then(dve.reciprocal(r_rhs[:, :], s_rhs[:, :]))
            for k in range(KK):
                wk = w[:, k, :, :]
                then(dve.tensor_tensor(wk, wk, r_rhs[:, :].unsqueeze(1).to_broadcast([P, TAPS, C]), ALU.mult))
                then(dve.tensor_scalar(wk, wk, QMAX, -QMAX, ALU.min, ALU.max))
                then(dve.tensor_scalar(wk, wk, ROUND, None, ALU.add))
                then(dve.tensor_scalar(qw[:, k, :, :], wk, ROUND, None, ALU.subtract))
            dve.nop().then_inc(s_w, 1)
            dve.sem_clear(s_vec)
            dve.sem_inc(s_o, 2 * TPB)
            with dve.Fori(0, NB) as i:
                steps[0] = 0

                def prepare(s):
                    dve.wait_ge(s_x[s], i * 16 + 16)
                    for t in range(TPB):
                        ins = dve.bn_stats(stats[:, t, :], xt[:, s, t, :])
                    then(ins)
                    for t in range(TPB):
                        ins = dve.bn_aggr(mv[:, t, :], stats[:, t, :])
                    then(ins)
                    dve.tensor_scalar(ve[:, :], mv[:, :, 1], 1e-6, None, ALU.add).then_inc(s_ve, 1)
                    dve.wait_ge(s_rstd, i * 2 + (s + 1))
                    for t in range(TPB):
                        ins = dve.tensor_scalar(xn[:, t, :], xt[:, s, t, :], mv[:, t, 0:1], rstd[:, t:t + 1],
                                                ALU.subtract, ALU.mult)
                    then(ins)
                    dve.tensor_reduce(amax[:, :], xn[:, :, :], AX.XY, ALU.max, apply_absolute_value=True).then_inc(s_am, 1)
                    dve.wait_ge(s_aa, i * 2 + (s + 1))
                    then(dve.tensor_scalar(s_lhs[:, s:s + 1], aall[:, :], 1e-6, 1.0 / QMAX, ALU.max, ALU.mult))
                    then(dve.reciprocal(r_lhs[:, s:s + 1], s_lhs[:, s:s + 1]))
                    then(dve.tensor_scalar(xn[:, :, :], xn[:, :, :], r_lhs[:, s:s + 1], QMAX, ALU.mult, ALU.min))
                    then(dve.tensor_scalar(xn[:, :, :], xn[:, :, :], -QMAX, ROUND, ALU.max, ALU.add))
                    then(dve.tensor_scalar(q[:, s, :, :], xn[:, :, :], ROUND, None, ALU.subtract))
                    dve.nop().then_inc(s_q, 1)

                def finish(s):
                    for t in range(TPB):
                        n = s * TPB + t
                        dve.wait_ge(s_o, i * (2 * TPB) + (2 * TPB + n + 1))
                        then(dve.scalar_tensor_tensor(y[:, t % 2, :], ps_o[t % 4][:, :], s_lhs[:, s:s + 1],
                                                      s_rhs[:, :], ALU.mult, ALU.mult))
                        dve.tensor_tensor(xt[:, s, t, :], y[:, t % 2, :], xt[:, s, t, :], ALU.add).then_inc(s_y, 1)

                prepare(0)
                prepare(1)
                finish(0)
                finish(1)
                dve.sem_clear(s_vec)

        @block.tensor
        def _(pe):
            pe.wait_ge(s_w, 1)
            pe.sem_inc(s_pad, 2)
            pe.sem_inc(s_y, 4)
            with pe.Fori(0, NB) as i:
                for s in range(2):
                    pe.wait_ge(s_q, i * 2 + (s + 1))
                    for t in range(TPB):
                        n = s * TPB + t
                        pe.wait_ge(s_pad, i * (2 * TPB) + (n + 1))
                        for k in range(KK):
                            ins = pe.transpose(ps_t[t % 2][:, k, :], q[:, s, t, P * k:P * k + P], identb[:, :])
                        ins.then_inc(s_tr, 1)
                for s in range(2):
                    pe.wait_ge(s_pad, i * (2 * TPB) + (2 + s * TPB + TPB))
                    for t in range(TPB):
                        n = s * TPB + t
                        pe.wait_ge(s_y, i * (2 * TPB) + (n + 1))
                        for a in range(KK * TAPS):
                            k, tap = a // TAPS, a % TAPS
                            dy, dx = tap // 3, tap % 3
                            ins = pe.matmul(ps_o[t % 4][:, :], pad[:, s, k, dx, 4 * t + dy:4 * t + dy + 4, :].rearrange("p r c -> p (r c)"),
                                            qw[:, k, tap, :], start=(a == 0), stop=(a == KK * TAPS - 1))
                        ins.then_inc(s_o, 1)

def build(nc, a, out):
    def dram(name, shape):
        return nc.dram_tensor(name, shape, F32).ap()

    x1, x2, x3 = (dram(n, (M, C)) for n in ("x1", "x2", "x3"))
    tT = dram("tT", (NGT, P, KK, GTOK))
    hs_rows = dram("hs_rows", (M, HSW))
    st = StateTables([dram(f"target_rows{k}", (M, STW)) for k in range(TABLES)])

    def gated_experts(layer, x_in, x_out):
        w = {n: a[f"L{layer}_{n}"] for n in ("w_gat", "att_src", "att_dst", "b_gat", "ln_gamma", "ln_beta",
                                            "w1", "b1", "w2", "b2", "edges")}
        tag = f"l{layer}"
        with ExitStack() as ctx:
            def sb(name, shape, dt=F32):
                return ctx.enter_context(nc.sbuf_tensor(f"{tag}_{name}", shape, dt))

            codes = sb("codes", [P, EC + 8], I32)
            count = sb("count", [P, NT])
            left = sb("left", [P, 1], I32)
            ad = sb("ad", [P, NT, GH])
            gates = sb("gates", [P, NT, GE])
            edge_lists(nc, tag, w["edges"], a["iota"], codes, count, left)
            normalised_nodes(nc, tag, x_in, tT, hs_rows, ad, w["w_gat"], w["att_src"], w["att_dst"], a["ident"])
            target_rows(nc, tag, hs_rows, ad, count, st)
            edge_sums(nc, tag, hs_rows, st, codes, left, a["ident"], a["below"])
            expert_gates(nc, tag, st, gates, w["b_gat"], w["ln_gamma"], w["ln_beta"])
            experts(nc, tag, x_in, x_out, tT, gates, w["w1"], w["b1"], w["w2"], w["b2"])

    attention_layer(nc, a["x"], x1, a["w_att"], a["cos"], a["sin"], a["qscale"], a["decay"], a["ln_g"], a["ln_b"],
                    a["ident"], a["blk"])
    gated_experts(0, x1, x2)
    conv_layer(nc, x2, x3, a["rhs"], a["ident"])
    gated_experts(1, x3, out)


class StateTables:

    def __init__(self, tables):
        self.tables = tables

    def __getitem__(self, at):
        if isinstance(at, tuple):
            return self.tables[at[0]][at[1:]]
        return self.tables[at]


def kernel(**inputs):
    import concourse.bacc as bacc
    from concourse.bass_utils import run_bass_kernel_spmd

    def rows_first(w, *lead):
        k = w.shape[-2] // P
        v = w.reshape(*w.shape[:-2], k, P, w.shape[-1])
        return np.ascontiguousarray(np.moveaxis(v, -2, 0))

    inputs = {k: np.asarray(v) for k, v in inputs.items()}
    cos, sin, qscale, decay, blk, eye = attention_constants()
    swapped = np.arange(C) ^ 1
    wq, wk, wv, wo = (inputs[f"L0_conv_W{k}"] for k in "qkvo")
    arrays = {
        "x": np.ascontiguousarray(inputs["x"].reshape(M, C)),
        "w_att": np.ascontiguousarray(np.stack([rows_first(w.T) for w in (wq, wq[swapped], wk, wk[swapped], wv, wo)], axis=1)),
        "cos": cos, "sin": sin, "qscale": qscale, "decay": decay, "blk": blk, "ident": eye,
        "ln_g": inputs["L0_conv_ln_g"].reshape(KD, 1),
        "ln_b": inputs["L0_conv_ln_b"].reshape(KD, 1),
        "below": np.tril(np.ones((P, P), np.float32), -1),
        "iota": np.ascontiguousarray(np.broadcast_to(np.arange(P)[None, :, None], (P, P, HIST))).astype(mybir.dt.np(BF16)),
        "rhs": np.ascontiguousarray(inputs["L1_conv_rhs"].reshape(TAPS, KK, P, C).transpose(2, 1, 0, 3)),
    }
    for layer in range(2):
        f, t = f"L{layer}_ffn_", f"L{layer}_"
        arrays[t + "w_gat"] = rows_first(inputs[f + "W_gat"])
        arrays[t + "w1"] = rows_first(inputs[f + "W1"])
        arrays[t + "w2"] = rows_first(inputs[f + "W2"])
        arrays[t + "b1"] = np.ascontiguousarray(inputs[f + "b1"].reshape(GE, MB, P).transpose(2, 0, 1))
        arrays[t + "b2"] = inputs[f + "b2"]
        arrays[t + "edges"] = inputs[f + "edge_index"]
        for name in ("att_src", "att_dst", "b_gat", "ln_gamma", "ln_beta"):
            arrays[t + name] = inputs[f + name].reshape(1, GF)
    nc = bacc.Bacc("TRN2", target_bir_lowering=False, num_devices=1)
    aps = {n: nc.dram_tensor("in_" + n, v.shape, mybir.dt.from_np(v.dtype), kind="ExternalInput").ap() for n, v in arrays.items()}
    out = nc.dram_tensor("out", (M, C), F32, kind="ExternalOutput").ap()
    build(nc, aps, out)
    r = run_bass_kernel_spmd(nc, [{"in_" + n: v for n, v in arrays.items()}], core_ids=[0])
    return r.results[0]["out"].reshape(B, N1, N2, C)
```
